# Optimizing a Trainium2 kernel written in Bass

```python
import numpy as np
import jax
import jax.numpy as jnp

def _softmax(x, axis=-1):
    return jax.nn.softmax(x, axis=axis)

def _gelu(x):
    return jax.nn.gelu(x, approximate=True)

def _silu(x):
    return jax.nn.silu(x)

def _sigmoid(x):
    return jax.nn.sigmoid(x)

def _layernorm(x, axis=-1, eps=1e-05):
    m = jnp.mean(x, axis=axis, keepdims=True)
    v = jnp.var(x, axis=axis, keepdims=True)
    return (x - m) / jnp.sqrt(v + eps)

def _scatter_add(tgt, idx, src, axis=0):
    return tgt.at[idx].add(src)

def _segment_sum(src, seg, n):
    return jax.ops.segment_sum(src, seg, n)
kernel_name = 'mk_early_fusion_d2_tok_img1024_r4_ea69bc'

def setup_inputs(seed: int=0):
    np.random.seed(seed)
    _w = jnp.asarray

    def _rec_inputs():
        import jax
        import jax.numpy as jnp
        _rk = jax.random.key(seed)
        x = -0.00016672 + 0.999947 * jax.random.normal(jax.random.fold_in(_rk, 1), (16, 3, 96, 96), jnp.float32)
        txt = -2.64394e-05 + 1.00035 * jax.random.normal(jax.random.fold_in(_rk, 2), (16, 128, 256), jnp.float32)
        return (x, txt)
    x, txt = _rec_inputs()

    def _L0_tok_setup():
        import jax, jax.numpy as jnp
        import numpy as np
        B, C, H, Wd = (64, 3, 96, 96)
        PH, PW, D = (16, 16, 256)
        PATCH_DIM = C * PH * PW
        N_TOK = H // PH * (Wd // PW)
        key = jax.random.key(seed)
        k1, k2, k3, k4, k5 = jax.random.split(key, 5)
        x = jax.random.normal(k1, (B, C, H, Wd), dtype=jnp.float32)
        W = jax.random.normal(k2, (D, PATCH_DIM), dtype=jnp.float32) * PATCH_DIM ** (-0.5)
        b = jax.random.normal(k3, (D,), dtype=jnp.float32) * 0.02
        cls_token = jax.random.normal(k4, (1, 1, D), dtype=jnp.float32)
        pos_embedding = jax.random.normal(k5, (1, N_TOK + 1, D), dtype=jnp.float32) * 0.02
        return {'x': x, 'W': W, 'b': b, 'cls_token': cls_token, 'pos_embedding': pos_embedding}
    _L0_tok_all = _L0_tok_setup()
    _L0_tok_in = {k: v for k, v in _L0_tok_all.items() if k in ('W', 'b', 'cls_token', 'pos_embedding')}
    del _L0_tok_all

    def _L0_attn_setup():
        import jax, jax.numpy as jnp
        import numpy as np
        N_HEAD = 16
        MAX_WAVELENGTH = 2500
        ROPE_PCT = 1.0

        def apply_p_rope(inputs, positions, head_dim, max_wavelength=MAX_WAVELENGTH, rope_percentage=ROPE_PCT):
            rope_angles = int(rope_percentage * head_dim // 2)
            nope_angles = head_dim // 2 - rope_angles
            fraction = 2.0 * jnp.arange(0, rope_angles) / head_dim
            timescale = max_wavelength ** fraction
            timescale = jnp.pad(timescale, (0, nope_angles), mode='constant', constant_values=(0, jnp.inf))
            sinusoid_inp = positions[..., None] / timescale[None, :]
            sin = jnp.sin(sinusoid_inp)
            cos = jnp.cos(sinusoid_inp)
            first_half, second_half = jnp.split(inputs, 2, axis=-1)
            first_part = first_half * cos - second_half * sin
            second_part = second_half * cos + first_half * sin
            return jnp.concatenate([first_part, second_part], axis=-1).astype(inputs.dtype)
        key = jax.random.key(seed)
        ks = jax.random.split(key, 4)
        B, T, C = (2, 512, 256)
        x = jax.random.normal(ks[0], (B, T, C), dtype=jnp.float32)
        W_attn = jax.random.normal(ks[1], (C, 3 * C), dtype=jnp.float32) * 0.02
        b_attn = jnp.zeros((3 * C,), dtype=jnp.float32)
        W_proj = jax.random.normal(ks[2], (C, C), dtype=jnp.float32) * 0.02
        b_proj = jnp.zeros((C,), dtype=jnp.float32)
        return {'x': x, 'W_attn': W_attn, 'b_attn': b_attn, 'W_proj': W_proj, 'b_proj': b_proj}
    _L0_attn_all = _L0_attn_setup()
    _L0_attn_in = {k: v for k, v in _L0_attn_all.items() if k in ('W_attn', 'b_attn', 'W_proj', 'b_proj')}
    del _L0_attn_all

    def _L0_ffn_setup():
        import jax, jax.numpy as jnp
        import numpy as np
        D_MODEL, D_FF, RANK = (256, 1024, 64)
        B, S = (4, 1024)
        key = jax.random.key(seed)
        ks = jax.random.split(key, 7)
        return {'x': jax.random.normal(ks[0], (B, S, D_MODEL), dtype=jnp.float32), 'U1': jax.random.normal(ks[1], (D_MODEL, RANK), dtype=jnp.float32) * 0.02, 'V1': jax.random.normal(ks[2], (RANK, D_FF), dtype=jnp.float32) * 0.02, 'b1': jnp.zeros((D_FF,), dtype=jnp.float32), 'U2': jax.random.normal(ks[3], (D_FF, RANK), dtype=jnp.float32) * 0.02, 'V2': jax.random.normal(ks[4], (RANK, D_MODEL), dtype=jnp.float32) * 0.02, 'b2': jnp.zeros((D_MODEL,), dtype=jnp.float32)}
    _L0_ffn_all = _L0_ffn_setup()
    _L0_ffn_in = {k: v for k, v in _L0_ffn_all.items() if k in ('U1', 'V1', 'b1', 'U2', 'V2', 'b2')}
    del _L0_ffn_all

    def _L1_attn_setup():
        import jax, jax.numpy as jnp
        import numpy as np
        DIMS = 256
        HEAD = 16
        HD = DIMS // HEAD
        CTX = 512
        B = 1

        def _ln(x, w, b, eps=1e-05):
            m = jnp.mean(x, axis=-1, keepdims=True)
            v = jnp.var(x, axis=-1, keepdims=True)
            return (x - m) * jax.lax.rsqrt(v + eps) * w + b

        def _rotary(x, xa, rh_w, rh_b):
            c = x.shape[2]
            d2 = x.shape[-1] // 2
            mel_max = 2595.0 * np.log10(1.0 + 4000.0 / 200.0)
            scale = jnp.power(10.0, jnp.linspace(0.0, mel_max, d2, dtype=jnp.float32) / 2595.0) - 1.0
            fb = 200.0 * scale / 1000.0
            freqs = jnp.arange(c, dtype=jnp.float32)[:, None] * fb[None, :]
            per_step = (xa @ rh_w + rh_b)[..., 0]
            radius = jnp.clip(per_step / 100.0, 0.5, 2.0)
            fr = radius[:, :, None] * jnp.cos(freqs)[None]
            fi = radius[:, :, None] * jnp.sin(freqs)[None]
            xr = x[..., 0::2]
            xi = x[..., 1::2]
            out_r = xr * fr[:, None] - xi * fi[:, None]
            out_i = xr * fi[:, None] + xi * fr[:, None]
            return jnp.stack([out_r, out_i], axis=-1).reshape(x.shape)
        key = jax.random.key(seed)
        ks = jax.random.split(key, 8)
        s = 0.02
        return {'x': jax.random.normal(ks[0], (B, CTX, DIMS), dtype=jnp.float32), 'qn_w': jnp.ones((DIMS,), jnp.float32), 'qn_b': jnp.zeros((DIMS,), jnp.float32), 'q_w': jax.random.normal(ks[1], (DIMS, DIMS), jnp.float32) * s, 'q_b': jnp.zeros((DIMS,), jnp.float32), 'kvn_w': jnp.ones((DIMS,), jnp.float32), 'kvn_b': jnp.zeros((DIMS,), jnp.float32), 'kv_w': jax.random.normal(ks[2], (DIMS, 2 * DIMS), jnp.float32) * s, 'kv_b': jnp.zeros((2 * DIMS,), jnp.float32), 'out_w': jax.random.normal(ks[3], (DIMS, DIMS), jnp.float32) * s, 'out_b': jnp.zeros((DIMS,), jnp.float32), 'ln_w': jnp.ones((HD,), jnp.float32), 'ln_b': jnp.zeros((HD,), jnp.float32), 'rh_w': jax.random.normal(ks[4], (DIMS, 1), jnp.float32) * s, 'rh_b': jnp.zeros((1,), jnp.float32)}
    _L1_attn_all = _L1_attn_setup()
    _L1_attn_in = {k: v for k, v in _L1_attn_all.items() if k in ('qn_w', 'qn_b', 'q_w', 'q_b', 'kvn_w', 'kvn_b', 'kv_w', 'kv_b', 'out_w', 'out_b', 'ln_w', 'ln_b', 'rh_w', 'rh_b')}
    del _L1_attn_all

    def _L1_ffn_setup():
        import jax, jax.numpy as jnp
        import numpy as np
        D_MODEL, D_FF, N_EXPERTS, TOP_K = (256, 512, 8, 2)
        B, S = (2, 512)
        key = jax.random.key(seed)
        k1, k2, k3, k4 = jax.random.split(key, 4)
        scale = 0.02
        return {'x': jax.random.normal(k1, (B, S, D_MODEL), dtype=jnp.float32), 'gate_w': jax.random.normal(k2, (D_MODEL, N_EXPERTS), dtype=jnp.float32) * scale, 'w1': jax.random.normal(k3, (N_EXPERTS, D_MODEL, D_FF), dtype=jnp.float32) * scale, 'w2': jax.random.normal(k4, (N_EXPERTS, D_FF, D_MODEL), dtype=jnp.float32) * scale}
    _L1_ffn_all = _L1_ffn_setup()
    _L1_ffn_in = {k: v for k, v in _L1_ffn_all.items() if k in ('gate_w', 'w1', 'w2')}
    del _L1_ffn_all
    return {'x': x, 'txt': txt, 'L0_tok_W': _L0_tok_in['W'], 'L0_tok_b': _L0_tok_in['b'], 'L0_tok_cls_token': _L0_tok_in['cls_token'], 'L0_tok_pos_embedding': _L0_tok_in['pos_embedding'], 'L0_attn_W_attn': _L0_attn_in['W_attn'], 'L0_attn_b_attn': _L0_attn_in['b_attn'], 'L0_attn_W_proj': _L0_attn_in['W_proj'], 'L0_attn_b_proj': _L0_attn_in['b_proj'], 'L0_ffn_U1': _L0_ffn_in['U1'], 'L0_ffn_V1': _L0_ffn_in['V1'], 'L0_ffn_b1': _L0_ffn_in['b1'], 'L0_ffn_U2': _L0_ffn_in['U2'], 'L0_ffn_V2': _L0_ffn_in['V2'], 'L0_ffn_b2': _L0_ffn_in['b2'], 'L1_attn_qn_w': _L1_attn_in['qn_w'], 'L1_attn_qn_b': _L1_attn_in['qn_b'], 'L1_attn_q_w': _L1_attn_in['q_w'], 'L1_attn_q_b': _L1_attn_in['q_b'], 'L1_attn_kvn_w': _L1_attn_in['kvn_w'], 'L1_attn_kvn_b': _L1_attn_in['kvn_b'], 'L1_attn_kv_w': _L1_attn_in['kv_w'], 'L1_attn_kv_b': _L1_attn_in['kv_b'], 'L1_attn_out_w': _L1_attn_in['out_w'], 'L1_attn_out_b': _L1_attn_in['out_b'], 'L1_attn_ln_w': _L1_attn_in['ln_w'], 'L1_attn_ln_b': _L1_attn_in['ln_b'], 'L1_attn_rh_w': _L1_attn_in['rh_w'], 'L1_attn_rh_b': _L1_attn_in['rh_b'], 'L1_ffn_gate_w': _L1_ffn_in['gate_w'], 'L1_ffn_w1': _L1_ffn_in['w1'], 'L1_ffn_w2': _L1_ffn_in['w2']}

def reference(x, txt, L0_tok_W, L0_tok_b, L0_tok_cls_token, L0_tok_pos_embedding, L0_attn_W_attn, L0_attn_b_attn, L0_attn_W_proj, L0_attn_b_proj, L0_ffn_U1, L0_ffn_V1, L0_ffn_b1, L0_ffn_U2, L0_ffn_V2, L0_ffn_b2, L1_attn_qn_w, L1_attn_qn_b, L1_attn_q_w, L1_attn_q_b, L1_attn_kvn_w, L1_attn_kvn_b, L1_attn_kv_w, L1_attn_kv_b, L1_attn_out_w, L1_attn_out_b, L1_attn_ln_w, L1_attn_ln_b, L1_attn_rh_w, L1_attn_rh_b, L1_ffn_gate_w, L1_ffn_w1, L1_ffn_w2):
    import jax
    import jax.numpy as jnp

    def _L0_tok_ref(x, W, b, cls_token, pos_embedding):
        import jax, jax.numpy as jnp
        import numpy as np
        B, C, H, Wd = (64, 3, 96, 96)
        PH, PW, D = (16, 16, 256)
        PATCH_DIM = C * PH * PW
        N_TOK = H // PH * (Wd // PW)
        Bc = x.shape[0]
        nh, nw = (H // PH, Wd // PW)
        patches = x.reshape(Bc, C, nh, PH, nw, PW)
        patches = patches.transpose(0, 2, 4, 1, 3, 5).reshape(Bc, nh * nw, PATCH_DIM)
        tokens = jnp.einsum('bnp,dp->bnd', patches, W) + b
        cls = jnp.broadcast_to(cls_token, (Bc, 1, D))
        tokens = jnp.concatenate([cls, tokens], axis=1)
        return tokens + pos_embedding

    def _L0_attn_ref(x, W_attn, b_attn, W_proj, b_proj):
        import jax, jax.numpy as jnp
        import numpy as np
        N_HEAD = 16
        MAX_WAVELENGTH = 2500
        ROPE_PCT = 1.0

        def apply_p_rope(inputs, positions, head_dim, max_wavelength=MAX_WAVELENGTH, rope_percentage=ROPE_PCT):
            rope_angles = int(rope_percentage * head_dim // 2)
            nope_angles = head_dim // 2 - rope_angles
            fraction = 2.0 * jnp.arange(0, rope_angles) / head_dim
            timescale = max_wavelength ** fraction
            timescale = jnp.pad(timescale, (0, nope_angles), mode='constant', constant_values=(0, jnp.inf))
            sinusoid_inp = positions[..., None] / timescale[None, :]
            sin = jnp.sin(sinusoid_inp)
            cos = jnp.cos(sinusoid_inp)
            first_half, second_half = jnp.split(inputs, 2, axis=-1)
            first_part = first_half * cos - second_half * sin
            second_part = second_half * cos + first_half * sin
            return jnp.concatenate([first_part, second_part], axis=-1).astype(inputs.dtype)
        B, T, C = x.shape
        H = N_HEAD
        D = C // H
        qkv = x @ W_attn + b_attn
        q, k, v = jnp.split(qkv, 3, axis=-1)

        def split_heads(t):
            return t.reshape(B, T, H, D).transpose(0, 2, 1, 3)
        q, k, v = (split_heads(q), split_heads(k), split_heads(v))
        positions = jnp.arange(T, dtype=q.dtype)
        q = apply_p_rope(q, positions, D)
        k = apply_p_rope(k, positions, D)
        scale = jnp.sqrt(D).astype(k.dtype)
        attn = jnp.einsum('bhqd,bhkd->bhqk', q, k) / scale
        causal_mask = jnp.tril(jnp.ones((T, T))).astype(bool)
        attn = jnp.where(causal_mask, attn, jnp.finfo(attn.dtype).min)
        attn = jax.nn.softmax(attn, axis=-1)
        y = jnp.einsum('bhqk,bhkd->bhqd', attn, v)
        y = y.transpose(0, 2, 1, 3).reshape(B, T, C)
        return y @ W_proj + b_proj

    def _L0_ffn_ref(x, U1, V1, b1, U2, V2, b2):
        import jax, jax.numpy as jnp
        import numpy as np
        D_MODEL, D_FF, RANK = (256, 1024, 64)
        B, S = (4, 1024)
        P = jnp.einsum('bsd,dr->bsr', x, U1)
        H = jax.nn.gelu(jnp.einsum('bsr,rf->bsf', P, V1) + b1)
        Q = jnp.einsum('bsf,fr->bsr', H, U2)
        return jnp.einsum('bsr,rd->bsd', Q, V2) + b2

    def _L1_attn_ref(x, qn_w, qn_b, q_w, q_b, kvn_w, kvn_b, kv_w, kv_b, out_w, out_b, ln_w, ln_b, rh_w, rh_b):
        import jax, jax.numpy as jnp
        import numpy as np
        DIMS = 256
        HEAD = 16
        HD = DIMS // HEAD
        CTX = 512
        B = 1

        def _ln(x, w, b, eps=1e-05):
            m = jnp.mean(x, axis=-1, keepdims=True)
            v = jnp.var(x, axis=-1, keepdims=True)
            return (x - m) * jax.lax.rsqrt(v + eps) * w + b

        def _rotary(x, xa, rh_w, rh_b):
            c = x.shape[2]
            d2 = x.shape[-1] // 2
            mel_max = 2595.0 * np.log10(1.0 + 4000.0 / 200.0)
            scale = jnp.power(10.0, jnp.linspace(0.0, mel_max, d2, dtype=jnp.float32) / 2595.0) - 1.0
            fb = 200.0 * scale / 1000.0
            freqs = jnp.arange(c, dtype=jnp.float32)[:, None] * fb[None, :]
            per_step = (xa @ rh_w + rh_b)[..., 0]
            radius = jnp.clip(per_step / 100.0, 0.5, 2.0)
            fr = radius[:, :, None] * jnp.cos(freqs)[None]
            fi = radius[:, :, None] * jnp.sin(freqs)[None]
            xr = x[..., 0::2]
            xi = x[..., 1::2]
            out_r = xr * fr[:, None] - xi * fi[:, None]
            out_i = xr * fi[:, None] + xi * fr[:, None]
            return jnp.stack([out_r, out_i], axis=-1).reshape(x.shape)
        b, c, dims = x.shape
        kv = _ln(x, kvn_w, kvn_b) @ kv_w + kv_b
        kv = kv.reshape(b, c, 2, HEAD, HD).transpose(2, 0, 3, 1, 4)
        k, v = (kv[0], kv[1])
        q = (_ln(x, qn_w, qn_b) @ q_w + q_b).reshape(b, c, HEAD, HD).transpose(0, 2, 1, 3)
        q = _rotary(q, x, rh_w, rh_b)
        k = _rotary(k, x, rh_w, rh_b)
        qn = _ln(q, ln_w, ln_b)
        kn = _ln(k, ln_w, ln_b)
        scores = jnp.einsum('bhqd,bhkd->bhqk', qn, kn) / np.sqrt(HD).astype(np.float32)
        attn = jax.nn.softmax(scores, axis=-1)
        a = jnp.einsum('bhqk,bhkd->bhqd', attn, v)
        a = a.transpose(0, 2, 1, 3).reshape(b, c, dims)
        return a @ out_w + out_b

    def _L1_ffn_ref(x, gate_w, w1, w2):
        import jax, jax.numpy as jnp
        import numpy as np
        D_MODEL, D_FF, N_EXPERTS, TOP_K = (256, 512, 8, 2)
        B, S = (2, 512)
        router_logits = jnp.einsum('bsd,de->bse', x, gate_w)
        top_logits, top_idx = jax.lax.top_k(router_logits, TOP_K)
        top_w = jax.nn.softmax(top_logits, axis=-1)
        combine = jnp.sum(jax.nn.one_hot(top_idx, N_EXPERTS, dtype=x.dtype) * top_w[..., None], axis=-2)
        h = jax.nn.silu(jnp.einsum('bsd,edf->ebsf', x, w1))
        y = jnp.einsum('ebsf,efd->ebsd', h, w2)
        out = jnp.einsum('ebsd,bse->bsd', y, combine)
        return out
    h = _L0_tok_ref(x, L0_tok_W, L0_tok_b, L0_tok_cls_token, L0_tok_pos_embedding)
    h = jnp.concatenate([h, txt], axis=1)
    h = h + _L0_attn_ref(_layernorm(h, axis=-1), L0_attn_W_attn, L0_attn_b_attn, L0_attn_W_proj, L0_attn_b_proj)
    h = h + _L0_ffn_ref(_layernorm(h, axis=-1), L0_ffn_U1, L0_ffn_V1, L0_ffn_b1, L0_ffn_U2, L0_ffn_V2, L0_ffn_b2)
    h = h + _L1_attn_ref(_layernorm(h, axis=-1), L1_attn_qn_w, L1_attn_qn_b, L1_attn_q_w, L1_attn_q_b, L1_attn_kvn_w, L1_attn_kvn_b, L1_attn_kv_w, L1_attn_kv_b, L1_attn_out_w, L1_attn_out_b, L1_attn_ln_w, L1_attn_ln_b, L1_attn_rh_w, L1_attn_rh_b)
    h = h + _L1_ffn_ref(_layernorm(h, axis=-1), L1_ffn_gate_w, L1_ffn_w1, L1_ffn_w2)
    return h

_drawn_inputs = setup_inputs


def setup_inputs(seed=0):
    import zlib

    import numpy as np

    out = dict(_drawn_inputs(seed))
    spreads = {'L0_attn_b_attn': (0.0, 0.1),
     'L0_attn_b_proj': (0.0, 0.1),
     'L0_ffn_b1': (0.0, 0.8),
     'L0_ffn_b2': (0.0, 0.8),
     'L1_attn_qn_w': (1.0, 0.6),
     'L1_attn_qn_b': (0.0, 2.0),
     'L1_attn_q_b': (0.0, 2.0),
     'L1_attn_kvn_w': (1.0, 0.6),
     'L1_attn_kvn_b': (0.0, 2.0),
     'L1_attn_kv_b': (0.0, 0.8),
     'L1_attn_out_b': (0.0, 0.8),
     'L1_attn_ln_w': (1.0, 0.6),
     'L1_attn_ln_b': (0.0, 2.0)}
    factors = {'L0_tok_b': 5.495,
     'L0_tok_pos_embedding': 5.76,
     'L0_attn_W_attn': 2.851,
     'L0_ffn_U1': 8.0,
     'L0_ffn_V1': 8.0,
     'L0_ffn_U2': 8.0,
     'L0_ffn_V2': 8.0,
     'L1_attn_q_w': 39.088,
     'L1_attn_kv_w': 6.631,
     'L1_attn_out_w': 6.95,
     'L1_ffn_gate_w': 8.0,
     'L1_ffn_w1': 8.0,
     'L1_ffn_w2': 8.0}
    for name, (base, spread) in spreads.items():
        noise = np.random.default_rng([zlib.crc32(name.encode()), seed]).standard_normal(out[name].shape)
        drawn = base * np.exp(spread * noise) if base else spread * noise
        out[name] = jnp.asarray(drawn.astype(out[name].dtype))
    for name, factor in factors.items():
        out[name] = (out[name] * factor).astype(out[name].dtype)
    return out
```

```python
from contextlib import ExitStack

import concourse.bass as bass
from concourse import mybir

F32 = mybir.dt.float32
F16 = mybir.dt.float16
BF16 = mybir.dt.bfloat16
I32 = mybir.dt.int32
U32 = mybir.dt.uint32
ALU = mybir.AluOpType
ACT = mybir.ActivationFunctionType
AX = mybir.AxisListType

B, T, D = 16, 165, 256
NP, TXT = 36, 128
R = (84, 81)
O = (0, 84)
H, HD = 16, 16
G = 4
NG = H // G
KD = D // 128
FF, RANK = 1024, 64
NE, EF = 8, 512
EPS = 1e-5
PB = 2
PK = 768 // 128


def first_rsqrt(nc, dve, link, y, yi, tmp, x):
    link(nc.vector.tensor_scalar(yi, x.bitcast(I32), 1, None, ALU.logical_shift_right))
    link(nc.vector.tensor_scalar(yi, yi, -1.0, float(0x5F3759DF), ALU.mult, ALU.add))
    for _ in range(3):
        link(nc.vector.scalar_tensor_tensor(out=tmp, in0=y, scalar=-0.5, in1=y, op0=ALU.mult, op1=ALU.mult))
        link(nc.vector.tensor_tensor(tmp, tmp, x, ALU.mult))
        link(nc.vector.scalar_tensor_tensor(out=y, in0=tmp, scalar=1.5, in1=y, op0=ALU.add, op1=ALU.mult))


class Chain:

    def __init__(self, eng, sem, per=0):
        self.eng, self.sem, self.per, self.k, self.turn = eng, sem, per, 0, 0

    def start(self, turn):
        assert not self.per or self.k in (0, self.per), self.k
        self.turn, self.k = turn, 0

    def count(self, ins):
        self.k += 1
        ins.then_inc(self.sem, 1)

    def __call__(self, ins):
        self.count(ins)
        self.hold()

    def hold(self):
        self.eng.wait_ge(self.sem, self.turn * self.per + self.k)


def build_program(nc, a, out):
    with ExitStack() as ctx:
        def sb(name, shape, dt=F32, to=ctx):
            return to.enter_context(nc.sbuf_tensor(name, shape, dt))

        def sem(name, to=ctx):
            return to.enter_context(nc.semaphore(name))

        def ps(name, shape, dt=F32):
            return ctx.enter_context(nc.psum_tensor(name, shape, dt))

        ring = [ps("ring0", [128, 4, 256]), ps("ring1", [128, 4, 256])]
        ps_qk = ps("ps_qk", [128, 512])
        ps_v = ps("ps_v", [128, 512])
        ps_t = ps("ps_t", [128, 512])
        ps_o = ps("ps_o", [128, 512])
        two = (ps_qk, ps_v)

        h = sb("h", [128, 2 * B, D])
        bst = sb("bst", [128, 2 * B, 6])
        mean = sb("mean", [128, 2 * B])
        var = sb("var", [128, 2 * B])
        rs = sb("rs", [128, 2 * B])
        rs_i = rs[:, :].bitcast(I32)
        vtmp = sb("vtmp", [128, 2 * B])
        vtmp2 = sb("vtmp2", [128, 2 * B])
        ratio = sb("ratio", [128, 2 * B])
        ident = sb("ident", [128, 128])
        ident16 = sb("ident16", [128, 128], F16)
        identb = sb("identb", [128, 128], BF16)
        bsel = sb("bsel", [128, 128])
        selh = sb("selh", [128, H, R[0]], BF16)
        mask_s = sb("mask_s", [R[0], 2, T], BF16)
        mask_t = sb("mask_t", [R[0], 2, T], BF16)
        w_qkv = [sb(f"w_qkv{l}", [128, KD, 3 * D + l]) for l in range(2)]
        b_qkv = [sb(f"b_qkv{l}", [R[0], 3 * D]) for l in range(2)]
        w_out = [sb(f"w_out{l}", [128, NG, D]) for l in range(2)]
        cos_t = [sb(f"cos_t{l}", [R[0], 2, HD]) for l in range(2)]
        sin_t = [sb(f"sin_t{l}", [R[0], 2, HD]) for l in range(2)]
        nrm_w = sb("nrm_w", [128, KD, 2])
        nrm_b = sb("nrm_b", [128, KD, 2])
        nrm_bb = sb("nrm_bb", [128, KD, 2, R[0]])
        ln_w = sb("ln_w", [R[0], HD])
        ln_b = sb("ln_b", [R[0], HD])
        rh_b = sb("rh_b", [R[0], 1])
        u1 = sb("u1", [128, KD, RANK])
        v1 = sb("v1", [RANK + 1, FF])
        u2 = sb("u2", [128, FF // 128, RANK])
        v2 = sb("v2", [RANK + 1, D])
        gate = sb("gate", [128, KD, NE])
        iota = sb("iota", [R[0], NE])

        loads = {n: sem(f"loaded_{n}") for n in ("embed", "txt", "consts", "attn0", "ffn0", "attn1", "moe")}
        moved = sem("moved")
        st_set = sem("st_set")

        with ExitStack() as e:
            patches = sb("patches", [128, PK, B * NP], to=e)
            w_tok = sb("w_tok", [128, PK, D], to=e)
            pos2 = sb("pos2", [PB * NP, D], to=e)
            tokb = sb("tokb", [PB * NP, D], to=e)
            cls0 = sb("cls0", [1, D], to=e)
            pos0 = sb("pos0", [1, D], to=e)
            stage = sb("stage", [PB * NP, B // PB, D], to=e)
            emb_mm = sem("emb_mm", e)
            emb_out = sem("emb_out", e)
            emb_add = sem("emb_add", e)
            cls_done = sem("cls_done", e)
            stats_l = sem("stats_l", e)
            selh_f = sb("selh_f", [128, H, R[0]], to=e)
            mask_sf = sb("mask_sf", [R[0], 2, T], to=e)
            mask_tf = sb("mask_tf", [R[0], 2, T], to=e)
            bias_mm = sem("bias_mm", e)
            bb_set = sem("bb_set", e)
            bias_done = sem("bias_done", e)
            with nc.Block() as block:

                @block.sync
                def _(sp):
                    L = loads["embed"]
                    sp.dma_start(patches[:, 0:3, :], a["patches"][:, 0:3, :]).then_inc(L, 16)
                    sp.dma_start(w_tok[:, :, :], a["w_tok"]).then_inc(L, 16)
                    sp.dma_start(patches[:, 3:6, :], a["patches"][:, 3:6, :]).then_inc(L, 16)
                    for i in range(PB):
                        sp.dma_start(pos2[NP * i:NP * i + NP, :], a["pos"][1:NP + 1, :]).then_inc(L, 16)
                    sp.dma_start(tokb[:, :], a["tok_b"].partition_broadcast(PB * NP)).then_inc(L, 16)
                    sp.dma_start(cls0[:, :], a["cls"]).then_inc(L, 16)
                    sp.dma_start(pos0[:, :], a["pos"][0:1, :]).then_inc(L, 16)
                    L = loads["txt"]
                    n0 = R[0] - NP - 1
                    sp.dma_start(h[NP + 1:R[0], 0:2 * B:2, :], a["txt"][:, 0:n0, :].rearrange("b t d -> t b d")).then_inc(L, 16)
                    sp.dma_start(h[0:R[1], 1:2 * B:2, :], a["txt"][:, n0:TXT, :].rearrange("b t d -> t b d")).then_inc(L, 16)
                    for j in range(B // PB):
                        sp.wait_ge(emb_out, j + 1)
                        for i in range(PB):
                            sp.dma_start(h[1:NP + 1, 2 * (PB * j + i), :], stage[NP * i:NP * i + NP, j, :]).then_inc(moved, 16)

                @block.scalar
                def _(act):
                    L = loads["attn0"]
                    act.dma_start(w_qkv[0][:, :, :], a["w_qkv0"]).then_inc(L, 16)
                    act.dma_start(b_qkv[0][:, :], a["b_qkv0"].partition_broadcast(R[0])).then_inc(L, 16)
                    act.dma_start(w_out[0][:, :, :], a["w_out0"]).then_inc(L, 16)
                    L = loads["consts"]
                    for t, n in ((ident, "ident"), (ident16, "ident16"), (bsel, "bsel"),
                                 (selh_f, "selh"), (mask_sf, "mask_s"), (mask_tf, "mask_t"), (cos_t[0], "cos0"),
                                 (sin_t[0], "sin0"), (cos_t[1], "cos1"), (sin_t[1], "sin1")):
                        act.dma_start(t[:], a[n]).then_inc(L, 16)
                    act.dma_start(iota[:, :], a["iota"].partition_broadcast(R[0])).then_inc(L, 16)
                    L = loads["attn1"]
                    act.dma_start(w_qkv[1][:, :, :], a["w_qkv1"]).then_inc(L, 16)
                    act.dma_start(b_qkv[1][:, :], a["b_qkv1"].partition_broadcast(R[0])).then_inc(L, 16)
                    act.dma_start(w_out[1][:, :, :], a["w_out1"]).then_inc(L, 16)
                    act.dma_start(nrm_w[:, :, :], a["nrm_w"]).then_inc(L, 16)
                    act.dma_start(nrm_b[:, :, :], a["nrm_b"]).then_inc(L, 16)
                    act.dma_start(ln_w[:, :], a["ln_w"].partition_broadcast(R[0])).then_inc(L, 16)
                    act.dma_start(ln_b[:, :], a["ln_b"].partition_broadcast(R[0])).then_inc(L, 16)
                    act.dma_start(rh_b[:, :], a["rh_b"].partition_broadcast(R[0])).then_inc(L, 16)
                    L = loads["ffn0"]
                    act.dma_start(u1[:, :, :], a["u1"]).then_inc(L, 16)
                    act.dma_start(v1[:, :], a["v1"]).then_inc(L, 16)
                    act.dma_start(u2[:, :, :], a["u2"]).then_inc(L, 16)
                    act.dma_start(v2[:, :], a["v2"]).then_inc(L, 16)
                    act.dma_start(gate[:, :, :], a["gate"]).then_inc(L, 16)

                @block.tensor
                def _(pe):
                    pe.wait_ge(loads["embed"], 16 * 8)
                    for j in range(B // PB):
                        if j >= 2:
                            pe.wait_ge(emb_out, j - 1)
                        for k in range(PK):
                            mm = nc.tensor.matmul(ring[j % 2][0:PB * NP, 0, :],
                                                  patches[:, k, PB * NP * j:PB * NP * (j + 1)], w_tok[:, k, :],
                                                  start=(k == 0), stop=(k == PK - 1))
                        mm.then_inc(emb_mm, 1)
                    pe.wait_ge(bb_set, 4)
                    pe.wait_ge(loads["attn1"], 16 * 8)
                    for col, n, which in ((0, D, 0), (D, D, 1), (2 * D, D, 1)):
                        o = (ps_qk if col < 512 else ps_v)[0:R[0], col % 512:col % 512 + n]
                        for k in range(KD):
                            mm = nc.tensor.matmul(o, nrm_bb[:, k, which, :], w_qkv[1][:, k, col:col + n],
                                                  start=(k == 0), stop=(k == KD - 1))
                    mm.then_inc(bias_mm, 1)

                @block.vector
                def _(dve):
                    link = Chain(dve, stats_l)
                    nc.vector.memset(bst[:, :, :], 1.0).then_inc(st_set, 1)
                    dve.wait_ge(loads["embed"], 16 * 8)
                    nc.vector.tensor_tensor(cls0[:, :], cls0[:, :], pos0[:, :], ALU.add).then_inc(emb_add, 1)
                    nc.vector.tensor_tensor(pos2[:, :], pos2[:, :], tokb[:, :], ALU.add).then_inc(emb_add, 1)
                    dve.wait_ge(emb_add, 2)
                    nc.vector.tensor_copy(h[0:1, 0:2 * B:2, :],
                                          cls0[:, :].unsqueeze(1).to_broadcast([1, B, D])).then_inc(cls_done, 1)
                    for j in range(B // PB):
                        dve.wait_ge(emb_mm, j + 1)
                        nc.vector.tensor_tensor(stage[:, j, :], ring[j % 2][0:PB * NP, 0, :], pos2[:, :],
                                                ALU.add).then_inc(emb_out, 1)
                    dve.wait_ge(loads["attn1"], 16 * 8)
                    for k in range(KD):
                        for w in range(2):
                            nc.vector.tensor_copy(nrm_bb[:, k, w, :], nrm_b[:, k, w:w + 1].to_broadcast([128, R[0]])).then_inc(bb_set, 1)
                    dve.wait_ge(loads["consts"], 16 * 11)
                    for t, x in ((identb, ident), (selh, selh_f), (mask_s, mask_sf), (mask_t, mask_tf)):
                        nc.vector.tensor_copy(t[:], x[:])
                    dve.wait_ge(loads["txt"], 32)
                    dve.wait_ge(st_set, 1)
                    dve.wait_ge(cls_done, 1)
                    dve.wait_ge(moved, 16 * B)
                    for t in range(2 * B):
                        nc.vector.bn_stats(bst[0:R[t % 2], t, :], h[0:R[t % 2], t, :])
                    dve.wait_ge(bias_mm, 1)
                    nc.vector.tensor_tensor(b_qkv[1][:, 0:512], b_qkv[1][:, 0:512], ps_qk[0:R[0], :], ALU.add)
                    nc.vector.tensor_tensor(b_qkv[1][:, 512:768], b_qkv[1][:, 512:768], ps_v[0:R[0], 0:D], ALU.add)
                    for k in range(KD):
                        nc.vector.tensor_scalar(w_qkv[1][:, k, 0:D], w_qkv[1][:, k, 0:D], nrm_w[:, k, 0:1], None, ALU.mult)
                        nc.vector.tensor_scalar(w_qkv[1][:, k, D:3 * D], w_qkv[1][:, k, D:3 * D], nrm_w[:, k, 1:2], None, ALU.mult)

        def row_norms(dve, link, second=False):
            link(nc.vector.tensor_tensor(mean[:, :], bst[:, :, 1], bst[:, :, 4], ALU.add))
            link(nc.vector.tensor_tensor(vtmp[:, :], bst[:, :, 1], bst[:, :, 4], ALU.subtract))
            link(nc.vector.tensor_tensor(vtmp[:, :], vtmp[:, :], vtmp[:, :], ALU.mult))
            link(nc.vector.tensor_tensor(var[:, :], bst[:, :, 2], bst[:, :, 5], ALU.add))
            link(nc.vector.tensor_scalar(vtmp[:, :], vtmp[:, :], 0.25, None, ALU.mult))
            link(nc.vector.scalar_tensor_tensor(out=var[:, :], in0=var[:, :], scalar=1.0 / D, in1=vtmp[:, :], op0=ALU.mult, op1=ALU.add))
            link(nc.vector.tensor_scalar(mean[:, :], mean[:, :], 0.5, None, ALU.mult))
            link(nc.vector.tensor_scalar(vtmp[:, :], var[:, :], EPS, None, ALU.add))
            first_rsqrt(nc, dve, link, rs[:, :], rs_i, vtmp2[:, :], vtmp[:, :])
            if second:
                link(nc.vector.tensor_tensor(vtmp2[:, :], rs[:, :], rs[:, :], ALU.mult))
                link(nc.vector.tensor_tensor(vtmp2[:, :], vtmp2[:, :], var[:, :], ALU.mult))
                link(nc.vector.tensor_scalar(vtmp2[:, :], vtmp2[:, :], EPS, None, ALU.add))
                first_rsqrt(nc, dve, link, vtmp[:, :], vtmp[:, :].bitcast(I32), ratio[:, :], vtmp2[:, :])
                link(nc.vector.tensor_tensor(rs[:, :], rs[:, :], vtmp[:, :], ALU.mult))
                link(nc.vector.tensor_tensor(ratio[:, :], vtmp[:, :], vtmp2[:, :], ALU.mult))

        def row_stats(dve, b, resid_done):
            for c in range(2):
                dve.wait_ge(st_set, 1)
                dve.wait_ge(resid_done, b * 2 + c + 1)
                nc.vector.bn_stats(bst[0:R[c], bass.ds(b * 2 + c, 1), :].squeeze(1), h[0:R[c], bass.ds(b * 2 + c, 1), :].squeeze(1))

        def normed(b, c, xhat, done):
            r, t = R[c], 2 * b + c
            nc.vector.tensor_scalar(xhat[0:r, c, :], h[0:r, bass.ds(t, 1), :],
                                    mean[0:r, bass.ds(t, 1)], rs[0:r, bass.ds(t, 1)], ALU.subtract, ALU.mult).then_inc(done, 1)

        def attention(layer):
            causal = layer == 0
            with ExitStack() as e:
                def s(name):
                    return sem(f"{name}_{layer}", e)

                def t_(name, shape, dt=F32):
                    return sb(f"{name}_{layer}", shape, dt, e)

                xhat = t_("xhat", [R[0], 2, D])
                xT = t_("xT", [128, KD, 168])
                qk = t_("qk", [R[0], 2, 2 * H, HD])
                ru = t_("ru", [R[0], 2, 2 * H, HD])
                rw = t_("rw", [R[0], 2, 2 * H, HD])
                hl = t_("hl", [R[0], 2, 2 * H, 4, HD], F16)
                vaug = [t_(f"vaug{p}", [R[0], 2, H, 32]) for p in range(2)]
                kst = [t_(f"kst{p}", [128, H // 2, 166], F16) for p in range(2)]
                qA = [t_(f"qA{p}", [128, H // 2, 166], F16) for p in range(2)]
                qB = [t_(f"qB{p}", [128, H // 2, 166], F16) for p in range(2)]
                mx = t_("mx", [R[0], 2, H])
                nm = t_("nm", [R[0], 2, H], BF16)
                nmT = t_("nmT", [128, 168], BF16)
                prob = [[t_(f"prob{p}{c}", [R[0], G, T]) for c in range(2)] for p in range(2)]
                oT = t_("oT", [128, NG, T])
                rinv = t_("rinv", [128, 2, T])
                yT = t_("yT", [128, NG, T])
                per = t_("per", [R[0], 2])
                rad2 = t_("rad2", [R[0], 2])
                hs1 = t_("hs1", [R[0], 2, 2 * H])
                hs2 = t_("hs2", [R[0], 2, 2 * H])
                hx = t_("hx", [R[0], 2, 2 * H])
                hy = t_("hy", [R[0], 2, 2 * H])
                hz = t_("hz", [R[0], 2, 2 * H])
                hv = t_("hv", [R[0], 2, 2 * H])

                start_l, chain_s = s("start_l"), s("chain")
                set_ok = s("buffers_set")
                xhat_ready, xhatT_done, xT_ready = s("xhat_ready"), s("xhatT_done"), s("xT_ready")
                qkv_done, qkv_read = s("qkv_done"), s("qkv_read")
                roped, pool_l = s("roped"), s("pool_l")
                centred, squared, scaled, normed_qk = s("centred"), s("squared"), s("scaled"), s("normed_qk")
                summed = s("summed")
                hi_ready, lo_ready = s("hi_ready"), s("lo_ready")
                kT_done, qT_done, k_ready, q_ready = s("kT_done"), s("qT_done"), s("k_ready"), s("q_ready")
                s_ready, max_done, nm_ready, nmT_done, nmT_ready = s("s_ready"), s("max_done"), s("nm_ready"), s("nmT_done"), s("nmT_ready")
                st_ready, exp_done, pv_done, oT_done = s("st_ready"), s("exp_done"), s("pv_done"), s("oT_done")
                sums_ready, recip_done, y_ready = s("sums_ready"), s("recip_done"), s("y_ready")
                proj_done, resid_done, stats_done = s("proj_done"), s("resid_done"), s("stats_done")

                t16 = ps_t[:, :].bitcast(F16)
                tb16 = ps_t[:, :].bitcast(BF16)

                def q_of(hd, p):
                    return (qA, qB)[hd % 2][p]

                def key_cols(c):
                    return R[0] if causal and c == 0 else T

                def run(eng, project, attend):
                    project(0, 0)
                    with eng.Fori(0, B // 2 - 1) as i:
                        attend(i * 2, 0, i * 2 + 1)
                        attend(i * 2 + 1, 1, i * 2 + 2)
                    attend(B - 2, 0, B - 1)
                    attend(B - 1, 1, None)

                with nc.Block() as block:

                    @block.vector
                    def _(dve):
                        link = Chain(dve, start_l)
                        for p in range(2):
                            nc.vector.memset(vaug[p][:, :, :, :], 0.0).then_inc(set_ok, 1)
                            nc.vector.memset(qA[p][64:128, :, :], 0.0).then_inc(set_ok, 1)
                            nc.vector.memset(qB[p][0:64, :, :], 0.0).then_inc(set_ok, 1)
                        nc.vector.memset(nmT[:, :], 0.0).then_inc(set_ok, 1)
                        nc.vector.memset(per[:, :], 1.0).then_inc(set_ok, 1)
                        nc.vector.memset(hx[:, :, :], 1.0).then_inc(set_ok, 1)
                        dve.wait_ge(set_ok, 9)
                        for p in range(2):
                            nc.vector.memset(vaug[p][:, :, :, HD:HD + 1], 1.0).then_inc(set_ok, 1)
                        row_norms(dve, link, second=layer == 1)
                        dve.wait_ge(loads["attn0"], 48)
                        dve.wait_ge(set_ok, 11)
                        if layer == 1:
                            dve.wait_ge(loads["attn1"], 16 * 8)
                        link = Chain(dve, chain_s, 19 if layer == 1 else 0)

                        def xhats(b):
                            dve.wait_ge(xhatT_done, b * 2)
                            for c in range(2):
                                normed(b, c, xhat, xhat_ready)

                        def qkv_in(b, p, c):
                            r = R[c]
                            dve.wait_ge(qkv_done, b * 2 + c + 1)
                            dve.wait_ge(roped, b * 2)
                            nc.vector.tensor_tensor(qk[0:r, c, :, :].rearrange("r h d -> r (h d)"), ps_qk[0:r, :],
                                                    b_qkv[layer][0:r, 0:512], ALU.add).then_inc(qkv_read, 1)
                            nc.vector.tensor_tensor(vaug[p][0:r, c, :, 0:HD], ps_v[0:r, 0:D].rearrange("r (h d) -> r h d", h=H),
                                                    b_qkv[layer][0:r, 512:768].rearrange("r (h d) -> r h d", h=H),
                                                    ALU.add).then_inc(qkv_read, 1)
                            if layer == 1:
                                nc.vector.tensor_tensor(per[0:r, c:c + 1], ps_v[0:r, D:D + 1],
                                                        ratio[0:r, bass.ds(b * 2 + c, 1)], ALU.mult).then_inc(qkv_read, 1)

                        def head_norms(b):
                            link.start(b)
                            dve.wait_ge(qkv_read, b * 6 + 6)
                            link(nc.vector.tensor_scalar(per[:, :], per[:, :], rh_b[:, 0:1], 0.01, ALU.add, ALU.mult))
                            link(nc.vector.tensor_scalar(per[:, :], per[:, :], 0.5, 2.0, ALU.max, ALU.min))
                            link(nc.vector.tensor_tensor(rad2[:, :], per[:, :], per[:, :], ALU.mult))
                            for c in range(2):
                                r = R[c]
                                dve.wait_ge(roped, b * 2 + c + 1)
                                nc.vector.tensor_reduce(hs1[0:r, c, :], ru[0:r, c, :, :], AX.X, ALU.add).then_inc(summed, 1)
                                dve.wait_ge(summed, b * 2 + c + 1)
                                nc.vector.tensor_scalar(hs2[0:r, c, :], hs1[0:r, c, :], -1.0 / HD, None, ALU.mult).then_inc(scaled, 1)
                            for c in range(2):
                                r = R[c]
                                dve.wait_ge(squared, b * 2 + c + 1)
                                link(nc.vector.tensor_reduce(hs1[0:r, c, :], rw[0:r, c, :, :], AX.X, ALU.add))
                                link(nc.vector.tensor_scalar(hx[0:r, c, :], hs1[0:r, c, :], rad2[0:r, c:c + 1], 1.0 / HD, ALU.mult, ALU.mult))
                            link(nc.vector.tensor_scalar(hv[:, :, :], hx[:, :, :], EPS, None, ALU.add))
                            first_rsqrt(nc, dve, link, hy[:, :, :], hy[:, :, :].bitcast(I32), hz[:, :, :], hv[:, :, :])

                        def head_scale(b):
                            for c in range(2):
                                r = R[c]
                                nc.vector.tensor_scalar(hz[0:r, c, :], hy[0:r, c, :], per[0:r, c:c + 1], None, ALU.mult).then_inc(scaled, 1)
                            for c in range(2):
                                r = R[c]
                                dve.wait_ge(scaled, b * 6 + 3 + c)
                                nc.vector.tensor_tensor(ru[0:r, c, :, :], ru[0:r, c, :, :],
                                                        hz[0:r, c, :].unsqueeze(2).to_broadcast([r, 2 * H, HD]), ALU.mult).then_inc(scaled, 1)

                        def lows(b):
                            for c in range(2):
                                r = R[c]
                                dve.wait_ge(hi_ready, b * 2 + c + 1)
                                nc.vector.tensor_tensor(hl[0:r, c, :, 1, :], ru[0:r, c, :, :], hl[0:r, c, :, 0, :],
                                                        ALU.subtract).then_inc(lo_ready, 1)
                            for c in range(2):
                                r = R[c]
                                dve.wait_ge(lo_ready, b * 6 + 2 + 2 * c)
                                nc.vector.tensor_copy(hl[0:r, c, 0:H, 2:4, :], hl[0:r, c, 0:H, 0:2, :]).then_inc(lo_ready, 1)
                                nc.vector.tensor_copy(hl[0:r, c, H:2 * H, 3:1:-1, :], hl[0:r, c, H:2 * H, 0:2, :]).then_inc(lo_ready, 1)

                        def q_in(b, p):
                            for c in range(2):
                                r = R[c]
                                dve.wait_ge(qT_done, b * 2 + c + 1)
                                for lo, q in ((0, qA[p]), (64, qB[p])):
                                    nc.vector.tensor_copy(q[lo:lo + 64, :, O[c]:O[c] + r],
                                                          t16[lo:lo + 64, 0:672].rearrange("p (h t) -> p h t", h=H // 2)[:, :, 0:r]).then_inc(q_ready, 1)

                        def maxes(b, n):
                            c, g = divmod(n, NG)
                            dve.wait_ge(s_ready, b * 8 + n + 1)
                            nc.vector.tensor_reduce(mx[0:R[c], c, G * g:G * g + G], ring[n % 2][0:R[c], :, 0:key_cols(c)],
                                                    AX.X, ALU.max).then_inc(max_done, 1)

                        def project(b, p):
                            xhats(b)
                            for c in range(2):
                                qkv_in(b, p, c)
                            if layer == 1:
                                head_norms(b)
                                head_scale(b)
                            lows(b)
                            q_in(b, p)

                        def attend(b, p, nb):
                            if nb is not None:
                                xhats(nb)
                            for n in range(8):
                                maxes(b, n)
                                if nb is not None and n % 4 == 3:
                                    qkv_in(nb, 1 - p, n // 4)
                            dve.wait_ge(max_done, b * 8 + 8)
                            for c in range(2):
                                nc.vector.tensor_scalar(nm[0:R[c], c, :], mx[0:R[c], c, :], -1.0, None, ALU.mult).then_inc(nm_ready, 1)
                            dve.wait_ge(nmT_done, b * 1 + 1)
                            nc.vector.tensor_copy(nmT[0:H, 0:T], tb16[0:H, 0:T]).then_inc(nmT_ready, 1)
                            if nb is not None and layer == 1:
                                head_norms(nb)
                                head_scale(nb)
                            for g in range(NG):
                                dve.wait_ge(sums_ready, b * 4 + g + 1)
                                nc.vector.reciprocal(rinv[:, g % 2, :], two[g % 2][:, 0:T]).then_inc(recip_done, 1)
                                dve.wait_ge(recip_done, b * 4 + g + 1)
                                nc.vector.tensor_tensor(yT[:, g, :], oT[:, g, :], rinv[:, g % 2, :], ALU.mult).then_inc(y_ready, 1)
                            for c in range(2):
                                r, t = R[c], b * 2 + c
                                dve.wait_ge(proj_done, b * 2 + c + 1)
                                nc.vector.tensor_tensor(h[0:r, bass.ds(t, 1), :].squeeze(1), h[0:r, bass.ds(t, 1), :].squeeze(1),
                                                        two[c][0:r, 0:D], ALU.add).then_inc(resid_done, 1)
                            row_stats(dve, b, resid_done)
                            if nb is not None:
                                lows(nb)
                                q_in(nb, 1 - p)

                        run(dve, project, attend)

                    @block.gpsimd
                    def _(pool):
                        pool.wait_ge(loads["consts"], 16 * 11)
                        npl = 4 if layer == 1 else 3

                        def project(b, p=0):
                            for c in range(2):
                                r = R[c]
                                cs = cos_t[layer][0:r, c, :].unsqueeze(1).to_broadcast([r, 2 * H, HD])
                                pool.wait_ge(qkv_read, b * (6 if layer == 1 else 4) + (3 if layer == 1 else 2) * c + 1)
                                if layer == 0:
                                    pool.wait_ge(lo_ready, b * 6)
                                else:
                                    pool.wait_ge(hi_ready, b * 2)
                                    pool.wait_ge(lo_ready, b * 6)
                                x = b * 2 + c
                                nc.gpsimd.tensor_tensor(ru[0:r, c, :, :], qk[0:r, c, :, :], cs, ALU.mult).then_inc(pool_l, 1)
                                for half in range(2):
                                    o = slice(8 * half, 8 * half + 8)
                                    i = slice(8 - 8 * half, 16 - 8 * half)
                                    sn = sin_t[layer][0:r, c, o].unsqueeze(1).to_broadcast([r, 2 * H, 8])
                                    nc.gpsimd.tensor_tensor(rw[0:r, c, :, o], qk[0:r, c, :, i], sn, ALU.mult).then_inc(pool_l, 1)
                                pool.wait_ge(pool_l, x * 3 + 3)
                                nc.gpsimd.tensor_tensor(ru[0:r, c, :, :], ru[0:r, c, :, :], rw[0:r, c, :, :], ALU.add).then_inc(roped, 1)
                            if layer == 1:
                                for c in range(2):
                                    r = R[c]
                                    pool.wait_ge(scaled, b * 6 + c + 1)
                                    nc.gpsimd.tensor_tensor(ru[0:r, c, :, :], ru[0:r, c, :, :],
                                                            hs2[0:r, c, :].unsqueeze(2).to_broadcast([r, 2 * H, HD]), ALU.add).then_inc(centred, 1)
                                for c in range(2):
                                    r = R[c]
                                    pool.wait_ge(scaled, b * 6 + 5 + c)
                                    nc.gpsimd.tensor_tensor(ru[0:r, c, :, :], ru[0:r, c, :, :],
                                                            ln_w[0:r, :].unsqueeze(1).to_broadcast([r, 2 * H, HD]), ALU.mult).then_inc(normed_qk, 1)
                                    pool.wait_ge(normed_qk, b * 4 + 2 * c + 1)
                                    nc.gpsimd.tensor_tensor(ru[0:r, c, :, :], ru[0:r, c, :, :],
                                                            ln_b[0:r, :].unsqueeze(1).to_broadcast([r, 2 * H, HD]), ALU.add).then_inc(normed_qk, 1)

                        def attend(b, p, nb):
                            if nb is not None:
                                project(nb)

                        run(pool, project, attend)

                    @block.scalar
                    def _(act):
                        def xT_in(b):
                            act.wait_ge(xhatT_done, b * 2 + 2)
                            act.wait_ge(qkv_done, b * 2)
                            nc.scalar.copy(xT[:, :, 0:T], ps_t[:, 0:336].rearrange("p (k t) -> p k t", k=KD)[:, :, 0:T]).then_inc(xT_ready, 1)

                        def squares(b, c):
                            r = R[c]
                            act.wait_ge(centred, b * 2 + c + 1)
                            nc.scalar.activation(rw[0:r, c, :, :], ru[0:r, c, :, :], ACT.Square).then_inc(squared, 1)

                        def highs(b, c):
                            r = R[c]
                            if layer == 1:
                                act.wait_ge(normed_qk, b * 4 + 2 * c + 2)
                            else:
                                act.wait_ge(roped, b * 2 + c + 1)
                            act.wait_ge(kT_done, b * 2)
                            act.wait_ge(qT_done, b * 2)
                            nc.scalar.copy(hl[0:r, c, :, 0, :], ru[0:r, c, :, :]).then_inc(hi_ready, 1)

                        def k_in(b, p):
                            for c in range(2):
                                r = R[c]
                                act.wait_ge(kT_done, b * 2 + c + 1)
                                nc.scalar.copy(kst[p][:, :, O[c]:O[c] + r],
                                               t16[:, 0:672].rearrange("p (h t) -> p h t", h=H // 2)[:, :, 0:r]).then_inc(k_ready, 1)

                        def exps(b, g, c):
                            m = 2 * g + c
                            r, q0 = R[c], (O[c] if causal else 0)
                            act.wait_ge(st_ready, b * 8 + m + 1)
                            act.wait_ge(pv_done, b * 4 + max(g - 1, 0))
                            nc.scalar.activation(prob[g % 2][c][0:r, :, q0:T], ring[m % 2][0:r, :, q0:T], ACT.Exp,
                                                 scale=HD ** -0.5).then_inc(exp_done, 1)

                        def out_in(b, g):
                            act.wait_ge(pv_done, b * 4 + g + 1)
                            act.wait_ge(y_ready, b * 4)
                            nc.scalar.copy(oT[:, g, :], ps_o[:, 0:T]).then_inc(oT_done, 1)

                        def project(b, p):
                            xT_in(b)
                            for c in range(2):
                                if layer == 1:
                                    squares(b, c)
                            for c in range(2):
                                highs(b, c)
                            k_in(b, p)

                        def attend(b, p, nb):
                            if nb is not None:
                                xT_in(nb)
                            for g in range(NG):
                                for c in range(2):
                                    exps(b, g, c)
                                if nb is not None and layer == 1 and g in (1, 2):
                                    squares(nb, g - 1)
                                if g >= 1:
                                    out_in(b, g - 1)
                            out_in(b, NG - 1)
                            if nb is not None:
                                for c in range(2):
                                    highs(nb, c)
                                k_in(nb, 1 - p)

                        run(act, project, attend)

                    @block.tensor
                    def _(pe):
                        pe.wait_ge(loads["consts"], 16 * 11)
                        pe.wait_ge(loads["attn0"], 48)
                        pe.wait_ge(set_ok, 11)

                        def xhat_turn(b, first=False):
                            for c in range(2):
                                r = R[c]
                                pe.wait_ge(xhat_ready, b * 2 + c + 1)
                                if c == 0:
                                    pe.wait_ge(q_ready, b * 4)
                                    pe.wait_ge(k_ready, b * 2)
                                for k in range(KD):
                                    mm = nc.tensor.transpose(ps_t[:, 168 * k + O[c]:168 * k + O[c] + r], xhat[0:r, c, 128 * k:128 * k + 128],
                                                             ident[0:r, 0:r])
                                mm.then_inc(xhatT_done, 1)

                        def qkv(b, c):
                            r = R[c]
                            pe.wait_ge(xT_ready, b * 1 + 1)
                            pe.wait_ge(qkv_read, (b * 2 + c) * (3 if layer == 1 else 2))
                            for col, n, o in ((0, 512, ps_qk), (512, D + layer, ps_v)):
                                for k in range(KD):
                                    mm = nc.tensor.matmul(o[0:r, 0:n], xT[:, k, O[c]:O[c] + r], w_qkv[layer][:, k, col:col + n],
                                                          start=(k == 0), stop=(k == KD - 1))
                            mm.then_inc(qkv_done, 1)

                        def stacks(b):
                            for c in range(2):
                                r = R[c]
                                if c == 0:
                                    pe.wait_ge(xT_ready, b * 1 + 1)
                                else:
                                    pe.wait_ge(q_ready, b * 4 + 2)
                                pe.wait_ge(lo_ready, b * 6 + 4 + 2 * c)
                                for i in range(H // 2):
                                    mm = nc.tensor.transpose(t16[:, 84 * i:84 * i + r],
                                                             hl[0:r, c, H + 2 * i:H + 2 * i + 2, :, :].rearrange("r h s d -> r (h s d)"),
                                                             ident16[0:r, 0:r])
                                mm.then_inc(kT_done, 1)
                                pe.wait_ge(k_ready, b * 2 + c + 1)
                                for i in range(H // 2):
                                    mm = nc.tensor.transpose(t16[:, 84 * i:84 * i + r],
                                                             hl[0:r, c, 2 * i:2 * i + 2, :, :].rearrange("r h s d -> r (h s d)"),
                                                             ident16[0:r, 0:r])
                                mm.then_inc(qT_done, 1)

                        def scores(b, p, n):
                            c, g = divmod(n, NG)
                            r, nk = R[c], key_cols(c)
                            if n == 0:
                                pe.wait_ge(k_ready, b * 2 + 2)
                                pe.wait_ge(q_ready, b * 4 + 4)
                            if n >= 2:
                                pe.wait_ge(max_done, b * 8 + n - 1)
                            for j in range(G):
                                hd = G * g + j
                                mm = nc.tensor.matmul(ring[n % 2][0:r, j, 0:nk], q_of(hd, p)[:, hd // 2, O[c]:O[c] + r],
                                                      kst[p][:, hd // 2, 0:nk], start=True, stop=not causal)
                                if causal:
                                    mm = nc.tensor.matmul(ring[n % 2][0:r, j, 0:nk], identb[0:R[0], 0:r],
                                                          mask_s[0:R[0], c, 0:nk], start=False, stop=True)
                            mm.then_inc(s_ready, 1)

                        def scores_T(b, p, m):
                            g, c = divmod(m, 2)
                            r, q0 = R[c], (O[c] if causal else 0)
                            if m == 0:
                                pe.wait_ge(nmT_ready, b * 1 + 1)
                            if m >= 2:
                                pe.wait_ge(exp_done, b * 8 + m - 1)
                            for j in range(G):
                                hd = G * g + j
                                o = ring[m % 2][0:r, j, q0:T]
                                nc.tensor.matmul(o, kst[p][:, hd // 2, O[c]:O[c] + r], q_of(hd, p)[:, hd // 2, q0:T],
                                                 start=True, stop=False)
                                if causal:
                                    nc.tensor.matmul(o, identb[0:R[0], 0:r], mask_t[0:R[0], c, q0:T], start=False, stop=False)
                                mm = nc.tensor.matmul(o, selh[:, hd, 0:r], nmT[:, q0:T], start=False, stop=True)
                            mm.then_inc(st_ready, 1)

                        def values(b, p, g):
                            pe.wait_ge(exp_done, b * 8 + 2 * g + 2)
                            pe.wait_ge(oT_done, b * 4 + g)
                            for c in range(2):
                                r, q0 = R[c], (O[c] if causal else 0)
                                for j in range(G):
                                    mm = nc.tensor.matmul(ps_o[32 * j:32 * j + 32, q0:T],
                                                          vaug[p][0:r, c, G * g + j, :], prob[g % 2][c][0:r, j, q0:T],
                                                          start=(c == 0), stop=(c == 1))
                            mm.then_inc(pv_done, 1)

                        def attend(b, p, nb):
                            if nb is not None:
                                xhat_turn(nb)
                            for n in range(8):
                                scores(b, p, n)
                                if nb is not None and n % 4 == 3:
                                    pe.wait_ge(resid_done, b * 2)
                                    qkv(nb, n // 4)
                            pe.wait_ge(nm_ready, b * 2 + 2)
                            if nb is not None:
                                pe.wait_ge(xT_ready, nb + 1)
                            for c in range(2):
                                mm = nc.tensor.transpose(tb16[0:H, O[c]:O[c] + R[c]], nm[0:R[c], c, :], identb[0:R[c], 0:R[c]])
                            mm.then_inc(nmT_done, 1)
                            scores_T(b, p, 0)
                            scores_T(b, p, 1)
                            for g in range(NG):
                                if g + 1 < NG:
                                    scores_T(b, p, 2 * g + 2)
                                    scores_T(b, p, 2 * g + 3)
                                values(b, p, g)
                            if nb is not None:
                                pe.wait_ge(qkv_read, (b + 1) * (3 if layer == 1 else 2) * 2 + (3 if layer == 1 else 2) * 2)
                            for g in range(NG):
                                pe.wait_ge(oT_done, b * 4 + g + 1)
                                pe.wait_ge(recip_done, b * 4 + max(g - 1, 0))
                                nc.tensor.matmul(two[g % 2][:, 0:T], bsel[:, :], oT[:, g, :], start=True, stop=True).then_inc(sums_ready, 1)
                            pe.wait_ge(y_ready, b * 4 + 4)
                            for c in range(2):
                                for g in range(NG):
                                    mm = nc.tensor.matmul(two[c][0:R[c], 0:D], yT[:, g, O[c]:O[c] + R[c]],
                                                          w_out[layer][:, g, :], start=(g == 0), stop=(g == NG - 1))
                                mm.then_inc(proj_done, 1)
                            if nb is not None:
                                stacks(nb)

                        def project(b, p):
                            xhat_turn(b)
                            for c in range(2):
                                qkv(b, c)
                            stacks(b)

                        run(pe, project, attend)

        def feed_forward():
            with ExitStack() as e:
                xhat = sb("xhat_f", [R[0], 2, D], to=e)
                xT = sb("xT_f", [128, KD, 168], to=e)
                pT = sb("pT_f", [RANK + 1, T], to=e)
                hT = [sb(f"hT_f{i}", [128, 4, T], to=e) for i in range(2)]
                qT = sb("qT_f", [RANK + 1, T], to=e)
                start_l, set_ok = sem("start_l_f", e), sem("set_ok_f", e)
                xhat_ready, xhatT_done, xT_ready = sem("xhat_ready_f", e), sem("xhatT_done_f", e), sem("xT_ready_f", e)
                p_done, p_ready, h_done, gelu_done = sem("p_done", e), sem("p_ready", e), sem("h_done", e), sem("gelu_done", e)
                q_done, q_ready, f_done, resid_done, stats_done = (sem("q_done", e), sem("q_ready_f", e), sem("f_done", e),
                                                                   sem("resid_done_f", e), sem("stats_done_f", e))
                with nc.Block() as block:

                    @block.vector
                    def _(dve):
                        nc.vector.memset(pT[RANK:RANK + 1, :], 1.0).then_inc(set_ok, 1)
                        nc.vector.memset(qT[RANK:RANK + 1, :], 1.0).then_inc(set_ok, 1)
                        row_norms(dve, Chain(dve, start_l))

                        def xhats(b):
                            dve.wait_ge(xhatT_done, b * 2)
                            for c in range(2):
                                normed(b, c, xhat, xhat_ready)

                        def finish(b):
                            for c in range(2):
                                r, t = R[c], b * 2 + c
                                dve.wait_ge(f_done, b * 2 + c + 1)
                                nc.vector.tensor_tensor(h[0:r, bass.ds(t, 1), :].squeeze(1), h[0:r, bass.ds(t, 1), :].squeeze(1),
                                                        (ps_v, ps_o)[c][0:r, 0:D], ALU.add).then_inc(resid_done, 1)
                            row_stats(dve, b, resid_done)

                        def turn(b, more):
                            if more:
                                xhats(b + 1)
                            dve.wait_ge(p_done, b * 1 + 1)
                            nc.vector.tensor_copy(pT[0:RANK, :], ps_qk[0:RANK, 0:T]).then_inc(p_ready, 1)
                            dve.wait_ge(q_done, b * 1 + 1)
                            nc.vector.tensor_copy(qT[0:RANK, :], ps_o[0:RANK, 0:T]).then_inc(q_ready, 1)
                            finish(b)

                        xhats(0)
                        with dve.Fori(0, B - 1) as i:
                            turn(i, True)
                        turn(B - 1, False)

                    @block.scalar
                    def _(act):
                        def turn(b):
                            act.wait_ge(xhatT_done, b * 2 + 2)
                            act.wait_ge(p_done, b * 1)
                            nc.scalar.copy(xT[:, :, 0:T], ps_t[:, 0:336].rearrange("p (k t) -> p k t", k=KD)[:, :, 0:T]).then_inc(xT_ready, 1)
                            for i in range(2):
                                act.wait_ge(h_done, b * 2 + i + 1)
                                act.wait_ge(q_done, b * 1)
                                nc.scalar.activation(hT[i][:, :, :], ring[i][:, :, 0:T], ACT.Gelu_apprx_tanh).then_inc(gelu_done, 1)

                        with act.Fori(0, B) as i:
                            turn(i)

                    @block.tensor
                    def _(pe):
                        pe.wait_ge(loads["ffn0"], 16 * 5)
                        pe.wait_ge(set_ok, 2)

                        def turn_x(b):
                            pe.wait_ge(xT_ready, b * 1)
                            for c in range(2):
                                r = R[c]
                                pe.wait_ge(xhat_ready, b * 2 + c + 1)
                                for k in range(KD):
                                    mm = nc.tensor.transpose(ps_t[:, 168 * k + O[c]:168 * k + O[c] + r], xhat[0:r, c, 128 * k:128 * k + 128],
                                                             ident[0:r, 0:r])
                                mm.then_inc(xhatT_done, 1)

                        def turn(b, more):
                            pe.wait_ge(xT_ready, b * 1 + 1)
                            for k in range(KD):
                                mm = nc.tensor.matmul(ps_qk[0:RANK, 0:T], u1[:, k, :], xT[:, k, 0:T], start=(k == 0), stop=(k == KD - 1))
                            mm.then_inc(p_done, 1)
                            pe.wait_ge(p_ready, b * 1 + 1)
                            for i in range(2):
                                pe.wait_ge(gelu_done, b * 2)
                                for j in range(4):
                                    n = 4 * i + j
                                    mm = nc.tensor.matmul(ring[i][:, j, 0:T], v1[:, 128 * n:128 * n + 128], pT[:, :], start=True, stop=True)
                                mm.then_inc(h_done, 1)
                            if more:
                                turn_x(b + 1)
                            pe.wait_ge(resid_done, b * 2)
                            for n in range(8):
                                pe.wait_ge(gelu_done, b * 2 + n // 4 + 1)
                                mm = nc.tensor.matmul(ps_o[0:RANK, 0:T], u2[:, n, :], hT[n // 4][:, n % 4, :], start=(n == 0), stop=(n == 7))
                            mm.then_inc(q_done, 1)
                            pe.wait_ge(q_ready, b * 1 + 1)
                            pe.wait_ge(resid_done, b * 2)
                            for c in range(2):
                                nc.tensor.matmul((ps_v, ps_o)[c][0:R[c], 0:D], qT[:, O[c]:O[c] + R[c]], v2[:, :],
                                                 start=True, stop=True).then_inc(f_done, 1)

                        turn_x(0)
                        with pe.Fori(0, B - 1) as i:
                            turn(i, True)
                        turn(B - 1, False)

        def router(comb):
            with ExitStack() as e:
                xhat = sb("xhat_r", [R[0], 2, D], to=e)
                xT = sb("xT_r", [128, KD, 168], to=e)
                lg = sb("lg", [R[0], 2 * B, NE], to=e)
                val = sb("val", [R[0], 2 * B, NE], to=e)
                hot = [sb(f"hot{i}", [R[0], 2 * B, NE], to=e) for i in range(2)]
                best = [sb(f"best{i}", [R[0], 2 * B], to=e) for i in range(2)]
                idx = sb("idx", [R[0], 2 * B], to=e)
                ex = sb("ex", [R[0], 2 * B], to=e)
                wt = [sb(f"wt{i}", [R[0], 2 * B], to=e) for i in range(2)]
                chain_s, lg_set = sem("chain_r", e), sem("lg_set", e)
                xhat_ready, xhatT_done, xT_ready = sem("xhat_ready_r", e), sem("xhatT_done_r", e), sem("xT_ready_r", e)
                lg_done, lg_read, diff_done, exp_done = sem("lg_done", e), sem("lg_read", e), sem("diff_done", e), sem("exp_done_r", e)
                with nc.Block() as block:

                    @block.vector
                    def _(dve):
                        link = Chain(dve, chain_s)
                        nc.vector.memset(lg[:, :, :], 0.0).then_inc(lg_set, 1)
                        row_norms(dve, link)

                        def turn(b):
                            dve.wait_ge(xhatT_done, b * 2)
                            for c in range(2):
                                normed(b, c, xhat, xhat_ready)
                            for c in range(2):
                                r = R[c]
                                dve.wait_ge(lg_done, b * 2 + c + 1)
                                nc.vector.tensor_scalar(lg[0:r, bass.ds(b * 2 + c, 1), :].squeeze(1), (ps_v, ps_o)[c][0:r, 0:NE],
                                                        1.0, None, ALU.mult).then_inc(lg_read, 1)

                        dve.wait_ge(lg_set, 1)
                        with dve.Fori(0, B) as i:
                            turn(i)
                        dve.wait_ge(lg_read, 2 * B)
                        full = [R[0], 2 * B, NE]

                        def over(x):
                            return x[:, :].unsqueeze(2).to_broadcast(full)

                        io = iota[:, :].unsqueeze(1).to_broadcast(full)
                        for i in range(2):
                            link(nc.vector.tensor_reduce(best[i][:, :], lg[:, :, :], AX.X, ALU.max))
                            link(nc.vector.tensor_tensor(val[:, :, :], lg[:, :, :], over(best[i]), ALU.is_lt))
                            link(nc.vector.scalar_tensor_tensor(out=val[:, :, :], in0=val[:, :, :], scalar=float(NE), in1=io, op0=ALU.mult, op1=ALU.add))
                            link(nc.vector.tensor_reduce(idx[:, :], val[:, :, :], AX.X, ALU.min))
                            link(nc.vector.tensor_tensor(hot[i][:, :, :], io, over(idx), ALU.is_equal))
                            if i == 0:
                                link(nc.vector.scalar_tensor_tensor(out=lg[:, :, :], in0=hot[0][:, :, :], scalar=-3e38, in1=lg[:, :, :],
                                                                    op0=ALU.mult, op1=ALU.add))
                        nc.vector.tensor_tensor(ex[:, :], best[1][:, :], best[0][:, :], ALU.subtract).then_inc(diff_done, 1)
                        dve.wait_ge(exp_done, 1)
                        link(nc.vector.tensor_scalar(wt[0][:, :], ex[:, :], 1.0, None, ALU.add))
                        link(nc.vector.reciprocal(wt[0][:, :], wt[0][:, :]))
                        link(nc.vector.tensor_tensor(wt[1][:, :], ex[:, :], wt[0][:, :], ALU.mult))
                        for i in range(2):
                            link(nc.vector.tensor_tensor(hot[i][:, :, :], hot[i][:, :, :], over(wt[i]), ALU.mult))
                        nc.vector.tensor_tensor(comb[:, :, :], hot[0][:, :, :], hot[1][:, :, :], ALU.add)

                    @block.scalar
                    def _(act):
                        def turn(b):
                            act.wait_ge(xhatT_done, b * 2 + 2)
                            act.wait_ge(lg_done, b * 2)
                            nc.scalar.copy(xT[:, :, 0:T], ps_t[:, 0:336].rearrange("p (k t) -> p k t", k=KD)[:, :, 0:T]).then_inc(xT_ready, 1)

                        with act.Fori(0, B) as i:
                            turn(i)
                        act.wait_ge(diff_done, 1)
                        nc.scalar.activation(ex[:, :], ex[:, :], ACT.Exp).then_inc(exp_done, 1)

                    @block.tensor
                    def _(pe):
                        def turn(b):
                            pe.wait_ge(xT_ready, b * 1)
                            for c in range(2):
                                r = R[c]
                                pe.wait_ge(xhat_ready, b * 2 + c + 1)
                                for k in range(KD):
                                    mm = nc.tensor.transpose(ps_t[:, 168 * k + O[c]:168 * k + O[c] + r], xhat[0:r, c, 128 * k:128 * k + 128],
                                                             ident[0:r, 0:r])
                                mm.then_inc(xhatT_done, 1)
                            pe.wait_ge(xT_ready, b * 1 + 1)
                            pe.wait_ge(lg_read, b * 2)
                            for c in range(2):
                                for k in range(KD):
                                    mm = nc.tensor.matmul((ps_v, ps_o)[c][0:R[c], 0:NE], xT[:, k, O[c]:O[c] + R[c]], gate[:, k, :],
                                                          start=(k == 0), stop=(k == KD - 1))
                                mm.then_inc(lg_done, 1)

                        with pe.Fori(0, B) as i:
                            turn(i)

        def experts(comb, w1, w2):
            with ExitStack() as e:
                xhat = sb("xhat_m", [R[0], 2, D], to=e)
                xT = sb("xT_m", [128, KD, 168], to=e)
                hT = [sb(f"hT_m{i}", [128, 4, T], to=e) for i in range(2)]
                xhat_ready, xhatT_done, xT_ready = sem("xhat_ready_m", e), sem("xhatT_done_m", e), sem("xT_ready_m", e)
                h_done, silu_done, y_done, added = sem("h_done_m", e), sem("silu_done", e), sem("y_done", e), sem("added", e)
                out_sent = sem("out_sent", e)
                with nc.Block() as block:

                    @block.sync
                    def _(sp):
                        def send(b):
                            sp.wait_ge(added, b * (2 * NE) + 2 * NE)
                            for c in range(2):
                                sp.dma_start(out[bass.ds(b, 1), O[c]:O[c] + R[c], :].rearrange("b t d -> t b d"),
                                             h[0:R[c], bass.ds(b * 2 + c, 1), :]).then_inc(out_sent, 16)

                        with sp.Fori(0, B) as i:
                            send(i)
                        sp.wait_ge(out_sent, 16 * 2 * B)

                    @block.vector
                    def _(dve):
                        def turn(b):
                            dve.wait_ge(xhatT_done, b * 2)
                            for c in range(2):
                                normed(b, c, xhat, xhat_ready)
                            for x in range(NE):
                                for c in range(2):
                                    r, t = R[c], b * 2 + c
                                    dve.wait_ge(y_done, b * (2 * NE) + 2 * x + c + 1)
                                    if x:
                                        dve.wait_ge(added, b * (2 * NE) + 2 * x + c - 1)
                                    hh = h[0:r, bass.ds(t, 1), :].squeeze(1)
                                    nc.vector.scalar_tensor_tensor(out=hh, in0=(ps_qk, ps_o)[c][0:r, 0:D],
                                                                   scalar=comb[0:r, bass.ds(t, 1), x:x + 1].squeeze(1),
                                                                   in1=hh, op0=ALU.mult, op1=ALU.add).then_inc(added, 1)

                        with dve.Fori(0, B) as i:
                            turn(i)

                    @block.scalar
                    def _(act):
                        def turn(b):
                            act.wait_ge(xhatT_done, b * 2 + 2)
                            act.wait_ge(h_done, b * NE)
                            nc.scalar.copy(xT[:, :, 0:T], ps_t[:, 0:336].rearrange("p (k t) -> p k t", k=KD)[:, :, 0:T]).then_inc(xT_ready, 1)
                            for x in range(NE):
                                act.wait_ge(h_done, b * NE + x + 1)
                                act.wait_ge(y_done, b * (2 * NE) + max(2 * x - 2, 0))
                                nc.scalar.activation(hT[x % 2][:, :, :], ring[x % 2][:, :, 0:T], ACT.Silu).then_inc(silu_done, 1)

                        with act.Fori(0, B) as i:
                            turn(i)

                    @block.tensor
                    def _(pe):
                        pe.wait_ge(loads["moe"], 16 * 2 * NE)

                        def outs(b, x):
                            pe.wait_ge(silu_done, b * NE + x + 1)
                            for c in range(2):
                                r = R[c]
                                pe.wait_ge(added, b * (2 * NE) + max(2 * x + c - 1, 0))
                                for k in range(4):
                                    mm = nc.tensor.matmul((ps_qk, ps_o)[c][0:r, 0:D], hT[x % 2][:, k, O[c]:O[c] + r], w2[:, x, k, :],
                                                          start=(k == 0), stop=(k == 3))
                                mm.then_inc(y_done, 1)

                        def turn(b):
                            pe.wait_ge(xT_ready, b * 1)
                            for c in range(2):
                                r = R[c]
                                pe.wait_ge(xhat_ready, b * 2 + c + 1)
                                for k in range(KD):
                                    mm = nc.tensor.transpose(ps_t[:, 168 * k + O[c]:168 * k + O[c] + r], xhat[0:r, c, 128 * k:128 * k + 128],
                                                             ident[0:r, 0:r])
                                mm.then_inc(xhatT_done, 1)
                            pe.wait_ge(xT_ready, b * 1 + 1)
                            for x in range(NE):
                                pe.wait_ge(silu_done, b * NE + max(x - 1, 0))
                                for m in range(4):
                                    for k in range(KD):
                                        mm = nc.tensor.matmul(ring[x % 2][:, m, 0:T], w1[:, x, k, 128 * m:128 * m + 128], xT[:, k, 0:T],
                                                              start=(k == 0), stop=(k == KD - 1))
                                mm.then_inc(h_done, 1)
                                if x:
                                    outs(b, x - 1)
                            outs(b, NE - 1)

                        with pe.Fori(0, B) as i:
                            turn(i)

        attention(0)
        feed_forward()
        attention(1)
        with ExitStack() as e:
            comb = sb("comb", [R[0], 2 * B, NE], to=e)
            w1 = sb("w1", [128, NE, KD, EF], to=e)
            w2 = sb("w2", [128, NE, EF // 128, D], to=e)
            for x in range(NE):
                nc.sync.dma_start(w1[:, x, :, :], a["w1"][:, x, :, :]).then_inc(loads["moe"], 16)
                nc.sync.dma_start(w2[:, x, :, :], a["w2"][:, x, :, :]).then_inc(loads["moe"], 16)
            router(comb)
            experts(comb, w1, w2)


def layouts(v):
    import numpy as np

    f = np.float32
    c = np.ascontiguousarray
    x = v["x"].reshape(B, 3, 6, 16, 6, 16).transpose(1, 3, 5, 0, 2, 4).reshape(PK, 128, B * NP)

    def rows(w):
        return c(w.reshape(-1, 128, w.shape[-1]).transpose(1, 0, 2))

    def halves(w):
        return w.reshape(*w.shape[:-1], -1, 8, 2).swapaxes(-1, -2).reshape(w.shape)

    def heads_out(w, b):
        o = np.zeros((G, 32, NG, D), f)
        o[:, 0:HD] = w.reshape(NG, G, HD, D).transpose(1, 2, 0, 3)
        o[0, HD, 0] = b
        return o.reshape(128, NG, D)

    def chunks(t):
        o = np.zeros((R[0], 2, t.shape[1]), t.dtype)
        for k in range(2):
            o[0:R[k], k] = t[O[k]:O[k] + R[k]]
        return o

    q_w, kv_w = v["L1_attn_q_w"], v["L1_attn_kv_w"]
    q_b, kv_b = v["L1_attn_q_b"], v["L1_attn_kv_b"]
    pos = np.arange(T, dtype=f)
    scale0 = (f(2500) ** (f(2.0) * np.arange(8, dtype=f) / f(16))).astype(f)
    ang0 = pos[:, None] / scale0[None, :]
    mel = f(2595.0 * np.log10(1.0 + 4000.0 / 200.0))
    fb = f(200.0) * (np.power(f(10.0), np.linspace(0.0, mel, 8, dtype=f) / f(2595.0)).astype(f) - f(1.0)) / f(1000.0)
    ang1 = pos[:, None] * fb[None, :].astype(f)
    qi, ki = np.arange(T)[:, None], np.arange(T)[None, :]
    mask = np.where(ki <= qi, 0.0, -1e30).astype(f)
    bsel = np.zeros((128, 128), f)
    for j in range(G):
        bsel[32 * j + HD, 32 * j:32 * j + 32] = 1.0
    selh = np.zeros((128, H, R[0]), f)
    for k in range(H):
        selh[k, k] = 1.0
    s = {
        "patches": c(x.transpose(1, 0, 2)), "w_tok": rows(c(v["L0_tok_W"].T)), "tok_b": v["L0_tok_b"],
        "cls": v["L0_tok_cls_token"].reshape(1, D), "pos": v["L0_tok_pos_embedding"].reshape(NP + 1, D), "txt": v["txt"],
        "w_qkv0": rows(v["L0_attn_W_attn"]), "b_qkv0": v["L0_attn_b_attn"],
        "w_out0": heads_out(v["L0_attn_W_proj"], v["L0_attn_b_proj"]),
        "w_qkv1": rows(np.concatenate([halves(q_w), halves(kv_w[:, 0:D]), kv_w[:, D:], v["L1_attn_rh_w"]], axis=1)),
        "b_qkv1": np.concatenate([halves(q_b), halves(kv_b[0:D]), kv_b[D:]]),
        "w_out1": heads_out(v["L1_attn_out_w"], v["L1_attn_out_b"]),
        "nrm_w": c(np.stack([v["L1_attn_qn_w"], v["L1_attn_kvn_w"]]).reshape(2, KD, 128).transpose(2, 1, 0)),
        "nrm_b": c(np.stack([v["L1_attn_qn_b"], v["L1_attn_kvn_b"]]).reshape(2, KD, 128).transpose(2, 1, 0)),
        "ln_w": halves(v["L1_attn_ln_w"]), "ln_b": halves(v["L1_attn_ln_b"]), "rh_b": v["L1_attn_rh_b"],
        "u1": rows(v["L0_ffn_U1"]), "v1": np.concatenate([v["L0_ffn_V1"], v["L0_ffn_b1"][None]]),
        "u2": rows(v["L0_ffn_U2"]), "v2": np.concatenate([v["L0_ffn_V2"], v["L0_ffn_b2"][None]]),
        "gate": rows(v["L1_ffn_gate_w"]),
        "w1": c(v["L1_ffn_w1"].reshape(NE, KD, 128, EF).transpose(2, 0, 1, 3)),
        "w2": c(v["L1_ffn_w2"].reshape(NE, EF // 128, 128, D).transpose(2, 0, 1, 3)),
        "ident": np.eye(128, dtype=f), "ident16": np.eye(128, dtype=np.float16),
        "bsel": bsel, "selh": selh, "mask_s": chunks(mask), "mask_t": chunks(c(mask.T)),
        "iota": np.arange(NE, dtype=f),
    }
    for n, ang in enumerate((ang0, ang1)):
        co, si = np.cos(ang).astype(f), np.sin(ang).astype(f)
        s[f"cos{n}"] = chunks(np.concatenate([co, co], axis=1))
        s[f"sin{n}"] = chunks(np.concatenate([-si, si], axis=1))
    return {k: c(a) for k, a in s.items()}


def kernel(**inputs):
    import numpy as np
    import concourse.bacc as bacc
    from concourse.bass_utils import run_bass_kernel_spmd

    nc = bacc.Bacc("TRN2", target_bir_lowering=False, num_devices=1)
    arrays = {f"in_{k}": a for k, a in layouts({k: np.asarray(a) for k, a in inputs.items()}).items()}
    a = {k[3:]: nc.dram_tensor(k, x.shape, mybir.dt.from_np(x.dtype), kind="ExternalInput").ap() for k, x in arrays.items()}
    out = nc.dram_tensor("out", (B, T, D), F32, kind="ExternalOutput").ap()
    build_program(nc, a, out)
    r = run_bass_kernel_spmd(nc, [arrays], core_ids=[0])
    return r.results[0]["out"]
```

```python
from contextlib import ExitStack

import concourse.bass as bass
from concourse import mybir

F32 = mybir.dt.float32
F16 = mybir.dt.float16
BF16 = mybir.dt.bfloat16
I32 = mybir.dt.int32
U32 = mybir.dt.uint32
ALU = mybir.AluOpType
ACT = mybir.ActivationFunctionType
AX = mybir.AxisListType

B, T, D = 16, 165, 256
NP, TXT = 36, 128
R = (84, 81)
O = (0, 84)
H, HD = 16, 16
G = 4
NG = H // G
KD = D // 128
FF, RANK = 1024, 64
NE, EF = 8, 512
EPS = 1e-5
PB = 2
PK = 768 // 128
NTOK = B * T
NT = -(-NTOK // 128)
HALVES = ((0, 11), (11, NT))
BK = 128
GT = 7
NBK = (2 * NTOK + NE * (BK - 1)) // BK


def rows_of(t):
    return min(128, NTOK - 128 * t)


def wait(eng, sm, value):
    if not isinstance(value, int) or value > 0:
        eng.wait_ge(sm, value)


def first_rsqrt(nc, dve, link, y, yi, tmp, x):
    link(nc.vector.tensor_scalar(yi, x.bitcast(I32), 1, None, ALU.logical_shift_right))
    link(nc.vector.tensor_scalar(yi, yi, -1.0, float(0x5F3759DF), ALU.mult, ALU.add))
    for _ in range(3):
        link(nc.vector.scalar_tensor_tensor(out=tmp, in0=y, scalar=-0.5, in1=y, op0=ALU.mult, op1=ALU.mult))
        link(nc.vector.tensor_tensor(tmp, tmp, x, ALU.mult))
        link(nc.vector.scalar_tensor_tensor(out=y, in0=tmp, scalar=1.5, in1=y, op0=ALU.add, op1=ALU.mult))


class Chain:

    def __init__(self, eng, sem, per=0):
        self.eng, self.sem, self.per, self.k, self.turn = eng, sem, per, 0, 0

    def start(self, turn):
        assert not self.per or self.k in (0, self.per), self.k
        self.turn, self.k = turn, 0

    def count(self, ins):
        self.k += 1
        ins.then_inc(self.sem, 1)

    def __call__(self, ins):
        self.count(ins)
        self.hold()

    def hold(self):
        self.eng.wait_ge(self.sem, self.turn * self.per + self.k)


def build_program(nc, a, out):
    with ExitStack() as ctx:
        def sb(name, shape, dt=F32, to=ctx):
            return to.enter_context(nc.sbuf_tensor(name, shape, dt))

        numbers = set()

        def sem(name, to=ctx):
            s = to.enter_context(nc.semaphore(name))
            assert s.num not in numbers, "a semaphore that was used before doesn't start at 0"
            numbers.add(s.num)
            return s

        def ps(name, shape, dt=F32):
            return ctx.enter_context(nc.psum_tensor(name, shape, dt))

        ring = [ps("ring0", [128, 4, 256]), ps("ring1", [128, 4, 256])]
        ps_qk = ps("ps_qk", [128, 512])
        ps_v = ps("ps_v", [128, 512])
        ps_t = ps("ps_t", [128, 512])
        ps_o = ps("ps_o", [128, 512])
        two = (ps_qk, ps_v)

        h = sb("h", [128, 2 * B, D])
        bst = sb("bst", [128, 2 * B, 6])
        mean = sb("mean", [128, 2 * B])
        var = sb("var", [128, 2 * B])
        rs = sb("rs", [128, 2 * B])
        vtmp = sb("vtmp", [128, 2 * B])
        vtmp2 = sb("vtmp2", [128, 2 * B])
        ratio = sb("ratio", [128, 2 * B])
        ident = sb("ident", [128, 128])
        ident16 = sb("ident16", [128, 128], F16)
        identb = sb("identb", [128, 128], BF16)
        selh = sb("selh", [128, H, R[0]], BF16)
        mask_s = sb("mask_s", [R[0], 2, T], BF16)
        mask_t = sb("mask_t", [128, 2, T], BF16)
        w_qkv = [sb(f"w_qkv{l}", [128, KD, 3 * D]) for l in range(2)]
        b_qkv = [sb(f"b_qkv{l}", [R[0], 3 * D]) for l in range(2)]
        w_out = [sb(f"w_out{l}", [128, KD, D]) for l in range(2)]
        b_out = [sb(f"b_out{l}", [128, D], BF16) for l in range(2)]
        ones_b = sb("ones_b", [128, 128], BF16)
        tri = sb("tri", [128, 128], BF16)
        rh_w = sb("rh_w", [R[0], D])
        cos_t = [sb(f"cos_t{l}", [R[0], 2, HD]) for l in range(2)]
        sin_t = [sb(f"sin_t{l}", [R[0], 2, HD]) for l in range(2)]
        nrm_w = sb("nrm_w", [128, KD, 2])
        nrm_b = sb("nrm_b", [128, KD, 2])
        nrm_bb = sb("nrm_bb", [128, KD, 2, R[0]])
        ln_w = sb("ln_w", [R[0], HD])
        ln_b = sb("ln_b", [R[0], HD])
        rh_b = sb("rh_b", [R[0], 1])
        u1 = sb("u1", [128, KD, RANK])
        v1 = sb("v1", [RANK + 1, FF])
        u2 = sb("u2", [128, FF // 128, RANK])
        v2 = sb("v2", [RANK + 1, D])
        gate = sb("gate", [128, KD, NE])
        iota = sb("iota", [128, NE])
        valid = sb("valid", [128, NT])
        block_no = sb("block_no", [1, NBK])
        zeros = sb("zeros", [128, D])
        x_slots = nc.dram_tensor("x_slots", (NBK * BK, D), F32, kind="Internal").ap()
        y_slots = nc.dram_tensor("y_slots", (NBK * BK, D), F32, kind="Internal").ap()
        h_rows = nc.dram_tensor("h_rows", (NTOK, D), F32, kind="Internal").ap()

        loads = {n: sem(f"loaded_{n}") for n in ("embed", "txt", "consts", "attn0", "ffn0", "attn1", "moe")}
        moved = sem("moved")
        st_set = sem("st_set")
        zeros_set, slots_cleared = sem("zeros_set"), sem("slots_cleared")
        rows_sent, hm_loaded = [sem(f"rows_sent{g}") for g in range(2)], [sem(f"hm_loaded{g}") for g in range(2)]
        st_tile = ring[1]

        with ExitStack() as e:
            patches = sb("patches", [128, PK, B * NP], to=e)
            w_tok = sb("w_tok", [128, PK, D], to=e)
            pos2 = sb("pos2", [PB * NP, D], to=e)
            tokb = sb("tokb", [PB * NP, D], to=e)
            cls0 = sb("cls0", [1, D], to=e)
            pos0 = sb("pos0", [1, D], to=e)
            stage = sb("stage", [PB * NP, B // PB, D], to=e)
            emb_mm = sem("emb_mm", e)
            emb_out = sem("emb_out", e)
            emb_add = sem("emb_add", e)
            cls_done = sem("cls_done", e)
            stats_l = sem("stats_l", e)
            tri_f = sb("tri_f", [128, 128], to=e)
            selh_f = sb("selh_f", [128, H, R[0]], to=e)
            mask_sf = sb("mask_sf", [R[0], 2, T], to=e)
            mask_tf = sb("mask_tf", [128, 2, T], to=e)
            bias3 = [[sb(f"bias{l}{i}", [1, D], to=e) for i in range(2)] for l in range(2)]
            bias_p = [[sb(f"bias_p{l}{i}", [1, D], BF16, to=e) for i in range(3)] for l in range(2)]
            bias_s = sem("bias_s", e)
            bias_l = sem("bias_l", e)
            bias_z = sem("bias_z", e)
            bias_m = sem("bias_m", e)
            bias_mm = sem("bias_mm", e)
            bb_set = sem("bb_set", e)
            bias_done = sem("bias_done", e)
            with nc.Block() as block:

                @block.sync
                def _(sp):
                    L = loads["embed"]
                    sp.dma_start(patches[:, 0:3, :], a["patches"][:, 0:3, :]).then_inc(L, 16)
                    sp.dma_start(w_tok[:, :, :], a["w_tok"]).then_inc(L, 16)
                    sp.dma_start(patches[:, 3:6, :], a["patches"][:, 3:6, :]).then_inc(L, 16)
                    for i in range(PB):
                        sp.dma_start(pos2[NP * i:NP * i + NP, :], a["pos"][1:NP + 1, :]).then_inc(L, 16)
                    sp.dma_start(tokb[:, :], a["tok_b"].partition_broadcast(PB * NP)).then_inc(L, 16)
                    sp.dma_start(cls0[:, :], a["cls"]).then_inc(L, 16)
                    sp.dma_start(pos0[:, :], a["pos"][0:1, :]).then_inc(L, 16)
                    for l in range(2):
                        sp.dma_start(bias3[l][0][:, :], a[f"b_out{l}"]).then_inc(bias_s, 16)
                    L = loads["txt"]
                    n0 = R[0] - NP - 1
                    sp.dma_start(h[NP + 1:R[0], 0:2 * B:2, :], a["txt"][:, 0:n0, :].rearrange("b t d -> t b d")).then_inc(L, 16)
                    sp.dma_start(h[0:R[1], 1:2 * B:2, :], a["txt"][:, n0:TXT, :].rearrange("b t d -> t b d")).then_inc(L, 16)
                    for j in range(B // PB):
                        sp.wait_ge(emb_out, j + 1)
                        for i in range(PB):
                            sp.dma_start(h[1:NP + 1, 2 * (PB * j + i), :], stage[NP * i:NP * i + NP, j, :]).then_inc(moved, 16)
                    sp.wait_ge(bias_l, 10)
                    sp.wait_ge(bias_z, 2)
                    for l in range(2):
                        for i in range(3):
                            sp.dma_start(b_out[l][i:i + 1, :], bias_p[l][i][:, :]).then_inc(bias_m, 16)
                    sp.wait_ge(bias_m, 16 * 6)

                @block.scalar
                def _(act):
                    L = loads["attn0"]
                    act.dma_start(w_qkv[0][:, :, :], a["w_qkv0"]).then_inc(L, 16)
                    act.dma_start(b_qkv[0][:, :], a["b_qkv0"].partition_broadcast(R[0])).then_inc(L, 16)
                    act.dma_start(w_out[0][:, :, :], a["w_out0"]).then_inc(L, 16)
                    L = loads["consts"]
                    for t, n in ((ident, "ident"), (ident16, "ident16"), 
                                 (selh_f, "selh"), (tri_f, "tri"), (valid, "valid"), (block_no, "block_no"), (mask_sf, "mask_s"), (mask_tf, "mask_t"), (cos_t[0], "cos0"),
                                 (sin_t[0], "sin0"), (cos_t[1], "cos1"), (sin_t[1], "sin1")):
                        act.dma_start(t[:], a[n]).then_inc(L, 16)
                    act.dma_start(iota[:, :], a["iota"].partition_broadcast(128)).then_inc(L, 16)
                    L = loads["attn1"]
                    act.dma_start(w_qkv[1][:, :, :], a["w_qkv1"]).then_inc(L, 16)
                    act.dma_start(b_qkv[1][:, :], a["b_qkv1"].partition_broadcast(R[0])).then_inc(L, 16)
                    act.dma_start(w_out[1][:, :, :], a["w_out1"]).then_inc(L, 16)
                    act.dma_start(nrm_w[:, :, :], a["nrm_w"]).then_inc(L, 16)
                    act.dma_start(nrm_b[:, :, :], a["nrm_b"]).then_inc(L, 16)
                    act.dma_start(ln_w[:, :], a["ln_w"].partition_broadcast(R[0])).then_inc(L, 16)
                    act.dma_start(ln_b[:, :], a["ln_b"].partition_broadcast(R[0])).then_inc(L, 16)
                    act.dma_start(rh_b[:, :], a["rh_b"].partition_broadcast(R[0])).then_inc(L, 16)
                    act.dma_start(rh_w[:, :], a["rh_w"].partition_broadcast(R[0])).then_inc(L, 16)
                    L = loads["ffn0"]
                    act.dma_start(u1[:, :, :], a["u1"]).then_inc(L, 16)
                    act.dma_start(v1[:, :], a["v1"]).then_inc(L, 16)
                    act.dma_start(u2[:, :, :], a["u2"]).then_inc(L, 16)
                    act.dma_start(v2[:, :], a["v2"]).then_inc(L, 16)
                    act.dma_start(gate[:, :, :], a["gate"]).then_inc(L, 16)

                @block.tensor
                def _(pe):
                    pe.wait_ge(loads["embed"], 16 * 8)
                    for j in range(B // PB):
                        if j >= 2:
                            pe.wait_ge(emb_out, j - 1)
                        for k in range(PK):
                            mm = nc.tensor.matmul(ring[j % 2][0:PB * NP, 0, :],
                                                  patches[:, k, PB * NP * j:PB * NP * (j + 1)], w_tok[:, k, :],
                                                  start=(k == 0), stop=(k == PK - 1))
                        mm.then_inc(emb_mm, 1)
                    pe.wait_ge(bb_set, 4)
                    pe.wait_ge(loads["attn1"], 16 * 9)
                    for col, n, which in ((0, D, 0), (D, D, 1), (2 * D, D, 1)):
                        o = (ps_qk if col < 512 else ps_v)[0:R[0], col % 512:col % 512 + n]
                        for k in range(KD):
                            mm = nc.tensor.matmul(o, nrm_bb[:, k, which, :], w_qkv[1][:, k, col:col + n],
                                                  start=(k == 0), stop=(k == KD - 1))
                    mm.then_inc(bias_mm, 1)

                @block.vector
                def _(dve):
                    link = Chain(dve, stats_l)
                    nc.vector.memset(zeros[:, :], 0.0).then_inc(zeros_set, 1)
                    nc.vector.memset(bst[:, :, :], 1.0).then_inc(st_set, 1)
                    dve.wait_ge(loads["embed"], 16 * 8)
                    nc.vector.tensor_tensor(cls0[:, :], cls0[:, :], pos0[:, :], ALU.add).then_inc(emb_add, 1)
                    nc.vector.tensor_tensor(pos2[:, :], pos2[:, :], tokb[:, :], ALU.add).then_inc(emb_add, 1)
                    dve.wait_ge(emb_add, 2)
                    nc.vector.tensor_copy(h[0:1, 0:2 * B:2, :],
                                          cls0[:, :].unsqueeze(1).to_broadcast([1, B, D])).then_inc(cls_done, 1)
                    for j in range(B // PB):
                        dve.wait_ge(emb_mm, j + 1)
                        nc.vector.tensor_tensor(stage[:, j, :], ring[j % 2][0:PB * NP, 0, :], pos2[:, :],
                                                ALU.add).then_inc(emb_out, 1)
                    dve.wait_ge(loads["attn1"], 16 * 9)
                    for k in range(KD):
                        for w in range(2):
                            nc.vector.tensor_copy(nrm_bb[:, k, w, :], nrm_b[:, k, w:w + 1].to_broadcast([128, R[0]])).then_inc(bb_set, 1)
                    dve.wait_ge(loads["consts"], 16 * 13)
                    nc.vector.memset(ones_b[:, :], 1.0)
                    for l in range(2):
                        nc.vector.memset(b_out[l][:, :], 0.0).then_inc(bias_z, 1)
                    dve.wait_ge(bias_s, 32)
                    link = Chain(dve, bias_l)
                    for l in range(2):
                        x, rest = bias3[l]
                        link(nc.vector.tensor_copy(bias_p[l][0][:, :], x[:, :]))
                        link(nc.vector.tensor_tensor(rest[:, :], x[:, :], bias_p[l][0][:, :], ALU.subtract))
                        link(nc.vector.tensor_copy(bias_p[l][1][:, :], rest[:, :]))
                        link(nc.vector.tensor_tensor(x[:, :], rest[:, :], bias_p[l][1][:, :], ALU.subtract))
                        link(nc.vector.tensor_copy(bias_p[l][2][:, :], x[:, :]))
                    for t, x in ((identb, ident), (tri, tri_f), (selh, selh_f), (mask_s, mask_sf), (mask_t, mask_tf)):
                        nc.vector.tensor_copy(t[:], x[:])
                    dve.wait_ge(loads["txt"], 32)
                    dve.wait_ge(st_set, 1)
                    dve.wait_ge(cls_done, 1)
                    dve.wait_ge(moved, 16 * B)
                    for t in range(2 * B):
                        nc.vector.bn_stats(bst[0:R[t % 2], t, :], h[0:R[t % 2], t, :])
                    dve.wait_ge(bias_mm, 1)
                    nc.vector.tensor_tensor(b_qkv[1][:, 0:512], b_qkv[1][:, 0:512], ps_qk[0:R[0], :], ALU.add)
                    nc.vector.tensor_tensor(b_qkv[1][:, 512:768], b_qkv[1][:, 512:768], ps_v[0:R[0], 0:D], ALU.add)
                    for k in range(KD):
                        nc.vector.tensor_scalar(w_qkv[1][:, k, 0:D], w_qkv[1][:, k, 0:D], nrm_w[:, k, 0:1], None, ALU.mult)
                        nc.vector.tensor_scalar(w_qkv[1][:, k, D:3 * D], w_qkv[1][:, k, D:3 * D], nrm_w[:, k, 1:2], None, ALU.mult)

        def row_norms(dve, link, second=False, cols=slice(0, 2 * B)):
            link(nc.vector.tensor_tensor(mean[:, cols], bst[:, cols, 1], bst[:, cols, 4], ALU.add))
            link(nc.vector.tensor_tensor(vtmp[:, cols], bst[:, cols, 1], bst[:, cols, 4], ALU.subtract))
            link(nc.vector.tensor_tensor(vtmp[:, cols], vtmp[:, cols], vtmp[:, cols], ALU.mult))
            link(nc.vector.tensor_tensor(var[:, cols], bst[:, cols, 2], bst[:, cols, 5], ALU.add))
            link(nc.vector.tensor_scalar(vtmp[:, cols], vtmp[:, cols], 0.25, None, ALU.mult))
            link(nc.vector.scalar_tensor_tensor(out=var[:, cols], in0=var[:, cols], scalar=1.0 / D, in1=vtmp[:, cols], op0=ALU.mult, op1=ALU.add))
            link(nc.vector.tensor_scalar(mean[:, cols], mean[:, cols], 0.5, None, ALU.mult))
            link(nc.vector.tensor_scalar(vtmp[:, cols], var[:, cols], EPS, None, ALU.add))
            first_rsqrt(nc, dve, link, rs[:, cols], rs[:, cols].bitcast(I32), vtmp2[:, cols], vtmp[:, cols])
            if second:
                link(nc.vector.tensor_tensor(vtmp2[:, cols], rs[:, cols], rs[:, cols], ALU.mult))
                link(nc.vector.tensor_tensor(vtmp2[:, cols], vtmp2[:, cols], var[:, cols], ALU.mult))
                link(nc.vector.tensor_scalar(vtmp2[:, cols], vtmp2[:, cols], EPS, None, ALU.add))
                first_rsqrt(nc, dve, link, vtmp[:, cols], vtmp[:, cols].bitcast(I32), ratio[:, cols], vtmp2[:, cols])
                link(nc.vector.tensor_tensor(rs[:, cols], rs[:, cols], vtmp[:, cols], ALU.mult))
                link(nc.vector.tensor_tensor(ratio[:, cols], vtmp[:, cols], vtmp2[:, cols], ALU.mult))

        def row_stats(dve, b, resid_done):
            for c in range(2):
                dve.wait_ge(st_set, 1)
                dve.wait_ge(resid_done, b * 2 + c + 1)
                nc.vector.bn_stats(bst[0:R[c], bass.ds(b * 2 + c, 1), :].squeeze(1), h[0:R[c], bass.ds(b * 2 + c, 1), :].squeeze(1))

        def normed(b, c, xhat, done):
            r, t = R[c], 2 * b + c
            nc.vector.tensor_scalar(xhat[0:r, c, :], h[0:r, bass.ds(t, 1), :],
                                    mean[0:r, bass.ds(t, 1)], rs[0:r, bass.ds(t, 1)], ALU.subtract, ALU.mult).then_inc(done, 1)

        def attention(layer):
            causal = layer == 0
            with ExitStack() as e:
                def s_(name):
                    return sem(f"{name}_{layer}", e)

                def t_(name, shape, dt=F32):
                    return sb(f"{name}_{layer}", shape, dt, e)

                def two_of(name, shape, dt=F32):
                    return [t_(f"{name}{p}", shape, dt) for p in range(2)]

                xhat = t_("xhat", [R[0], 2, D])
                xT = two_of("xT", [128, KD, T])
                qk = t_("qk", [R[0], 2, 2 * H, HD])
                ru = t_("ru", [R[0], 2, 2 * H, HD])
                rw = t_("rw", [R[0], 2, 2 * H, HD])
                hl = t_("hl", [R[0], 2, 2 * H, 4, HD], F16)
                vaug = two_of("vaug", [R[0], 2, H, 32])
                kst = two_of("kst", [128, H // 2, 166], F16)
                qA = two_of("qA", [128, H // 2, 166], F16)
                qB = two_of("qB", [128, H // 2, 166], F16)
                mx = t_("mx", [R[0], 2, H])
                nm = t_("nm", [R[0], 2, H], BF16)
                nmT = two_of("nmT", [128, T], BF16)
                prob = [two_of(f"prob{g}", [R[0], G, T]) for g in range(2)]
                oT = two_of("oT", [128, NG, T])
                den = t_("den", [R[0], 2, H])
                y = t_("y", [R[0], 2, H, HD])
                yT = t_("yT", [128, KD, T])
                if layer == 1:
                    junk = t_("junk", [R[0], 2, D])
                    raw = two_of("raw", [R[0], 2])
                    per = two_of("per", [R[0], 2])
                    rad2 = t_("rad2", [R[0], 2])
                    hs1 = t_("hs1", [R[0], 2, 2 * H])
                    hs2 = t_("hs2", [R[0], 2, 2 * H])
                    hx = t_("hx", [R[0], 2, 2 * H])
                    hy = t_("hy", [R[0], 2, 2 * H])
                    hz = t_("hz", [R[0], 2, 2 * H])
                    hv = t_("hv", [R[0], 2, 2 * H])

                start_l = s_("start_l")
                chain_s = s_("chain") if layer == 1 else None
                set_ok, ones_ok = s_("buffers_set"), s_("ones_set")
                xhat_ready, xhatT_done, xT_ready = s_("xhat_ready"), s_("xhatT_done"), s_("xT_ready")
                qk_done, qk_read, v_done, v_read = s_("qk_done"), s_("qk_read"), s_("v_done"), s_("v_read")
                rope_parts, roped = s_("rope_parts"), s_("roped")
                if layer == 1:
                    raw_ready, per_ready = s_("raw_ready"), s_("per_ready")
                    summed, mean_ready, centred, squared = s_("summed"), s_("mean_ready"), s_("centred"), s_("squared")
                    scale_ready, scaled, weighted, shifted = s_("scale_ready"), s_("scaled"), s_("weighted"), s_("shifted")
                hi_ready, lo_ready, twice_ready = s_("hi_ready"), s_("lo_ready"), s_("twice_ready")
                kT_done, qT_done, k_ready, qa_ready, qb_ready = s_("kT_done"), s_("qT_done"), s_("k_ready"), s_("qa_ready"), s_("qb_ready")
                s_ready, max_done, nm_ready, nmT_done, nmT_ready = s_("s_ready"), s_("max_done"), s_("nm_ready"), s_("nmT_done"), s_("nmT_ready")
                st_ready, exp_done, pv_done, oT_ready = s_("st_ready"), s_("exp_done"), s_("pv_done"), s_("oT_ready")
                o_done, den_ready, y_ready, yT_done, yT_ready = s_("o_done"), s_("den_ready"), s_("y_ready"), s_("yT_done"), s_("yT_ready")
                proj_done, resid_done = s_("proj_done"), s_("resid_done")

                t16 = ps_t[:, :].bitcast(F16)
                v16 = ps_v[:, :].bitcast(F16)
                tb16 = ps_t[:, :].bitcast(BF16)
                s_tile, st_tile = ring

                def stacked(x, lo=0, hi=128, r=R[0]):
                    return x[lo:hi, 0:672].rearrange("p (h t) -> p h t", h=H // 2)[:, :, 0:r]

                def q_of(hd, p):
                    return (qA, qB)[hd % 2][p]

                def key_cols(c):
                    return R[0] if causal and c == 0 else T

                def first_q(c):
                    return O[c] if causal else 0

                def run(eng, turn):
                    for t in range(-3, 3):
                        turn(t, t % 2, lambda k, t=t: 0 <= t + k < B)
                    with eng.Fori(0, (B - 6) // 2) as i:
                        turn(i * 2 + 3, 1, lambda k: True)
                        turn(i * 2 + 4, 0, lambda k: True)
                    for t in range(B - 3, B + 1):
                        turn(t, t % 2, lambda k, t=t: 0 <= t + k < B)

                with nc.Block() as block:

                    @block.sync
                    def _(sp):
                        if causal:
                            sp.wait_ge(zeros_set, 1)
                            slots = x_slots.rearrange("(g j p) d -> g p j d", g=7, p=BK)
                            for g in range(7):
                                sp.dma_start(slots[g], zeros[:, :].unsqueeze(1).to_broadcast([128, NBK // 7, D])).then_inc(slots_cleared, 16)
                            return

                        def send(b, sent):
                            sp.wait_ge(resid_done, b * 2 + 2)
                            for c in range(2):
                                sp.dma_start(h_rows.rearrange("(b t) d -> t b d", t=T)[O[c]:O[c] + R[c], bass.ds(b, 1), :],
                                             h[0:R[c], bass.ds(b * 2 + c, 1), :]).then_inc(sent, 16)

                        done = -(-128 * HALVES[0][1] // T)
                        with sp.Fori(0, done) as i:
                            send(i, rows_sent[0])
                        sp.wait_ge(rows_sent[0], 16 * 2 * done)
                        t0, t1 = HALVES[0]
                        sp.dma_start(hm[:, t0:t1, :], h_rows[0:128 * t1, :].rearrange("(t p) d -> p t d", p=128)).then_inc(hm_loaded[0], 16)
                        with sp.Fori(done, B) as i:
                            send(i, rows_sent[1])
                        sp.wait_ge(rows_sent[1], 16 * 2 * (B - done))
                        sp.wait_ge(hm_set, 1)
                        t0, t1 = HALVES[1]
                        sp.dma_start(hm[:, t0:t1 - 1, :], h_rows[128 * t0:128 * (t1 - 1), :].rearrange("(t p) d -> p t d", p=128)).then_inc(hm_loaded[1], 16)
                        sp.dma_start(hm[0:rows_of(NT - 1), NT - 1, :], h_rows[128 * (NT - 1):NTOK, :]).then_inc(hm_loaded[1], 16)

                    @block.vector
                    def _(dve):
                        link = Chain(dve, start_l)
                        if layer == 1:
                            nc.vector.memset(hm[:, NT - 1, :], 0.0).then_inc(hm_set, 1)
                        for p in range(2):
                            nc.vector.memset(vaug[p][:, :, :, :], 0.0).then_inc(set_ok, 1)
                            nc.vector.memset(qA[p][64:128, :, :], 0.0).then_inc(set_ok, 1)
                            nc.vector.memset(qB[p][0:64, :, :], 0.0).then_inc(set_ok, 1)
                            nc.vector.memset(nmT[p][:, :], 0.0).then_inc(set_ok, 1)
                            if layer == 1:
                                nc.vector.memset(raw[p][:, :], 1.0).then_inc(set_ok, 1)
                                nc.vector.memset(per[p][:, :], 1.0).then_inc(set_ok, 1)
                        if layer == 1:
                            nc.vector.memset(hx[:, :, :], 1.0).then_inc(set_ok, 1)
                        dve.wait_ge(set_ok, 13 if layer == 1 else 8)
                        for p in range(2):
                            nc.vector.memset(vaug[p][:, :, :, HD:HD + 1], 1.0).then_inc(ones_ok, 1)
                            if causal:
                                nc.vector.tensor_copy(nmT[p][:, :], mask_t[:, p, :]).then_inc(ones_ok, 1)
                        row_norms(dve, link, second=layer == 1)
                        dve.wait_ge(loads["attn0"], 48)
                        dve.wait_ge(ones_ok, 4 if causal else 2)
                        if layer == 1:
                            dve.wait_ge(loads["attn1"], 16 * 9)
                        link = Chain(dve, chain_s, 19 if layer == 1 else 0)

                        def xhats(b, p):
                            wait(dve, xhatT_done, b * 1)
                            for c in range(2):
                                normed(b, c, xhat, xhat_ready)
                            if layer == 1:
                                wait(dve, raw_ready, b * 2)
                                for c in range(2):
                                    r = R[c]
                                    dve.wait_ge(xhat_ready, b * 2 + c + 1)
                                    nc.vector.tensor_tensor_reduce(out=junk[0:r, c, :], in0=xhat[0:r, c, :], in1=rh_w[0:r, :], scale=1.0, scalar=0.0,
                                                                   op0=ALU.mult, op1=ALU.add, accum_out=raw[p][0:r, c:c + 1]).then_inc(raw_ready, 1)
                                dve.wait_ge(raw_ready, b * 2 + 2)
                                nc.vector.tensor_tensor(per[p][:, :], raw[p][:, :], ratio[0:R[0], bass.ds(b * 2, 2)], ALU.mult).then_inc(per_ready, 1)

                        def qk_in(b, c):
                            r = R[c]
                            dve.wait_ge(qk_done, b * 2 + c + 1)
                            wait(dve, roped, b * 2)
                            nc.vector.tensor_tensor(qk[0:r, c, :, :].rearrange("r h d -> r (h d)"), ps_qk[0:r, :],
                                                    b_qkv[layer][0:r, 0:512], ALU.add).then_inc(qk_read, 1)

                        def v_in(b, p, c):
                            r = R[c]
                            dve.wait_ge(v_done, b * 2 + c + 1)
                            nc.vector.tensor_tensor(vaug[p][0:r, c, :, 0:HD], ps_v[0:r, 0:D].rearrange("r (h d) -> r h d", h=H),
                                                    b_qkv[layer][0:r, 512:768].rearrange("r (h d) -> r h d", h=H),
                                                    ALU.add).then_inc(v_read, 1)

                        def q_in(b, p, c):
                            r = R[c]
                            dve.wait_ge(qT_done, b * 2 + c + 1)
                            nc.vector.tensor_copy(qA[p][0:64, :, O[c]:O[c] + r], stacked(v16, 0, 64, r)).then_inc(qa_ready, 1)

                        def head_means(b):
                            for c in range(2):
                                r = R[c]
                                dve.wait_ge(roped, b * 2 + c + 1)
                                nc.vector.tensor_reduce(hs1[0:r, c, :], ru[0:r, c, :, :], AX.X, ALU.add).then_inc(summed, 1)
                            for c in range(2):
                                r = R[c]
                                dve.wait_ge(summed, b * 2 + c + 1)
                                nc.vector.tensor_scalar(hs2[0:r, c, :], hs1[0:r, c, :], -1.0 / HD, None, ALU.mult).then_inc(mean_ready, 1)

                        def head_scales(b, p):
                            link.start(b)
                            dve.wait_ge(per_ready, b * 1 + 1)
                            link(nc.vector.tensor_scalar(per[p][:, :], per[p][:, :], rh_b[:, 0:1], 0.01, ALU.add, ALU.mult))
                            link(nc.vector.tensor_scalar(per[p][:, :], per[p][:, :], 0.5, 2.0, ALU.max, ALU.min))
                            link(nc.vector.tensor_tensor(rad2[:, :], per[p][:, :], per[p][:, :], ALU.mult))
                            for c in range(2):
                                r = R[c]
                                dve.wait_ge(squared, b * 2 + c + 1)
                                link.count(nc.vector.tensor_reduce(hs1[0:r, c, :], rw[0:r, c, :, :], AX.X, ALU.add))
                            link.hold()
                            for c in range(2):
                                r = R[c]
                                link.count(nc.vector.tensor_scalar(hx[0:r, c, :], hs1[0:r, c, :], rad2[0:r, c:c + 1], 1.0 / HD, ALU.mult, ALU.mult))
                            link.hold()
                            link(nc.vector.tensor_scalar(hv[:, :, :], hx[:, :, :], EPS, None, ALU.add))
                            first_rsqrt(nc, dve, link, hy[:, :, :], hy[:, :, :].bitcast(I32), hz[:, :, :], hv[:, :, :])
                            for c in range(2):
                                r = R[c]
                                nc.vector.tensor_scalar(hz[0:r, c, :], hy[0:r, c, :], per[p][0:r, c:c + 1], None, ALU.mult).then_inc(scale_ready, 1)
                            for c in range(2):
                                r = R[c]
                                dve.wait_ge(scale_ready, b * 2 + c + 1)
                                nc.vector.tensor_tensor(ru[0:r, c, :, :], ru[0:r, c, :, :],
                                                        hz[0:r, c, :].unsqueeze(2).to_broadcast([r, 2 * H, HD]), ALU.mult).then_inc(scaled, 1)

                        def lows(b):
                            for c in range(2):
                                r = R[c]
                                dve.wait_ge(hi_ready, b * 2 + c + 1)
                                nc.vector.tensor_tensor(hl[0:r, c, :, 1, :], ru[0:r, c, :, :], hl[0:r, c, :, 0, :],
                                                        ALU.subtract).then_inc(lo_ready, 1)
                            for c in range(2):
                                r = R[c]
                                dve.wait_ge(lo_ready, b * 2 + c + 1)
                                nc.vector.tensor_copy(hl[0:r, c, 0:H, 2:4, :], hl[0:r, c, 0:H, 0:2, :]).then_inc(twice_ready, 1)
                                nc.vector.tensor_copy(hl[0:r, c, H:2 * H, 3:1:-1, :], hl[0:r, c, H:2 * H, 0:2, :]).then_inc(twice_ready, 1)

                        def maxes(b, n):
                            c, g = divmod(n, NG)
                            dve.wait_ge(s_ready, b * 8 + n + 1)
                            nc.vector.tensor_reduce(mx[0:R[c], c, G * g:G * g + G], s_tile[0:R[c], :, 0:key_cols(c)],
                                                    AX.X, ALU.max).then_inc(max_done, 1)

                        def max_rows(b):
                            dve.wait_ge(max_done, b * 8 + 8)
                            for c in range(2):
                                nc.vector.tensor_scalar(nm[0:R[c], c, :], mx[0:R[c], c, :], -1.0, None, ALU.mult).then_inc(nm_ready, 1)
                            dve.wait_ge(nmT_done, b * 1 + 1)
                            wait(dve, st_ready, b * 8)
                            for p in range(2 if causal else 1):
                                nc.vector.tensor_copy(nmT[p][0:H, :], tb16[0:H, 0:T]).then_inc(nmT_ready, 1)

                        def normalize(b, c):
                            r = R[c]
                            o = two[c][0:r, :].rearrange("r (h x) -> r h x", h=H)
                            dve.wait_ge(o_done, b * 2 + c + 1)
                            nc.vector.reciprocal(den[0:r, c, :], o[:, :, HD:HD + 1].squeeze(2)).then_inc(den_ready, 1)
                            dve.wait_ge(den_ready, b * 2 + c + 1)
                            nc.vector.tensor_tensor(y[0:r, c, :, :], o[:, :, 0:HD],
                                                    den[0:r, c, :].unsqueeze(2).to_broadcast([r, H, HD]), ALU.mult).then_inc(y_ready, 1)

                        def residual(b):
                            for c in range(2):
                                r, t = R[c], b * 2 + c
                                dve.wait_ge(proj_done, b * 2 + c + 1)
                                nc.vector.tensor_tensor(h[0:r, bass.ds(t, 1), :].squeeze(1), h[0:r, bass.ds(t, 1), :].squeeze(1),
                                                        two[c][0:r, 0:D], ALU.add).then_inc(resid_done, 1)

                        def turn(s, p, on):
                            if on(2):
                                qk_in(s + 2, 0)
                            if on(1):
                                q_in(s + 1, 1 - p, 0)
                            if on(2):
                                qk_in(s + 2, 1)
                            if on(1):
                                q_in(s + 1, 1 - p, 1)
                            for i in range(8):
                                if on(1):
                                    if i in (0, 1):
                                        v_in(s + 1, 1 - p, i)
                                    maxes(s + 1, i)
                                if on(-1) and i in (1, 2):
                                    normalize(s - 1, i - 1)
                                if on(2) and layer == 1 and i == 3:
                                    head_means(s + 2)
                                if on(-1) and i == 5:
                                    residual(s - 1)
                                if on(3) and i == 6:
                                    xhats(s + 3, 1 - p)
                            if on(-1) and causal:
                                row_stats(dve, s - 1, resid_done)
                            if on(1):
                                max_rows(s + 1)
                            if on(2):
                                if layer == 1:
                                    head_scales(s + 2, p)
                                lows(s + 2)

                        run(dve, turn)

                    @block.gpsimd
                    def _(pool):
                        pool.wait_ge(loads["consts"], 16 * 13)

                        def rope(b, c):
                            r = R[c]
                            cs = cos_t[layer][0:r, c, :].unsqueeze(1).to_broadcast([r, 2 * H, HD])
                            pool.wait_ge(qk_read, b * 2 + c + 1)
                            wait(pool, lo_ready, b * 2)
                            nc.gpsimd.tensor_tensor(ru[0:r, c, :, :], qk[0:r, c, :, :], cs, ALU.mult).then_inc(rope_parts, 1)
                            for half in range(2):
                                o = slice(8 * half, 8 * half + 8)
                                i = slice(8 - 8 * half, 16 - 8 * half)
                                sn = sin_t[layer][0:r, c, o].unsqueeze(1).to_broadcast([r, 2 * H, 8])
                                nc.gpsimd.tensor_tensor(rw[0:r, c, :, o], qk[0:r, c, :, i], sn, ALU.mult).then_inc(rope_parts, 1)
                            pool.wait_ge(rope_parts, b * 6 + 3 * c + 3)
                            nc.gpsimd.tensor_tensor(ru[0:r, c, :, :], ru[0:r, c, :, :], rw[0:r, c, :, :], ALU.add).then_inc(roped, 1)

                        def head_norms(b):
                            for c in range(2):
                                r = R[c]
                                pool.wait_ge(mean_ready, b * 2 + c + 1)
                                nc.gpsimd.tensor_tensor(ru[0:r, c, :, :], ru[0:r, c, :, :],
                                                        hs2[0:r, c, :].unsqueeze(2).to_broadcast([r, 2 * H, HD]), ALU.add).then_inc(centred, 1)
                            for c in range(2):
                                r = R[c]
                                pool.wait_ge(scaled, b * 2 + c + 1)
                                nc.gpsimd.tensor_tensor(ru[0:r, c, :, :], ru[0:r, c, :, :],
                                                        ln_w[0:r, :].unsqueeze(1).to_broadcast([r, 2 * H, HD]), ALU.mult).then_inc(weighted, 1)
                                pool.wait_ge(weighted, b * 2 + c + 1)
                                nc.gpsimd.tensor_tensor(ru[0:r, c, :, :], ru[0:r, c, :, :],
                                                        ln_b[0:r, :].unsqueeze(1).to_broadcast([r, 2 * H, HD]), ALU.add).then_inc(shifted, 1)

                        def turn(s, p, on):
                            if on(2):
                                for c in range(2):
                                    rope(s + 2, c)
                                if layer == 1:
                                    head_norms(s + 2)

                        run(pool, turn)

                    @block.scalar
                    def _(act):
                        act.wait_ge(set_ok, 13 if layer == 1 else 8)

                        def k_in(b, p, c):
                            r = R[c]
                            act.wait_ge(kT_done, b * 2 + c + 1)
                            nc.scalar.copy(kst[p][:, :, O[c]:O[c] + r], stacked(t16, r=r)).then_inc(k_ready, 1)
                            act.wait_ge(qT_done, b * 2 + c + 1)
                            nc.scalar.copy(qB[p][64:128, :, O[c]:O[c] + r], stacked(v16, 64, 128, r)).then_inc(qb_ready, 1)

                        def exps(b, m):
                            g, c = divmod(m, 2)
                            r, q0 = R[c], first_q(c)
                            act.wait_ge(st_ready, b * 8 + m + 1)
                            wait(act, pv_done, b * 4 + max(g - 1, 0))
                            nc.scalar.activation(prob[g % 2][c][0:r, :, q0:T], st_tile[0:r, :, q0:T], ACT.Exp,
                                                 scale=HD ** -0.5).then_inc(exp_done, 1)

                        def out_in(b, p, g):
                            act.wait_ge(pv_done, b * 4 + g + 1)
                            nc.scalar.copy(oT[p][:, g, :], ps_o[:, 0:T]).then_inc(oT_ready, 1)

                        def squares(b, c):
                            r = R[c]
                            act.wait_ge(centred, b * 2 + c + 1)
                            nc.scalar.activation(rw[0:r, c, :, :], ru[0:r, c, :, :], ACT.Square).then_inc(squared, 1)

                        def highs(b, c):
                            r = R[c]
                            if layer == 1:
                                act.wait_ge(shifted, b * 2 + c + 1)
                            else:
                                act.wait_ge(roped, b * 2 + c + 1)
                            wait(act, qT_done, b * 2)
                            nc.scalar.copy(hl[0:r, c, :, 0, :], ru[0:r, c, :, :]).then_inc(hi_ready, 1)

                        def turn_in(done, b, dst, ready):
                            act.wait_ge(done, b * 1 + 1)
                            nc.scalar.copy(dst[:, :, :], ps_t[:, 0:336].rearrange("p (k t) -> p k t", k=KD)[:, :, 0:T]).then_inc(ready, 1)

                        def turn(s, p, on):
                            if on(1):
                                for c in range(2):
                                    k_in(s + 1, 1 - p, c)
                            for i in range(8):
                                if on(0):
                                    exps(s, i)
                                    if i in (2, 4, 6):
                                        out_in(s, p, i // 2 - 1)
                                if on(-1) and i == 3:
                                    turn_in(yT_done, s - 1, yT, yT_ready)
                            if on(0):
                                out_in(s, p, NG - 1)
                            if on(2) and layer == 1:
                                for c in range(2):
                                    squares(s + 2, c)
                            if on(3):
                                turn_in(xhatT_done, s + 3, xT[1 - p], xT_ready)
                            if on(2):
                                for c in range(2):
                                    highs(s + 2, c)

                        run(act, turn)

                    @block.tensor
                    def _(pe):
                        pe.wait_ge(loads["consts"], 16 * 13)
                        pe.wait_ge(loads["attn0"], 48)
                        pe.wait_ge(set_ok, 13 if layer == 1 else 8)
                        pe.wait_ge(ones_ok, 4 if causal else 2)

                        def turned(src, done):
                            for c in range(2):
                                r = R[c]
                                for k in range(KD):
                                    mm = nc.tensor.transpose(ps_t[:, 168 * k + O[c]:168 * k + O[c] + r],
                                                             src[0:r, c, 128 * k:128 * k + 128], ident[0:r, 0:r])
                            mm.then_inc(done, 1)

                        def product(o, b, p, c, col, n, done):
                            r = R[c]
                            for k in range(KD):
                                mm = nc.tensor.matmul(o[0:r, 0:n], xT[p][:, k, O[c]:O[c] + r], w_qkv[layer][:, k, col:col + n],
                                                      start=(k == 0), stop=(k == KD - 1))
                            mm.then_inc(done, 1)

                        def q_and_k(b, p, c):
                            pe.wait_ge(xT_ready, b * 1 + 1)
                            wait(pe, qk_read, b * 2 + c)
                            if c == 0:
                                wait(pe, resid_done, b * 2 - 6)
                            product(ps_qk, b, p, c, 0, 512, qk_done)

                        def v(b, p, c):
                            wait(pe, qa_ready, b * 2 + 2)
                            wait(pe, qb_ready, b * 2 + 2)
                            wait(pe, v_read, b * 2 + c)
                            product(ps_v, b, p, c, 512, D, v_done)

                        def stacks(b, c):
                            r = R[c]
                            if c == 0:
                                wait(pe, nmT_ready, b * (2 if causal else 1))
                                wait(pe, resid_done, b * 2 - 4)
                                wait(pe, v_read, b * 2)
                            wait(pe, k_ready, b * 2 + c)
                            pe.wait_ge(twice_ready, b * 4 + 2 * c + 2)
                            for i in range(H // 2):
                                mm = nc.tensor.transpose(t16[:, 84 * i:84 * i + r], hl[0:r, c, H + 2 * i:H + 2 * i + 2, :, :].rearrange("r h s d -> r (h s d)"),
                                                         ident16[0:r, 0:r])
                            mm.then_inc(kT_done, 1)
                            wait(pe, qa_ready, b * 2 + c)
                            wait(pe, qb_ready, b * 2 + c)
                            for i in range(H // 2):
                                mm = nc.tensor.transpose(v16[:, 84 * i:84 * i + r], hl[0:r, c, 2 * i:2 * i + 2, :, :].rearrange("r h s d -> r (h s d)"),
                                                         ident16[0:r, 0:r])
                            mm.then_inc(qT_done, 1)

                        def scores(b, p, n):
                            c, g = divmod(n, NG)
                            r, nk = R[c], key_cols(c)
                            if n == 0:
                                pe.wait_ge(k_ready, b * 2 + 2)
                                pe.wait_ge(qa_ready, b * 2 + 2)
                                pe.wait_ge(qb_ready, b * 2 + 2)
                            wait(pe, max_done, b * 8 + n)
                            for j in range(G):
                                hd = G * g + j
                                mm = nc.tensor.matmul(s_tile[0:r, j, 0:nk], q_of(hd, p)[:, hd // 2, O[c]:O[c] + r],
                                                      kst[p][:, hd // 2, 0:nk], start=True, stop=not causal)
                                if causal:
                                    mm = nc.tensor.matmul(s_tile[0:r, j, O[c]:nk], identb[0:R[0], 0:r],
                                                          mask_s[0:R[0], c, O[c]:nk], start=False, stop=True)
                            mm.then_inc(s_ready, 1)

                        def scores_T(b, p, m):
                            g, c = divmod(m, 2)
                            r, q0 = R[c], first_q(c)
                            if m == 0:
                                pe.wait_ge(nmT_ready, b * (2 if causal else 1) + (2 if causal else 1))
                            wait(pe, exp_done, b * 8 + m)
                            for j in range(G):
                                hd = G * g + j
                                nc.tensor.matmul(st_tile[0:r, j, q0:T], kst[p][:, hd // 2, O[c]:O[c] + r], q_of(hd, p)[:, hd // 2, q0:T],
                                                 start=True, stop=False)
                                mm = nc.tensor.matmul(st_tile[0:r, j, q0:T], selh[:, hd, 0:r], nmT[c if causal else 0][:, q0:T], start=False, stop=True)
                            mm.then_inc(st_ready, 1)

                        def values(b, p, g):
                            pe.wait_ge(exp_done, b * 8 + 2 * g + 2)
                            if g == 0:
                                pe.wait_ge(v_read, b * 2 + 2)
                            wait(pe, oT_ready, b * 4 + g)
                            for c in range(2):
                                r, q0 = R[c], first_q(c)
                                for j in range(G):
                                    mm = nc.tensor.matmul(ps_o[32 * j:32 * j + 32, q0:T], vaug[p][0:r, c, G * g + j, :],
                                                          prob[g % 2][c][0:r, j, q0:T], start=(c == 0), stop=(c == 1))
                            mm.then_inc(pv_done, 1)

                        def outs_turned(b, p, c):
                            r = R[c]
                            pe.wait_ge(oT_ready, b * 4 + 4)
                            wait(pe, resid_done, b * 2)
                            for g in range(NG):
                                mm = nc.tensor.transpose(two[c][0:r, 128 * g:128 * g + 128], oT[p][:, g, O[c]:O[c] + r], ident[:, :])
                            mm.then_inc(o_done, 1)

                        def project(b, c):
                            r = R[c]
                            pe.wait_ge(yT_ready, b * 1 + 1)
                            for k in range(KD):
                                nc.tensor.matmul(two[c][0:r, 0:D], yT[:, k, O[c]:O[c] + r], w_out[layer][:, k, :],
                                                 start=(k == 0), stop=False)
                            nc.tensor.matmul(two[c][0:r, 0:D], ones_b[:, 0:r], b_out[layer][:, :], start=False, stop=True).then_inc(proj_done, 1)

                        def turn(s, p, on):
                            if on(2):
                                q_and_k(s + 2, p, 0)
                            if on(1):
                                stacks(s + 1, 0)
                            if on(2):
                                q_and_k(s + 2, p, 1)
                            if on(1):
                                stacks(s + 1, 1)
                            for i in range(8):
                                if on(0):
                                    scores_T(s, p, i)
                                if on(1):
                                    if i in (0, 1):
                                        v(s + 1, 1 - p, i)
                                    scores(s + 1, 1 - p, i)
                                if on(0) and i % 2 == 1:
                                    values(s, p, i // 2)
                                if on(-1) and i in (0, 1):
                                    if i == 0 and on(2):
                                        pe.wait_ge(qk_read, s * 2 + 6)
                                    if i == 1 and on(1):
                                        pe.wait_ge(v_read, s * 2 + 4)
                                    outs_turned(s - 1, 1 - p, i)
                                if on(-1) and i == 3:
                                    pe.wait_ge(y_ready, s * 2)
                                    if on(1):
                                        pe.wait_ge(k_ready, s * 2 + 4)
                                    turned(y_rows, yT_done)
                                if on(-1) and i == 4:
                                    for c in range(2):
                                        project(s - 1, c)
                            if on(3):
                                pe.wait_ge(xhat_ready, (s + 3) * 2 + 2)
                                if on(-1):
                                    pe.wait_ge(yT_ready, s * 1)
                                elif on(1):
                                    pe.wait_ge(k_ready, s * 2 + 4)
                                turned(xhat, xhatT_done)
                            if on(1):
                                pe.wait_ge(nm_ready, s * 2 + 4)
                                if on(3):
                                    pe.wait_ge(xT_ready, s + 4)
                                elif on(-1):
                                    pe.wait_ge(yT_ready, s * 1)
                                for c in range(2):
                                    mm = nc.tensor.transpose(tb16[0:H, O[c]:O[c] + R[c]], nm[0:R[c], c, :], identb[0:R[c], 0:R[c]])
                                mm.then_inc(nmT_done, 1)

                        y_rows = y[:, :, :, :].rearrange("r c h d -> r c (h d)")
                        run(pe, turn)

        def feed_forward():
            with ExitStack() as e:
                xhat = sb("xhat_f", [R[0], 2, D], to=e)
                xT = sb("xT_f", [128, KD, 168], to=e)
                pT = sb("pT_f", [RANK + 1, T], to=e)
                hT = [sb(f"hT_f{i}", [128, 4, T], to=e) for i in range(2)]
                qT = sb("qT_f", [RANK + 1, T], to=e)
                start_l, set_ok = sem("start_l_f", e), sem("set_ok_f", e)
                xhat_ready, xhatT_done, xT_ready = sem("xhat_ready_f", e), sem("xhatT_done_f", e), sem("xT_ready_f", e)
                p_done, p_ready, h_done, gelu_done = sem("p_done", e), sem("p_ready", e), sem("h_done", e), sem("gelu_done", e)
                q_done, q_ready, f_done, resid_done, stats_done = (sem("q_done", e), sem("q_ready_f", e), sem("f_done", e),
                                                                   sem("resid_done_f", e), sem("stats_done_f", e))
                with nc.Block() as block:

                    @block.vector
                    def _(dve):
                        nc.vector.memset(pT[RANK:RANK + 1, :], 1.0).then_inc(set_ok, 1)
                        nc.vector.memset(qT[RANK:RANK + 1, :], 1.0).then_inc(set_ok, 1)
                        row_norms(dve, Chain(dve, start_l))

                        def xhats(b):
                            dve.wait_ge(xhatT_done, b * 2)
                            for c in range(2):
                                normed(b, c, xhat, xhat_ready)

                        def finish(b):
                            for c in range(2):
                                r, t = R[c], b * 2 + c
                                dve.wait_ge(f_done, b * 2 + c + 1)
                                nc.vector.tensor_tensor(h[0:r, bass.ds(t, 1), :].squeeze(1), h[0:r, bass.ds(t, 1), :].squeeze(1),
                                                        (ps_v, ps_o)[c][0:r, 0:D], ALU.add).then_inc(resid_done, 1)
                            row_stats(dve, b, resid_done)

                        def turn(b, more):
                            if more:
                                xhats(b + 1)
                            dve.wait_ge(p_done, b * 1 + 1)
                            nc.vector.tensor_copy(pT[0:RANK, :], ps_qk[0:RANK, 0:T]).then_inc(p_ready, 1)
                            dve.wait_ge(q_done, b * 1 + 1)
                            nc.vector.tensor_copy(qT[0:RANK, :], ps_o[0:RANK, 0:T]).then_inc(q_ready, 1)
                            finish(b)

                        xhats(0)
                        with dve.Fori(0, B - 1) as i:
                            turn(i, True)
                        turn(B - 1, False)

                    @block.scalar
                    def _(act):
                        def turn(b):
                            act.wait_ge(xhatT_done, b * 2 + 2)
                            act.wait_ge(p_done, b * 1)
                            nc.scalar.copy(xT[:, :, 0:T], ps_t[:, 0:336].rearrange("p (k t) -> p k t", k=KD)[:, :, 0:T]).then_inc(xT_ready, 1)
                            for i in range(2):
                                act.wait_ge(h_done, b * 2 + i + 1)
                                act.wait_ge(q_done, b * 1)
                                nc.scalar.activation(hT[i][:, :, :], ring[i][:, :, 0:T], ACT.Gelu_apprx_tanh).then_inc(gelu_done, 1)

                        with act.Fori(0, B) as i:
                            turn(i)

                    @block.tensor
                    def _(pe):
                        pe.wait_ge(loads["ffn0"], 16 * 5)
                        pe.wait_ge(set_ok, 2)

                        def turn_x(b):
                            pe.wait_ge(xT_ready, b * 1)
                            for c in range(2):
                                r = R[c]
                                pe.wait_ge(xhat_ready, b * 2 + c + 1)
                                for k in range(KD):
                                    mm = nc.tensor.transpose(ps_t[:, 168 * k + O[c]:168 * k + O[c] + r], xhat[0:r, c, 128 * k:128 * k + 128],
                                                             ident[0:r, 0:r])
                                mm.then_inc(xhatT_done, 1)

                        def turn(b, more):
                            pe.wait_ge(xT_ready, b * 1 + 1)
                            for k in range(KD):
                                mm = nc.tensor.matmul(ps_qk[0:RANK, 0:T], u1[:, k, :], xT[:, k, 0:T], start=(k == 0), stop=(k == KD - 1))
                            mm.then_inc(p_done, 1)
                            pe.wait_ge(p_ready, b * 1 + 1)
                            for i in range(2):
                                pe.wait_ge(gelu_done, b * 2)
                                for j in range(4):
                                    n = 4 * i + j
                                    mm = nc.tensor.matmul(ring[i][:, j, 0:T], v1[:, 128 * n:128 * n + 128], pT[:, :], start=True, stop=True)
                                mm.then_inc(h_done, 1)
                            if more:
                                turn_x(b + 1)
                            pe.wait_ge(resid_done, b * 2)
                            for n in range(8):
                                pe.wait_ge(gelu_done, b * 2 + n // 4 + 1)
                                mm = nc.tensor.matmul(ps_o[0:RANK, 0:T], u2[:, n, :], hT[n // 4][:, n % 4, :], start=(n == 0), stop=(n == 7))
                            mm.then_inc(q_done, 1)
                            pe.wait_ge(q_ready, b * 1 + 1)
                            pe.wait_ge(resid_done, b * 2)
                            for c in range(2):
                                nc.tensor.matmul((ps_v, ps_o)[c][0:R[c], 0:D], qT[:, O[c]:O[c] + R[c]], v2[:, :],
                                                 start=True, stop=True).then_inc(f_done, 1)

                        turn_x(0)
                        with pe.Fori(0, B - 1) as i:
                            turn(i, True)
                        turn(B - 1, False)

        def route(slot, weight, block_expert, w1, w2):
            with ExitStack() as e:
                xr = sb("xhat_r", [128, NT, D], to=e)
                xT = [sb(f"xT_r{p}", [128, KD, 128], to=e) for p in range(2)]
                lg = sb("lg", [128, NT, NE], to=e)
                val = sb("val", [128, NT, NE], to=e)
                hot = [sb(f"hot{i}", [128, NT, NE], to=e) for i in range(2)]
                taken = sb("taken", [128, NT + 1, NE], BF16, to=e)
                best = [sb(f"best{i}", [128, NT], to=e) for i in range(2)]
                idx = sb("idx", [128, NT], to=e)
                ex = sb("ex", [128, NT], to=e)
                n_i = sb("n_i", [128, NE], I32, to=e)
                blocks = sb("blocks", [128, NE], to=e)
                first_block = sb("first_block", [128, NE + 1], to=e)
                before = sb("before", [1, NBK, NE], to=e)
                expert_f = sb("expert_f", [1, NBK], to=e)
                chain_s, norm_s, stats_done = sem("chain_r", e), sem("norm_r", e), sem("stats_done_r", e)
                xhat_ready, xhatT_done, xT_ready = sem("xhat_ready_r", e), sem("xhatT_done_r", e), sem("xT_ready_r", e)
                lg_done, diff_done, exp_done = sem("lg_done", e), sem("diff_done", e), sem("exp_done_r", e)
                taken_set, taken_ready, ranks_done = sem("taken_set", e), sem("taken_ready", e), sem("ranks_done", e)
                slots_ready, scattered = sem("slots_ready", e), sem("scattered", e)
                turned = (ps_t, ps_v)
                ranks = ps_qk[:, 0:(NT + 1) * NE].rearrange("p (t x) -> p t x", x=NE)
                with nc.Block() as block:

                    @block.sync
                    def _(sp):
                        for x in range(NE):
                            sp.dma_start(w1[:, x, :, :], a["w1"][:, x, :, :]).then_inc(loads["moe"], 16)
                            sp.dma_start(w2[:, x, :, :], a["w2"][:, x, :, :]).then_inc(loads["moe"], 16)

                    @block.vector
                    def _(dve):
                        link = Chain(dve, chain_s)
                        nc.vector.memset(taken[:, NT, :], 0.0).then_inc(taken_set, 1)
                        norms = Chain(dve, norm_s)
                        for g, (t0, t1) in enumerate(HALVES):
                            dve.wait_ge(hm_loaded[g], 16 * (g + 1))
                            with dve.Fori(t0, t1) as t:
                                nc.vector.bn_stats(bst[:, bass.ds(t, 1), :].squeeze(1), hm[:, bass.ds(t, 1), :].squeeze(1)).then_inc(stats_done, 1)
                            dve.wait_ge(stats_done, t1)
                            row_norms(dve, norms, cols=slice(t0, t1))
                            with dve.Fori(t0, t1) as t:
                                nc.vector.tensor_scalar(xr[:, bass.ds(t, 1), :], hm[:, bass.ds(t, 1), :],
                                                        mean[:, bass.ds(t, 1)], rs[:, bass.ds(t, 1)], ALU.subtract, ALU.mult).then_inc(xhat_ready, 1)
                        dve.wait_ge(lg_done, NT)
                        link(nc.vector.tensor_copy(lg[:, :, :], ps_o[:, 0:NT * NE].rearrange("p (t x) -> p t x", x=NE)))
                        full = [128, NT, NE]

                        def over(x):
                            return x[:, :].unsqueeze(2).to_broadcast(full)

                        io = iota[:, :].unsqueeze(1).to_broadcast(full)
                        for i in range(2):
                            link(nc.vector.tensor_reduce(best[i][:, :], lg[:, :, :], AX.X, ALU.max))
                            link(nc.vector.tensor_tensor(val[:, :, :], lg[:, :, :], over(best[i]), ALU.is_lt))
                            link(nc.vector.scalar_tensor_tensor(out=val[:, :, :], in0=val[:, :, :], scalar=float(NE), in1=io, op0=ALU.mult, op1=ALU.add))
                            link(nc.vector.tensor_reduce(idx[:, :], val[:, :, :], AX.X, ALU.min))
                            link(nc.vector.tensor_tensor(hot[i][:, :, :], io, over(idx), ALU.is_equal))
                            if i == 0:
                                link(nc.vector.scalar_tensor_tensor(out=lg[:, :, :], in0=hot[0][:, :, :], scalar=-3e38, in1=lg[:, :, :],
                                                                    op0=ALU.mult, op1=ALU.add))
                        nc.vector.tensor_tensor(ex[:, :], best[1][:, :], best[0][:, :], ALU.subtract).then_inc(diff_done, 1)
                        link(nc.vector.tensor_tensor(val[:, :, :], hot[0][:, :, :], hot[1][:, :, :], ALU.add))
                        dve.wait_ge(taken_set, 1)
                        nc.vector.tensor_tensor(taken[:, 0:NT, :], val[:, :, :], over(valid), ALU.mult).then_inc(taken_ready, 1)
                        dve.wait_ge(exp_done, 1)
                        link(nc.vector.tensor_scalar(weight[0][:, :], ex[:, :], 1.0, None, ALU.add))
                        link(nc.vector.reciprocal(weight[0][:, :], weight[0][:, :]))
                        link(nc.vector.tensor_tensor(weight[1][:, :], ex[:, :], weight[0][:, :], ALU.mult))
                        dve.wait_ge(ranks_done, 1)
                        link(nc.vector.tensor_scalar(n_i[:, :], ranks[:, NT, :], float(BK - 1), None, ALU.add))
                        link(nc.vector.tensor_scalar(n_i[:, :], n_i[:, :], BK.bit_length() - 1, None, ALU.logical_shift_right))
                        link(nc.vector.tensor_copy(blocks[:, :], n_i[:, :]))
                        link(nc.vector.memset(first_block[:, 0:1], 0.0))
                        for x in range(NE):
                            link(nc.vector.tensor_tensor(first_block[:, x + 1:x + 2], first_block[:, x:x + 1], blocks[:, x:x + 1], ALU.add))
                        link(nc.vector.scalar_tensor_tensor(out=val[:, :, :], in0=first_block[:, 0:NE].unsqueeze(1).to_broadcast(full), scalar=float(BK),
                                                            in1=ranks[:, 0:NT, :], op0=ALU.mult, op1=ALU.add))
                        for i in range(2):
                            link(nc.vector.tensor_tensor(hot[i][:, :, :], hot[i][:, :, :], val[:, :, :], ALU.mult))
                            link(nc.vector.tensor_reduce(idx[:, :], hot[i][:, :, :], AX.X, ALU.add))
                            nc.vector.tensor_copy(slot[i][:, :], idx[:, :]).then_inc(slots_ready, 1)
                            dve.wait_ge(slots_ready, i + 1)
                        link(nc.vector.tensor_tensor(before[:, :, :], first_block[0:1, 1:NE + 1].unsqueeze(1).to_broadcast([1, NBK, NE]),
                                                     block_no[:, :].unsqueeze(2).to_broadcast([1, NBK, NE]), ALU.is_le))
                        link(nc.vector.tensor_reduce(expert_f[:, :], before[:, :, :], AX.X, ALU.add))
                        link(nc.vector.tensor_scalar(expert_f[:, :], expert_f[:, :], float(NE - 1), None, ALU.min))
                        link(nc.vector.tensor_copy(block_expert[:, :], expert_f[:, :]))

                    @block.scalar
                    def _(act):
                        def turn(t, p):
                            wait(act, lg_done, t - 1)
                            act.wait_ge(xhatT_done, t + 1)
                            nc.scalar.copy(xT[p][:, :, :], turned[p][:, 0:KD * 128].rearrange("p (k t) -> p k t", k=KD)).then_inc(xT_ready, 1)

                        for t in range(3):
                            turn(t, t % 2)
                        with act.Fori(0, (NT - 3) // 2) as i:
                            turn(i * 2 + 3, 1)
                            turn(i * 2 + 4, 0)
                        act.wait_ge(diff_done, 1)
                        nc.scalar.activation(ex[:, :], ex[:, :], ACT.Exp).then_inc(exp_done, 1)

                    @block.tensor
                    def _(pe):
                        def transposes(t, p):
                            pe.wait_ge(xhat_ready, t + 1)
                            wait(pe, xT_ready, t - 1)
                            for k in range(KD):
                                mm = nc.tensor.transpose(turned[p][:, 128 * k:128 * k + 128],
                                                         xr[:, t, 128 * k:128 * k + 128], ident[:, :])
                            mm.then_inc(xhatT_done, 1)

                        def logits(t, p):
                            pe.wait_ge(xT_ready, t + 1)
                            for k in range(KD):
                                mm = nc.tensor.matmul(ps_o[:, NE * t:NE * t + NE], xT[p][:, k, :], gate[:, k, :],
                                                      start=(k == 0), stop=(k == KD - 1))
                            mm.then_inc(lg_done, 1)

                        transposes(0, 0)
                        for t in range(1, NT):
                            transposes(t, t % 2)
                            logits(t - 1, (t - 1) % 2)
                        logits(NT - 1, 0)
                        pe.wait_ge(taken_ready, 1)
                        nc.tensor.matmul(ranks[:, :, :], tri[:, :], taken[:, :, :], start=True, stop=False)
                        for t in range(NT):
                            mm = nc.tensor.matmul(ranks[:, t + 1:NT + 1, :], ones_b[:, :], taken[:, t, :].unsqueeze(1).to_broadcast([128, NT - t, NE]),
                                                  start=False, stop=(t == NT - 1))
                        mm.then_inc(ranks_done, 1)

                    @block.gpsimd
                    def _(pool):
                        pool.wait_ge(slots_cleared, 16 * 7)
                        for i in range(2):
                            pool.wait_ge(slots_ready, i + 1)
                            for t in range(NT):
                                r = rows_of(t)
                                pool.indirect_dma_start(x_slots, bass.IndirectOffsetOnAxis(ap=slot[i][0:r, t:t + 1], axis=0),
                                                        xr[0:r, t, :], None).then_inc(scattered, 16)
                        pool.wait_ge(scattered, 16 * 2 * NT)

        def experts(slot, weight, block_expert, w1, w2):
            with ExitStack() as e:
                def pair(name, shape):
                    return [sb(f"{name}{p}", shape, to=e) for p in range(2)]

                x_in, xT = pair("x_in", [128, D]), pair("xT_m", [128, KD, 128])
                hs, hT = pair("hs", [128, EF]), pair("hT_m", [128, EF // 128, 128])
                y_out = pair("y_out", [128, D])
                yg = (h, sb("yg", [128, NT, D], to=e))
                x_loaded, y_sent = [sem(f"x_loaded{p}", e) for p in range(2)], [sem(f"y_sent{p}", e) for p in range(2)]
                xT_done, xT_ready, h_done, silu_done = sem("xT_done_m", e), sem("xT_ready_m", e), sem("h_done_m", e), sem("silu_done", e)
                hT_done, hT_ready, y_done, y_ready = sem("hT_done_m", e), sem("hT_ready_m", e), sem("y_done", e), sem("y_ready_m", e)
                got = [sem(f"got{g}", e) for g in range(NT // GT)]
                added, out_sent = sem("added", e), sem("out_sent", e)
                x_blocks = x_slots.rearrange("(j p) d -> j p d", p=BK)
                y_blocks = y_slots.rearrange("(j p) d -> j p d", p=BK)
                out_rows = out.rearrange("b t d -> (b t) d")
                y_bank = (ps_o[:, 0:D], st_tile[:, 0, :])
                hT_bank = ring[0][:, 0:2, :].rearrange("p a c -> p (a c)")

                def run(eng, turn, lead):
                    for t in range(-lead, 3):
                        turn(t, t % 2, lambda k, t=t: (t + k) // 2, lambda k, t=t: 0 <= t + k < NBK)
                    n = (NBK - 6) // 2
                    with eng.Fori(0, n) as i:
                        turn(i * 2 + 3, 1, lambda k: i + (k + 3) // 2, lambda k: True)
                        turn(i * 2 + 4, 0, lambda k: i + (k + 4) // 2, lambda k: True)
                    for t in range(2 * n + 3, NBK + 1):
                        turn(t, t % 2, lambda k, t=t: (t + k) // 2, lambda k, t=t: 0 <= t + k < NBK)

                with nc.Block() as block:

                    @block.sync
                    def _(sp):
                        def turn(t, p, half, on):
                            if on(-1):
                                sp.wait_ge(y_ready, t * 1)
                                sp.dma_start(y_blocks[bass.ds(t - 1, 1), :, :].squeeze(0), y_out[1 - p][:, :]).then_inc(y_sent[1 - p], 16)
                            if on(3):
                                wait(sp, xT_done, t + 2)
                                sp.dma_start(x_in[1 - p][:, :], x_blocks[bass.ds(t + 3, 1), :, :].squeeze(0)).then_inc(x_loaded[1 - p], 16)

                        run(sp, turn, 3)
                        for t in range(NT):
                            sp.wait_ge(added, 2 * t + 2)
                            r = rows_of(t)
                            sp.dma_start(out_rows[128 * t:128 * t + r, :], hm[0:r, t, :]).then_inc(out_sent, 16)
                        sp.wait_ge(out_sent, 16 * NT)

                    @block.tensor
                    def _(pe):
                        pe.wait_ge(loads["moe"], 16 * 2 * NE)

                        def turn(t, p, half, on):
                            if on(1):
                                e1 = pe.value_load(block_expert[0:1, bass.ds(t + 1, 1)], min_val=0, max_val=NE - 1)
                            if on(0):
                                e2 = pe.value_load(block_expert[0:1, bass.ds(t, 1)], min_val=0, max_val=NE - 1)
                                pe.wait_ge(silu_done, t + 1)
                                wait(pe, hT_ready, t * 1)
                                for m in range(EF // 128):
                                    mm = nc.tensor.transpose(hT_bank[:, 128 * m:128 * m + 128], hs[p][:, 128 * m:128 * m + 128], ident[:, :])
                                mm.then_inc(hT_done, 1)
                            if on(2):
                                pe.wait_ge(x_loaded[p], half(2) * 16 + 16)
                                wait(pe, xT_ready, t + 2)
                                for k in range(KD):
                                    mm = nc.tensor.transpose(ps_t[:, 128 * k:128 * k + 128], x_in[p][:, 128 * k:128 * k + 128], ident[:, :])
                                mm.then_inc(xT_done, 1)
                            if on(1):
                                pe.wait_ge(xT_ready, t + 2)
                                wait(pe, silu_done, t * 1)
                                for k in range(KD):
                                    mm = nc.tensor.matmul(two[1 - p][:, :], xT[1 - p][:, k, :], w1[:, bass.ds(e1, 1), k, :].squeeze(1),
                                                          start=(k == 0), stop=(k == KD - 1))
                                mm.then_inc(h_done, 1)
                            if on(0):
                                pe.wait_ge(hT_ready, t + 1)
                                wait(pe, y_ready, t - 1)
                                for m in range(EF // 128):
                                    mm = nc.tensor.matmul(y_bank[p], hT[p][:, m, :], w2[:, bass.ds(e2, 1), m, :].squeeze(1),
                                                          start=(m == 0), stop=(m == EF // 128 - 1))
                                mm.then_inc(y_done, 1)

                        run(pe, turn, 2)

                    @block.scalar
                    def _(act):
                        def turn(t, p, half, on):
                            if on(2):
                                act.wait_ge(xT_done, t + 3)
                                wait(act, h_done, t + 1)
                                nc.scalar.copy(xT[p][:, :, :], ps_t[:, 0:KD * 128].rearrange("p (k t) -> p k t", k=KD)).then_inc(xT_ready, 1)
                            if on(1):
                                act.wait_ge(h_done, t + 2)
                                wait(act, hT_done, t * 1)
                                nc.scalar.activation(hs[1 - p][:, :], two[1 - p][:, :], ACT.Silu).then_inc(silu_done, 1)

                        run(act, turn, 2)

                    @block.vector
                    def _(dve):
                        def turn(t, p, half, on):
                            if on(0):
                                dve.wait_ge(hT_done, t + 1)
                                wait(dve, y_done, t - 1)
                                nc.vector.tensor_copy(hT[p][:, :, :], hT_bank.rearrange("p (m t) -> p m t", t=128)).then_inc(hT_ready, 1)
                                dve.wait_ge(y_done, t + 1)
                                wait(dve, y_sent[p], half(0) * 16)
                                nc.vector.tensor_copy(y_out[p][:, :], y_bank[p]).then_inc(y_ready, 1)

                        run(dve, turn, 0)
                        for t in range(NT):
                            r = rows_of(t)
                            dve.wait_ge(got[t // GT], 32 * GT)
                            for i in range(2):
                                nc.vector.scalar_tensor_tensor(out=hm[0:r, t, :], in0=yg[i][0:r, t, :], scalar=weight[i][0:r, t:t + 1],
                                                               in1=hm[0:r, t, :], op0=ALU.mult, op1=ALU.add).then_inc(added, 1)
                                dve.wait_ge(added, 2 * t + i + 1)

                    @block.gpsimd
                    def _(pool):
                        for p in range(2):
                            pool.wait_ge(y_sent[p], 16 * ((NBK + 1 - p) // 2))
                        for t in range(NT):
                            r = rows_of(t)
                            for i in range(2):
                                pool.indirect_dma_start(yg[i][0:r, t, :], None, y_slots,
                                                        bass.IndirectOffsetOnAxis(ap=slot[i][0:r, t:t + 1], axis=0)).then_inc(got[t // GT], 16)

        attention(0)
        feed_forward()
        hm = sb("hm", [128, NT, D])
        hm_set = sem("hm_set")
        attention(1)
        with ExitStack() as e:
            slot = [sb(f"slot{i}", [128, NT], I32, to=e) for i in range(2)]
            weight = [sb(f"weight{i}", [128, NT], to=e) for i in range(2)]
            block_expert = sb("block_expert", [1, NBK], I32, to=e)
            w1 = sb("w1", [128, NE, KD, EF], to=e)
            w2 = sb("w2", [128, NE, EF // 128, D], to=e)
            route(slot, weight, block_expert, w1, w2)
            experts(slot, weight, block_expert, w1, w2)


def layouts(v):
    import numpy as np

    f = np.float32
    c = np.ascontiguousarray
    x = v["x"].reshape(B, 3, 6, 16, 6, 16).transpose(1, 3, 5, 0, 2, 4).reshape(PK, 128, B * NP)

    def rows(w):
        return c(w.reshape(-1, 128, w.shape[-1]).transpose(1, 0, 2))

    def halves(w):
        return w.reshape(*w.shape[:-1], -1, 8, 2).swapaxes(-1, -2).reshape(w.shape)

    def chunks(t):
        o = np.zeros((R[0], 2, t.shape[1]), t.dtype)
        for k in range(2):
            o[0:R[k], k] = t[O[k]:O[k] + R[k]]
        return o

    q_w, kv_w = v["L1_attn_q_w"], v["L1_attn_kv_w"]
    q_b, kv_b = v["L1_attn_q_b"], v["L1_attn_kv_b"]
    pos = np.arange(T, dtype=f)
    scale0 = (f(2500) ** (f(2.0) * np.arange(8, dtype=f) / f(16))).astype(f)
    ang0 = pos[:, None] / scale0[None, :]
    mel = f(2595.0 * np.log10(1.0 + 4000.0 / 200.0))
    fb = f(200.0) * (np.power(f(10.0), np.linspace(0.0, mel, 8, dtype=f) / f(2595.0)).astype(f) - f(1.0)) / f(1000.0)
    ang1 = pos[:, None] * fb[None, :].astype(f)
    qi, ki = np.arange(T)[:, None], np.arange(T)[None, :]
    mask = np.where(ki <= qi, 0.0, -1e30).astype(f)
    selh = np.zeros((128, H, R[0]), f)
    for k in range(H):
        selh[k, k] = 1.0
        selh[32:32 + R[0], k] = np.eye(R[0])
    mask_t = np.zeros((128, 2, T), f)
    mask_t[32:32 + R[0]] = chunks(c(mask.T))
    s = {
        "patches": c(x.transpose(1, 0, 2)), "w_tok": rows(c(v["L0_tok_W"].T)), "tok_b": v["L0_tok_b"],
        "cls": v["L0_tok_cls_token"].reshape(1, D), "pos": v["L0_tok_pos_embedding"].reshape(NP + 1, D), "txt": v["txt"],
        "w_qkv0": rows(v["L0_attn_W_attn"]), "b_qkv0": v["L0_attn_b_attn"],
        "w_out0": rows(v["L0_attn_W_proj"]), "b_out0": v["L0_attn_b_proj"].reshape(1, D),
        "w_qkv1": rows(np.concatenate([halves(q_w), halves(kv_w[:, 0:D]), kv_w[:, D:]], axis=1)),
        "b_qkv1": np.concatenate([halves(q_b), halves(kv_b[0:D]), kv_b[D:]]),
        "w_out1": rows(v["L1_attn_out_w"]), "b_out1": v["L1_attn_out_b"].reshape(1, D),
        "rh_w": v["L1_attn_rh_w"].reshape(D),
        "nrm_w": c(np.stack([v["L1_attn_qn_w"], v["L1_attn_kvn_w"]]).reshape(2, KD, 128).transpose(2, 1, 0)),
        "nrm_b": c(np.stack([v["L1_attn_qn_b"], v["L1_attn_kvn_b"]]).reshape(2, KD, 128).transpose(2, 1, 0)),
        "ln_w": halves(v["L1_attn_ln_w"]), "ln_b": halves(v["L1_attn_ln_b"]), "rh_b": v["L1_attn_rh_b"],
        "u1": rows(v["L0_ffn_U1"]), "v1": np.concatenate([v["L0_ffn_V1"], v["L0_ffn_b1"][None]]),
        "u2": rows(v["L0_ffn_U2"]), "v2": np.concatenate([v["L0_ffn_V2"], v["L0_ffn_b2"][None]]),
        "gate": rows(v["L1_ffn_gate_w"]),
        "w1": c(v["L1_ffn_w1"].reshape(NE, KD, 128, EF).transpose(2, 0, 1, 3)),
        "w2": c(v["L1_ffn_w2"].reshape(NE, EF // 128, 128, D).transpose(2, 0, 1, 3)),
        "ident": np.eye(128, dtype=f), "ident16": np.eye(128, dtype=np.float16),
        "selh": selh, "mask_s": chunks(mask), "mask_t": mask_t,
        "iota": np.arange(NE, dtype=f), "block_no": np.arange(NBK, dtype=f).reshape(1, NBK),
        "tri": np.triu(np.ones((128, 128), f), 1),
        "valid": (np.arange(128)[:, None] + 128 * np.arange(NT)[None, :] < NTOK).astype(f),
    }
    for n, ang in enumerate((ang0, ang1)):
        co, si = np.cos(ang).astype(f), np.sin(ang).astype(f)
        s[f"cos{n}"] = chunks(np.concatenate([co, co], axis=1))
        s[f"sin{n}"] = chunks(np.concatenate([-si, si], axis=1))
    return {k: c(a) for k, a in s.items()}


def kernel(**inputs):
    import numpy as np
    import concourse.bacc as bacc
    from concourse.bass_utils import run_bass_kernel_spmd

    nc = bacc.Bacc("TRN2", target_bir_lowering=False, num_devices=1)
    arrays = {f"in_{k}": a for k, a in layouts({k: np.asarray(a) for k, a in inputs.items()}).items()}
    a = {k[3:]: nc.dram_tensor(k, x.shape, mybir.dt.from_np(x.dtype), kind="ExternalInput").ap() for k, x in arrays.items()}
    out = nc.dram_tensor("out", (B, T, D), F32, kind="ExternalOutput").ap()
    build_program(nc, a, out)
    r = run_bass_kernel_spmd(nc, [arrays], core_ids=[0])
    return r.results[0]["out"]
```

```python
from contextlib import ExitStack

import concourse.bass as bass
from concourse import mybir

F32 = mybir.dt.float32
F16 = mybir.dt.float16
BF16 = mybir.dt.bfloat16
I32 = mybir.dt.int32
ALU = mybir.AluOpType
ACT = mybir.ActivationFunctionType
AX = mybir.AxisListType

B, T, D = 16, 165, 256
NP, TXT = 36, 128
R = (84, 81)
O = (0, 84)
H, HD = 16, 16
G = 4
NG = H // G
KD = D // 128
FF, RANK = 1024, 64
NE, EF = 8, 512
EPS = 1e-5
PB = 2
PK = 768 // 128
NTOK = B * T
NT = -(-NTOK // 128)
HALVES = ((0, 11), (11, NT))
BK = 128
NBK = (2 * NTOK + NE * (BK - 1)) // BK


def rows_of(t):
    return min(128, NTOK - 128 * t)


def wait(eng, sm, value):
    if not isinstance(value, int) or value > 0:
        eng.wait_ge(sm, value)


def rsqrt_guess(nc, link, yi, x):
    link(nc.vector.tensor_scalar(yi, x.bitcast(I32), 1, None, ALU.logical_shift_right))
    link(nc.vector.tensor_scalar(yi, yi, -1.0, float(0x5F3759DF), ALU.mult, ALU.add))


def rsqrt_step(nc, link, y, tmp, x):
    link(nc.vector.scalar_tensor_tensor(out=tmp, in0=y, scalar=-0.5, in1=y, op0=ALU.mult, op1=ALU.mult))
    link(nc.vector.tensor_tensor(tmp, tmp, x, ALU.mult))
    link(nc.vector.scalar_tensor_tensor(out=y, in0=tmp, scalar=1.5, in1=y, op0=ALU.add, op1=ALU.mult))


def rsqrt(nc, link, y, yi, tmp, x):
    rsqrt_guess(nc, link, yi, x)
    for _ in range(3):
        rsqrt_step(nc, link, y, tmp, x)


class Chain:

    def __init__(self, eng, sem, per=0):
        self.eng, self.sem, self.per, self.k, self.turn = eng, sem, per, 0, 0

    def start(self, turn):
        assert not self.per or self.k in (0, self.per), self.k
        self.turn, self.k = turn, 0

    def count(self, ins):
        self.k += 1
        ins.then_inc(self.sem, 1)

    def __call__(self, ins):
        self.count(ins)
        self.hold()

    def hold(self):
        self.eng.wait_ge(self.sem, self.turn * self.per + self.k)


def build_program(nc, a, out):
    with ExitStack() as ctx:
        def sb(name, shape, dt=F32, to=ctx):
            return to.enter_context(nc.sbuf_tensor(name, shape, dt))

        numbers = set()

        def sem(name, to=ctx):
            s = to.enter_context(nc.semaphore(name))
            assert s.num not in numbers, "a semaphore that was used before doesn't start at 0"
            numbers.add(s.num)
            return s

        def ps(name, shape, dt=F32):
            return ctx.enter_context(nc.psum_tensor(name, shape, dt))

        ring = [ps("ring0", [128, 4, 256]), ps("ring1", [128, 4, 256])]
        ps_qk = ps("ps_qk", [128, 512])
        ps_v = ps("ps_v", [128, 512])
        ps_t = ps("ps_t", [128, 512])
        ps_o = ps("ps_o", [128, 512])
        two = (ps_qk, ps_v)

        h = sb("h", [128, 2 * B, D])
        bst = sb("bst", [128, 2 * B, 6])
        mean = sb("mean", [128, 2 * B])
        var = sb("var", [128, 2 * B])
        rs = sb("rs", [128, 2 * B])
        vtmp = sb("vtmp", [128, 2 * B])
        vtmp2 = sb("vtmp2", [128, 2 * B])
        ratio = sb("ratio", [128, 2 * B])
        ident = sb("ident", [128, 128])
        ident16 = sb("ident16", [128, 128], F16)
        identb = sb("identb", [128, 128], BF16)
        selh = sb("selh", [128, H, R[0]], BF16)
        mask_s = sb("mask_s", [R[0], 2, T], BF16)
        mask_t = sb("mask_t", [128, 2, T], BF16)
        w_qkv = [sb(f"w_qkv{l}", [128, KD, 3 * D + l]) for l in range(2)]
        b_qkv = [sb(f"b_qkv{l}", [R[0], 3 * D]) for l in range(2)]
        w_out = [sb(f"w_out{l}", [128, KD, D]) for l in range(2)]
        b_out = [sb(f"b_out{l}", [128, D], BF16) for l in range(2)]
        ones_b = sb("ones_b", [128, 128], BF16)
        tri = sb("tri", [128, 128], BF16)
        cos_t = [sb(f"cos_t{l}", [R[0], 2, HD]) for l in range(2)]
        sin_t = [sb(f"sin_t{l}", [R[0], 2, HD]) for l in range(2)]
        nrm_w = sb("nrm_w", [128, KD, 2])
        nrm_b = sb("nrm_b", [128, KD, 2])
        nrm_bb = sb("nrm_bb", [128, KD, 2, R[0]])
        ln_w = sb("ln_w", [R[0], HD])
        ln_b = sb("ln_b", [R[0], HD])
        rh_b = sb("rh_b", [R[0], 1])
        u1 = sb("u1", [128, KD, RANK])
        v1 = sb("v1", [RANK + 1, FF])
        u2 = sb("u2", [128, FF // 128, RANK])
        v2 = sb("v2", [RANK + 1, D])
        gate = sb("gate", [128, KD, NE])
        iota = sb("iota", [128, NE])
        valid = sb("valid", [128, NT])
        block_no = sb("block_no", [128, NBK])
        lane_no = sb("lane_no", [128, BK])
        token_1 = sb("token_1", [128, NT])
        spare_1 = sb("spare_1", [128, 1])
        zeros = sb("zeros", [128, D])
        x_rows = nc.dram_tensor("x_rows", (NTOK, D), F32, kind="Internal").ap()
        h_rows = nc.dram_tensor("h_rows", (NTOK + BK, D), F32, kind="Internal").ap()

        loads = {n: sem(f"loaded_{n}") for n in ("embed", "txt", "consts", "attn0", "ffn0", "attn1", "moe")}
        moved = sem("moved")
        st_set = sem("st_set")
        zeros_set, spare_cleared = sem("zeros_set"), sem("spare_cleared")
        rows_sent, hm_loaded = [sem(f"rows_sent{g}") for g in range(2)], [sem(f"hm_loaded{g}") for g in range(2)]
        st_tile = ring[1]

        with ExitStack() as e:
            patches = sb("patches", [128, PK, B * NP], to=e)
            w_tok = sb("w_tok", [128, PK, D], to=e)
            pos2 = sb("pos2", [PB * NP, D], to=e)
            tokb = sb("tokb", [PB * NP, D], to=e)
            cls0 = sb("cls0", [1, D], to=e)
            pos0 = sb("pos0", [1, D], to=e)
            stage = sb("stage", [PB * NP, B // PB, D], to=e)
            emb_mm = sem("emb_mm", e)
            emb_out = sem("emb_out", e)
            emb_add = sem("emb_add", e)
            cls_done = sem("cls_done", e)
            tri_f = sb("tri_f", [128, 128], to=e)
            selh_f = sb("selh_f", [128, H, R[0]], to=e)
            mask_sf = sb("mask_sf", [R[0], 2, T], to=e)
            mask_tf = sb("mask_tf", [128, 2, T], to=e)
            bias3 = [[sb(f"bias{l}{i}", [1, D], to=e) for i in range(2)] for l in range(2)]
            bias_p = [[sb(f"bias_p{l}{i}", [1, D], BF16, to=e) for i in range(3)] for l in range(2)]
            bias_s = sem("bias_s", e)
            bias_l = sem("bias_l", e)
            bias_z = sem("bias_z", e)
            bias_m = sem("bias_m", e)
            bias_mm = sem("bias_mm", e)
            bb_set = sem("bb_set", e)
            bias_done = sem("bias_done", e)
            with nc.Block() as block:

                @block.sync
                def _(sp):
                    L = loads["embed"]
                    sp.dma_start(patches[:, 0:3, :], a["patches"][:, 0:3, :]).then_inc(L, 16)
                    sp.dma_start(w_tok[:, :, :], a["w_tok"]).then_inc(L, 16)
                    sp.dma_start(patches[:, 3:6, :], a["patches"][:, 3:6, :]).then_inc(L, 16)
                    for i in range(PB):
                        sp.dma_start(pos2[NP * i:NP * i + NP, :], a["pos"][1:NP + 1, :]).then_inc(L, 16)
                    sp.dma_start(tokb[:, :], a["tok_b"].partition_broadcast(PB * NP)).then_inc(L, 16)
                    sp.dma_start(cls0[:, :], a["cls"]).then_inc(L, 16)
                    sp.dma_start(pos0[:, :], a["pos"][0:1, :]).then_inc(L, 16)
                    for l in range(2):
                        sp.dma_start(bias3[l][0][:, :], a[f"b_out{l}"]).then_inc(bias_s, 16)
                    L = loads["txt"]
                    n0 = R[0] - NP - 1
                    sp.dma_start(h[NP + 1:R[0], 0:2 * B:2, :], a["txt"][:, 0:n0, :].rearrange("b t d -> t b d")).then_inc(L, 16)
                    sp.dma_start(h[0:R[1], 1:2 * B:2, :], a["txt"][:, n0:TXT, :].rearrange("b t d -> t b d")).then_inc(L, 16)
                    for j in range(B // PB):
                        sp.wait_ge(emb_out, j + 1)
                        for i in range(PB):
                            sp.dma_start(h[1:NP + 1, 2 * (PB * j + i), :], stage[NP * i:NP * i + NP, j, :]).then_inc(moved, 16)
                    sp.wait_ge(bias_l, 10)
                    sp.wait_ge(bias_z, 2)
                    for l in range(2):
                        for i in range(3):
                            sp.dma_start(b_out[l][i:i + 1, :], bias_p[l][i][:, :]).then_inc(bias_m, 16)
                    sp.wait_ge(bias_m, 16 * 6)

                @block.scalar
                def _(act):
                    L = loads["attn0"]
                    act.dma_start(w_qkv[0][:, :, :], a["w_qkv0"]).then_inc(L, 16)
                    act.dma_start(b_qkv[0][:, :], a["b_qkv0"].partition_broadcast(R[0])).then_inc(L, 16)
                    act.dma_start(w_out[0][:, :, :], a["w_out0"]).then_inc(L, 16)
                    L = loads["consts"]
                    for t, n in ((ident, "ident"), (ident16, "ident16"), 
                                 (selh_f, "selh"), (tri_f, "tri"), (valid, "valid"), (token_1, "token_1"), (spare_1, "spare_1"), (mask_sf, "mask_s"), (mask_tf, "mask_t"), (cos_t[0], "cos0"),
                                 (sin_t[0], "sin0"), (cos_t[1], "cos1"), (sin_t[1], "sin1")):
                        act.dma_start(t[:], a[n]).then_inc(L, 16)
                    for t, n in ((iota, "iota"), (block_no, "block_no"), (lane_no, "lane_no")):
                        act.dma_start(t[:, :], a[n].partition_broadcast(128)).then_inc(L, 16)
                    L = loads["attn1"]
                    act.dma_start(w_qkv[1][:, :, :], a["w_qkv1"]).then_inc(L, 16)
                    act.dma_start(b_qkv[1][:, :], a["b_qkv1"].partition_broadcast(R[0])).then_inc(L, 16)
                    act.dma_start(w_out[1][:, :, :], a["w_out1"]).then_inc(L, 16)
                    act.dma_start(nrm_w[:, :, :], a["nrm_w"]).then_inc(L, 16)
                    act.dma_start(nrm_b[:, :, :], a["nrm_b"]).then_inc(L, 16)
                    act.dma_start(ln_w[:, :], a["ln_w"].partition_broadcast(R[0])).then_inc(L, 16)
                    act.dma_start(ln_b[:, :], a["ln_b"].partition_broadcast(R[0])).then_inc(L, 16)
                    act.dma_start(rh_b[:, :], a["rh_b"].partition_broadcast(R[0])).then_inc(L, 16)
                    L = loads["ffn0"]
                    act.dma_start(u1[:, :, :], a["u1"]).then_inc(L, 16)
                    act.dma_start(v1[:, :], a["v1"]).then_inc(L, 16)
                    act.dma_start(u2[:, :, :], a["u2"]).then_inc(L, 16)
                    act.dma_start(v2[:, :], a["v2"]).then_inc(L, 16)
                    act.dma_start(gate[:, :, :], a["gate"]).then_inc(L, 16)
                    act.wait_ge(loads["consts"], 16 * 16)
                    for t, x in ((identb, ident), (tri, tri_f), (selh, selh_f), (mask_s, mask_sf), (mask_t, mask_tf)):
                        nc.scalar.copy(t[:], x[:])

                @block.tensor
                def _(pe):
                    pe.wait_ge(loads["embed"], 16 * 8)
                    for j in range(B // PB):
                        if j >= 2:
                            pe.wait_ge(emb_out, j - 1)
                        for k in range(PK):
                            mm = nc.tensor.matmul(ring[j % 2][0:PB * NP, 0, :],
                                                  patches[:, k, PB * NP * j:PB * NP * (j + 1)], w_tok[:, k, :],
                                                  start=(k == 0), stop=(k == PK - 1))
                        mm.then_inc(emb_mm, 1)
                    pe.wait_ge(bb_set, 4)
                    pe.wait_ge(loads["attn1"], 16 * 8)
                    for col, n, which in ((0, D, 0), (D, D, 1), (2 * D, D, 1)):
                        o = (ps_qk if col < 512 else ps_v)[0:R[0], col % 512:col % 512 + n]
                        for k in range(KD):
                            mm = nc.tensor.matmul(o, nrm_bb[:, k, which, :], w_qkv[1][:, k, col:col + n],
                                                  start=(k == 0), stop=(k == KD - 1))
                    mm.then_inc(bias_mm, 1)

                @block.vector
                def _(dve):
                    nc.vector.memset(zeros[:, :], 0.0).then_inc(zeros_set, 1)
                    nc.vector.memset(bst[:, :, :], 1.0).then_inc(st_set, 1)
                    dve.wait_ge(loads["embed"], 16 * 8)
                    nc.vector.tensor_tensor(cls0[:, :], cls0[:, :], pos0[:, :], ALU.add).then_inc(emb_add, 1)
                    nc.vector.tensor_tensor(pos2[:, :], pos2[:, :], tokb[:, :], ALU.add).then_inc(emb_add, 1)
                    dve.wait_ge(emb_add, 2)
                    nc.vector.tensor_copy(h[0:1, 0:2 * B:2, :],
                                          cls0[:, :].unsqueeze(1).to_broadcast([1, B, D])).then_inc(cls_done, 1)
                    dve.wait_ge(loads["txt"], 32)
                    dve.wait_ge(st_set, 1)
                    for j in range(B // PB):
                        for t in range(2 * PB * j + 1, 2 * PB * (j + 1), 2):
                            nc.vector.bn_stats(bst[0:R[1], t, :], h[0:R[1], t, :])
                        dve.wait_ge(emb_mm, j + 1)
                        nc.vector.tensor_tensor(stage[:, j, :], ring[j % 2][0:PB * NP, 0, :], pos2[:, :],
                                                ALU.add).then_inc(emb_out, 1)
                    dve.wait_ge(cls_done, 1)
                    dve.wait_ge(moved, 16 * B)
                    for t in range(0, 2 * B, 2):
                        nc.vector.bn_stats(bst[0:R[0], t, :], h[0:R[0], t, :])
                    dve.wait_ge(loads["attn1"], 16 * 8)
                    dve.wait_ge(bias_mm, 1)
                    nc.vector.tensor_tensor(b_qkv[1][:, 0:512], b_qkv[1][:, 0:512], ps_qk[0:R[0], :], ALU.add)
                    nc.vector.tensor_tensor(b_qkv[1][:, 512:768], b_qkv[1][:, 512:768], ps_v[0:R[0], 0:D], ALU.add)

                @block.gpsimd
                def _(pool):
                    nc.gpsimd.memset(ones_b[:, :], 1.0)
                    for l in range(2):
                        nc.gpsimd.memset(b_out[l][:, :], 0.0).then_inc(bias_z, 1)
                    pool.wait_ge(bias_s, 32)
                    link = Chain(pool, bias_l)
                    for l in range(2):
                        x, rest = bias3[l]
                        link(nc.gpsimd.tensor_copy(bias_p[l][0][:, :], x[:, :]))
                        link(nc.gpsimd.tensor_tensor(rest[:, :], x[:, :], bias_p[l][0][:, :], ALU.subtract))
                        link(nc.gpsimd.tensor_copy(bias_p[l][1][:, :], rest[:, :]))
                        link(nc.gpsimd.tensor_tensor(x[:, :], rest[:, :], bias_p[l][1][:, :], ALU.subtract))
                        link(nc.gpsimd.tensor_copy(bias_p[l][2][:, :], x[:, :]))
                    pool.wait_ge(loads["attn1"], 16 * 8)
                    for k in range(KD):
                        for w in range(2):
                            nc.gpsimd.tensor_copy(nrm_bb[:, k, w, :], nrm_b[:, k, w:w + 1].to_broadcast([128, R[0]])).then_inc(bb_set, 1)
                    pool.wait_ge(bias_mm, 1)
                    for k in range(KD):
                        nc.gpsimd.tensor_scalar(w_qkv[1][:, k, 0:D], w_qkv[1][:, k, 0:D], nrm_w[:, k, 0:1], None, ALU.mult)
                        nc.gpsimd.tensor_scalar(w_qkv[1][:, k, D:3 * D], w_qkv[1][:, k, D:3 * D], nrm_w[:, k, 1:2], None, ALU.mult)

        def row_norms(dve, link, second=False, cols=slice(0, 2 * B)):
            link(nc.vector.tensor_tensor(mean[:, cols], bst[:, cols, 1], bst[:, cols, 4], ALU.add))
            link(nc.vector.tensor_tensor(vtmp[:, cols], bst[:, cols, 1], bst[:, cols, 4], ALU.subtract))
            link(nc.vector.tensor_tensor(vtmp[:, cols], vtmp[:, cols], vtmp[:, cols], ALU.mult))
            link(nc.vector.tensor_tensor(var[:, cols], bst[:, cols, 2], bst[:, cols, 5], ALU.add))
            link(nc.vector.tensor_scalar(vtmp[:, cols], vtmp[:, cols], 0.25, None, ALU.mult))
            link(nc.vector.scalar_tensor_tensor(out=var[:, cols], in0=var[:, cols], scalar=1.0 / D, in1=vtmp[:, cols], op0=ALU.mult, op1=ALU.add))
            link(nc.vector.tensor_scalar(mean[:, cols], mean[:, cols], 0.5, None, ALU.mult))
            link(nc.vector.tensor_scalar(vtmp[:, cols], var[:, cols], EPS, None, ALU.add))
            rsqrt(nc, link, rs[:, cols], rs[:, cols].bitcast(I32), vtmp2[:, cols], vtmp[:, cols])
            if second:
                link(nc.vector.tensor_tensor(vtmp2[:, cols], rs[:, cols], rs[:, cols], ALU.mult))
                link(nc.vector.tensor_tensor(vtmp2[:, cols], vtmp2[:, cols], var[:, cols], ALU.mult))
                link(nc.vector.tensor_scalar(vtmp2[:, cols], vtmp2[:, cols], EPS, None, ALU.add))
                rsqrt(nc, link, vtmp[:, cols], vtmp[:, cols].bitcast(I32), ratio[:, cols], vtmp2[:, cols])
                link(nc.vector.tensor_tensor(rs[:, cols], rs[:, cols], vtmp[:, cols], ALU.mult))
                link(nc.vector.tensor_tensor(ratio[:, cols], vtmp[:, cols], vtmp2[:, cols], ALU.mult))

        def tile_norms(dve, link, g):
            t0, t1 = HALVES[g]
            dve.wait_ge(hm_loaded[g], 16 * (g + 1))
            for t in range(t0, t1):
                nc.vector.bn_stats(bst[:, t, :], hm[:, t, :]).then_inc(tile_stats, 1)
            dve.wait_ge(tile_stats, t1)
            row_norms(dve, link, cols=slice(t0, t1))

        def row_stats(dve, b, resid_done):
            for c in range(2):
                dve.wait_ge(st_set, 1)
                dve.wait_ge(resid_done, b * 2 + c + 1)
                nc.vector.bn_stats(bst[0:R[c], bass.ds(b * 2 + c, 1), :].squeeze(1), h[0:R[c], bass.ds(b * 2 + c, 1), :].squeeze(1))

        def normed(b, c, xhat, done):
            r, t = R[c], 2 * b + c
            nc.vector.tensor_scalar(xhat[0:r, c, :], h[0:r, bass.ds(t, 1), :],
                                    mean[0:r, bass.ds(t, 1)], rs[0:r, bass.ds(t, 1)], ALU.subtract, ALU.mult).then_inc(done, 1)

        def attention(layer):
            causal = layer == 0
            with ExitStack() as e:
                def s_(name):
                    return sem(f"{name}_{layer}", e)

                def t_(name, shape, dt=F32):
                    return sb(f"{name}_{layer}", shape, dt, e)

                def two_of(name, shape, dt=F32):
                    return [t_(f"{name}{p}", shape, dt) for p in range(2)]

                xhat = t_("xhat", [R[0], 2, D])
                xT = two_of("xT", [128, KD, T])
                qk = t_("qk", [R[0], 2, 2 * H, HD])
                ru = two_of("ru", [R[0], 2, 2 * H, HD])
                rw = t_("rw", [R[0], 2, 2 * H, HD])
                hl = t_("hl", [R[0], 2, 2 * H, 4, HD], F16)
                v_row = two_of("v_row", [R[0], 2, D])
                vaug = two_of("vaug", [R[0], 2, H, 32])
                kst = two_of("kst", [128, H // 2, 166], F16)
                qA = two_of("qA", [128, H // 2, 166], F16)
                qB = two_of("qB", [128, H // 2, 166], F16)
                mx = t_("mx", [R[0], 2, H])
                nm = t_("nm", [R[0], 2, H], BF16)
                nmT = two_of("nmT", [128, T], BF16)
                prob = [two_of(f"prob{g}", [R[0], G, T]) for g in range(2)]
                oT = two_of("oT", [128, NG, T])
                den = t_("den", [R[0], 2, H])
                y = t_("y", [R[0], 2, H, HD])
                yT = t_("yT", [128, KD, T])
                if layer == 1:
                    per = two_of("per", [R[0], 2])
                    rad2 = t_("rad2", [R[0], 2])
                    hs1 = t_("hs1", [R[0], 2, 2 * H])
                    hs2 = t_("hs2", [R[0], 2, 2 * H])
                    hsq = two_of("hsq", [R[0], 2, 2 * H])
                    hx = t_("hx", [R[0], 2, 2 * H])
                    hv = t_("hv", [R[0], 2, 2 * H])
                    hy = t_("hy", [R[0], 2, 2 * H])
                    hz = t_("hz", [R[0], 2, 2 * H])

                start_l = s_("start_l")
                chain_s = s_("chain") if layer == 1 else None
                set_ok, ones_ok = s_("buffers_set"), s_("ones_set")
                xhat_ready, xhatT_done, xT_ready = s_("xhat_ready"), s_("xhatT_done"), s_("xT_ready")
                qk_done, qk_read, v_done, v_read = s_("qk_done"), s_("qk_read"), s_("v_done"), s_("v_read")
                v_kept = s_("v_kept")
                rope_parts, roped = s_("rope_parts"), s_("roped")
                if layer == 1:
                    per_ready = s_("per_ready")
                    sq_summed = s_("sq_summed")
                    summed, mean_ready, centred, squared = s_("summed"), s_("mean_ready"), s_("centred"), s_("squared")
                    scale_ready, scaled, weighted, shifted = s_("scale_ready"), s_("scaled"), s_("weighted"), s_("shifted")
                hi_ready, lo_ready, twice_ready = s_("hi_ready"), s_("lo_ready"), s_("twice_ready")
                kT_done, qT_done, k_ready, qa_ready, qb_ready = s_("kT_done"), s_("qT_done"), s_("k_ready"), s_("qa_ready"), s_("qb_ready")
                s_ready, max_done, nm_ready, nmT_done, nmT_ready = s_("s_ready"), s_("max_done"), s_("nm_ready"), s_("nmT_done"), s_("nmT_ready")
                st_ready, exp_done, pv_done, oT_ready = s_("st_ready"), s_("exp_done"), s_("pv_done"), s_("oT_ready")
                o_done, den_ready, y_ready, yT_done, yT_ready = s_("o_done"), s_("den_ready"), s_("y_ready"), s_("yT_done"), s_("yT_ready")
                proj_done, resid_done = s_("proj_done"), s_("resid_done")

                t16 = ps_t[:, :].bitcast(F16)
                v16 = ps_v[:, :].bitcast(F16)
                ob16 = ps_o[:, :].bitcast(BF16)
                s_tile, st_tile = ring

                def stacked(x, lo=0, hi=128, r=R[0]):
                    return x[lo:hi, 0:672].rearrange("p (h t) -> p h t", h=H // 2)[:, :, 0:r]

                def q_of(hd, p):
                    return (qA, qB)[hd % 2][p]

                def key_cols(c):
                    return R[0] if causal and c == 0 else T

                def first_q(c):
                    return O[c] if causal else 0

                def run(eng, turn):
                    for t in range(-4, 3):
                        turn(t, t % 2, lambda k, t=t: 0 <= t + k < B)
                    n = (B - 7) // 2
                    with eng.Fori(0, n) as i:
                        turn(i * 2 + 3, 1, lambda k: True)
                        turn(i * 2 + 4, 0, lambda k: True)
                    for t in range(2 * n + 3, B + 1):
                        turn(t, t % 2, lambda k, t=t: 0 <= t + k < B)

                with nc.Block() as block:

                    @block.sync
                    def _(sp):
                        if causal:
                            sp.wait_ge(zeros_set, 1)
                            sp.dma_start(h_rows[NTOK:NTOK + BK, :], zeros[:, :]).then_inc(spare_cleared, 16)
                            return

                        def send(b, sent):
                            sp.wait_ge(resid_done, b * 2 + 2)
                            for c in range(2):
                                sp.dma_start(h_rows[0:NTOK, :].rearrange("(b t) d -> t b d", t=T)[O[c]:O[c] + R[c], bass.ds(b, 1), :],
                                             h[0:R[c], bass.ds(b * 2 + c, 1), :]).then_inc(sent, 16)

                        done = -(-128 * HALVES[0][1] // T)
                        with sp.Fori(0, done) as i:
                            send(i, rows_sent[0])
                        sp.wait_ge(rows_sent[0], 16 * 2 * done)
                        t0, t1 = HALVES[0]
                        sp.dma_start(hm[:, t0:t1, :], h_rows[0:128 * t1, :].rearrange("(t p) d -> p t d", p=128)).then_inc(hm_loaded[0], 16)
                        with sp.Fori(done, B) as i:
                            send(i, rows_sent[1])
                        sp.wait_ge(rows_sent[1], 16 * 2 * (B - done))
                        sp.wait_ge(hm_set, 1)
                        t0, t1 = HALVES[1]
                        sp.dma_start(hm[:, t0:t1 - 1, :], h_rows[128 * t0:128 * (t1 - 1), :].rearrange("(t p) d -> p t d", p=128)).then_inc(hm_loaded[1], 16)
                        sp.dma_start(hm[0:rows_of(NT - 1), NT - 1, :], h_rows[128 * (NT - 1):NTOK, :]).then_inc(hm_loaded[1], 16)

                    @block.vector
                    def _(dve):
                        link = Chain(dve, start_l)
                        if layer == 1:
                            nc.vector.memset(hm[:, NT - 1, :], 0.0).then_inc(hm_set, 1)
                        row_norms(dve, link, second=layer == 1)
                        dve.wait_ge(loads["attn0"], 48)
                        dve.wait_ge(set_ok, 7 if layer == 1 else 4)
                        dve.wait_ge(ones_ok, 4 if causal else 2)
                        if layer == 1:
                            dve.wait_ge(loads["attn1"], 16 * 8)
                        start, link = link, Chain(dve, chain_s, 17 if layer == 1 else 0)

                        def xhats(b, p):
                            wait(dve, xhatT_done, b * 1)
                            for c in range(2):
                                normed(b, c, xhat, xhat_ready)

                        def qk_in(b, c):
                            r = R[c]
                            dve.wait_ge(qk_done, b * 2 + c + 1)
                            wait(dve, roped, b * 2)
                            nc.vector.tensor_tensor(qk[0:r, c, :, :].rearrange("r h d -> r (h d)"), ps_qk[0:r, :],
                                                    b_qkv[layer][0:r, 0:512], ALU.add).then_inc(qk_read, 1)

                        def v_in(b, p, c):
                            r = R[c]
                            dve.wait_ge(v_done, b * 2 + c + 1)
                            wait(dve, v_kept, b * 2 - 2)
                            nc.vector.tensor_tensor(v_row[p][0:r, c, :], ps_v[0:r, 0:D], b_qkv[layer][0:r, 512:768], ALU.add).then_inc(v_read, 1)
                            if layer == 1:
                                nc.vector.tensor_tensor(per[p][0:r, c:c + 1], ps_v[0:r, D:D + 1], ratio[0:r, bass.ds(b * 2 + c, 1)],
                                                        ALU.mult).then_inc(per_ready, 1)

                        def q_in(b, p, c):
                            r = R[c]
                            dve.wait_ge(qT_done, b * 2 + c + 1)
                            nc.vector.tensor_copy(qA[p][0:64, :, O[c]:O[c] + r], stacked(v16, 0, 64, r)).then_inc(qa_ready, 1)

                        def head_means(b, p):
                            for c in range(2):
                                r = R[c]
                                dve.wait_ge(roped, b * 2 + c + 1)
                                nc.vector.tensor_reduce(hs1[0:r, c, :], ru[p][0:r, c, :, :], AX.X, ALU.add).then_inc(summed, 1)
                            for c in range(2):
                                r = R[c]
                                dve.wait_ge(summed, b * 2 + c + 1)
                                nc.vector.tensor_scalar(hs2[0:r, c, :], hs1[0:r, c, :], -1.0 / HD, None, ALU.mult).then_inc(mean_ready, 1)

                        def head_squares(b, p):
                            for c in range(2):
                                r = R[c]
                                dve.wait_ge(squared, b * 2 + c + 1)
                                nc.vector.tensor_reduce(hsq[p][0:r, c, :], rw[0:r, c, :, :], AX.X, ALU.add).then_inc(sq_summed, 1)

                        def radii(b, p):
                            link.start(b)
                            dve.wait_ge(per_ready, b * 2 + 2)
                            link(nc.vector.tensor_scalar(per[p][:, :], per[p][:, :], rh_b[:, 0:1], 0.01, ALU.add, ALU.mult))
                            link(nc.vector.tensor_scalar(per[p][:, :], per[p][:, :], 0.5, 2.0, ALU.max, ALU.min))
                            link(nc.vector.tensor_tensor(rad2[:, :], per[p][:, :], per[p][:, :], ALU.mult))

                        def variances(b, p):
                            for c in range(2):
                                r = R[c]
                                dve.wait_ge(sq_summed, b * 2 + c + 1)
                                link.count(nc.vector.tensor_scalar(hx[0:r, c, :], hsq[p][0:r, c, :], rad2[0:r, c:c + 1], 1.0 / HD, ALU.mult, ALU.mult))
                            link.hold()
                            link(nc.vector.tensor_scalar(hv[:, :, :], hx[:, :, :], EPS, None, ALU.add))
                            rsqrt_guess(nc, link, hy[:, :, :].bitcast(I32), hv[:, :, :])

                        def newton():
                            rsqrt_step(nc, link, hy[:, :, :], hz[:, :, :], hv[:, :, :])

                        def scale_heads(b, p):
                            for c in range(2):
                                r = R[c]
                                nc.vector.tensor_scalar(hz[0:r, c, :], hy[0:r, c, :], per[p][0:r, c:c + 1], None, ALU.mult).then_inc(scale_ready, 1)
                            for c in range(2):
                                r = R[c]
                                dve.wait_ge(scale_ready, b * 2 + c + 1)
                                nc.vector.tensor_tensor(ru[p][0:r, c, :, :], ru[p][0:r, c, :, :],
                                                        hz[0:r, c, :].unsqueeze(2).to_broadcast([r, 2 * H, HD]), ALU.mult).then_inc(scaled, 1)

                        def lows(b, p):
                            for c in range(2):
                                r = R[c]
                                dve.wait_ge(hi_ready, b * 2 + c + 1)
                                nc.vector.tensor_tensor(hl[0:r, c, :, 1, :], ru[p][0:r, c, :, :], hl[0:r, c, :, 0, :],
                                                        ALU.subtract).then_inc(lo_ready, 1)
                                dve.wait_ge(lo_ready, b * 2 + c + 1)
                                nc.vector.tensor_copy(hl[0:r, c, 0:H, 2:4, :], hl[0:r, c, 0:H, 0:2, :]).then_inc(twice_ready, 1)
                                nc.vector.tensor_copy(hl[0:r, c, H:2 * H, 3:1:-1, :], hl[0:r, c, H:2 * H, 0:2, :]).then_inc(twice_ready, 1)

                        def maxes(b, n):
                            c, g = divmod(n, NG)
                            dve.wait_ge(s_ready, b * 8 + n + 1)
                            nc.vector.tensor_reduce(mx[0:R[c], c, G * g:G * g + G], s_tile[0:R[c], :, 0:key_cols(c)],
                                                    AX.X, ALU.max).then_inc(max_done, 1)

                        def max_rows(b):
                            dve.wait_ge(max_done, b * 8 + 8)
                            for c in range(2):
                                nc.vector.tensor_scalar(nm[0:R[c], c, :], mx[0:R[c], c, :], -1.0, None, ALU.mult).then_inc(nm_ready, 1)

                        def maxima_in(b):
                            dve.wait_ge(nmT_done, b * 1 + 1)
                            wait(dve, st_ready, b * 8)
                            for p in range(2 if causal else 1):
                                nc.vector.tensor_copy(nmT[p][0:H, :], ob16[0:H, 0:T]).then_inc(nmT_ready, 1)

                        def normalize(b, c):
                            r = R[c]
                            o = two[c][0:r, :].rearrange("r (h x) -> r h x", h=H)
                            dve.wait_ge(o_done, b * 2 + c + 1)
                            nc.vector.reciprocal(den[0:r, c, :], o[:, :, HD:HD + 1].squeeze(2)).then_inc(den_ready, 1)
                            dve.wait_ge(den_ready, b * 2 + c + 1)
                            nc.vector.tensor_tensor(y[0:r, c, :, :], o[:, :, 0:HD],
                                                    den[0:r, c, :].unsqueeze(2).to_broadcast([r, H, HD]), ALU.mult).then_inc(y_ready, 1)

                        def residual(b):
                            for c in range(2):
                                r, t = R[c], b * 2 + c
                                dve.wait_ge(proj_done, b * 2 + c + 1)
                                nc.vector.tensor_tensor(h[0:r, bass.ds(t, 1), :].squeeze(1), h[0:r, bass.ds(t, 1), :].squeeze(1),
                                                        two[c][0:r, 0:D], ALU.add).then_inc(resid_done, 1)

                        def turn(s, p, on):
                            if on(0):
                                maxima_in(s)
                            if on(3):
                                qk_in(s + 3, 0)
                            if on(1):
                                q_in(s + 1, 1 - p, 0)
                            if on(2) and layer == 1:
                                head_squares(s + 2, p)
                            if on(1):
                                q_in(s + 1, 1 - p, 1)
                            if on(3):
                                qk_in(s + 3, 1)
                            for i in range(8):
                                if on(1):
                                    maxes(s + 1, i)
                                if on(3) and i in (0, 1):
                                    v_in(s + 3, 1 - p, i)
                                if on(-1) and i in (2, 3):
                                    normalize(s - 1, i - 2)
                                if on(2) and layer == 1:
                                    if i == 0:
                                        radii(s + 2, p)
                                        variances(s + 2, p)
                                    if i in (1, 2, 3):
                                        newton()
                                    if i == 4:
                                        scale_heads(s + 2, p)
                                if on(-1) and i == 6:
                                    residual(s - 1)
                                if on(4) and i == (4 if causal else 5):
                                    xhats(s + 4, p)
                                if on(2) and causal and i == 5:
                                    lows(s + 2, p)
                                if on(3) and layer == 1 and i == 5:
                                    head_means(s + 3, 1 - p)
                            if on(1):
                                max_rows(s + 1)
                            if on(2) and not causal:
                                lows(s + 2, p)
                            if on(4) and not on(3):
                                for q in range(2):
                                    nc.vector.memset(qA[q][64:128, :, :], 0.0)
                                    nc.vector.memset(qB[q][0:64, :, :], 0.0)
                            if on(-1) and causal:
                                row_stats(dve, s - 1, resid_done)
                            if layer == 1 and not on(2) and not on(1) and on(0):
                                tile_norms(dve, start, 0)

                        run(dve, turn)

                    @block.gpsimd
                    def _(pool):
                        for p in range(2):
                            nc.gpsimd.memset(vaug[p][:, :, :, :], 0.0).then_inc(set_ok, 1)
                            nc.gpsimd.memset(nmT[p][:, :], 0.0).then_inc(set_ok, 1)
                            if layer == 1:
                                nc.gpsimd.memset(per[p][:, :], 1.0).then_inc(set_ok, 1)
                        if layer == 1:
                            nc.gpsimd.memset(hx[:, :, :], 1.0).then_inc(set_ok, 1)
                        pool.wait_ge(set_ok, 7 if layer == 1 else 4)
                        for p in range(2):
                            nc.gpsimd.memset(vaug[p][:, :, :, HD:HD + 1], 1.0).then_inc(ones_ok, 1)
                            if causal:
                                nc.gpsimd.tensor_copy(nmT[p][:, :], mask_t[:, p, :]).then_inc(ones_ok, 1)
                        pool.wait_ge(loads["consts"], 16 * 16)

                        def rope(b, p, c):
                            r = R[c]
                            cs = cos_t[layer][0:r, c, :].unsqueeze(1).to_broadcast([r, 2 * H, HD])
                            pool.wait_ge(qk_read, b * 2 + c + 1)
                            wait(pool, lo_ready, b * 2 - 2)
                            nc.gpsimd.tensor_tensor(ru[p][0:r, c, :, :], qk[0:r, c, :, :], cs, ALU.mult).then_inc(rope_parts, 1)
                            if layer == 1:
                                wait(pool, sq_summed, b * 2)
                            for half in range(2):
                                o = slice(8 * half, 8 * half + 8)
                                i = slice(8 - 8 * half, 16 - 8 * half)
                                sn = sin_t[layer][0:r, c, o].unsqueeze(1).to_broadcast([r, 2 * H, 8])
                                nc.gpsimd.tensor_tensor(rw[0:r, c, :, o], qk[0:r, c, :, i], sn, ALU.mult).then_inc(rope_parts, 1)
                            pool.wait_ge(rope_parts, b * 6 + 3 * c + 3)
                            nc.gpsimd.tensor_tensor(ru[p][0:r, c, :, :], ru[p][0:r, c, :, :], rw[0:r, c, :, :], ALU.add).then_inc(roped, 1)

                        def centre(b, p):
                            for c in range(2):
                                r = R[c]
                                pool.wait_ge(mean_ready, b * 2 + c + 1)
                                nc.gpsimd.tensor_tensor(ru[p][0:r, c, :, :], ru[p][0:r, c, :, :],
                                                        hs2[0:r, c, :].unsqueeze(2).to_broadcast([r, 2 * H, HD]), ALU.add).then_inc(centred, 1)

                        def weigh_heads(b, p):
                            for c in range(2):
                                r = R[c]
                                pool.wait_ge(scaled, b * 2 + c + 1)
                                nc.gpsimd.tensor_tensor(ru[p][0:r, c, :, :], ru[p][0:r, c, :, :],
                                                        ln_w[0:r, :].unsqueeze(1).to_broadcast([r, 2 * H, HD]), ALU.mult).then_inc(weighted, 1)
                                pool.wait_ge(weighted, b * 2 + c + 1)
                                nc.gpsimd.tensor_tensor(ru[p][0:r, c, :, :], ru[p][0:r, c, :, :],
                                                        ln_b[0:r, :].unsqueeze(1).to_broadcast([r, 2 * H, HD]), ALU.add).then_inc(shifted, 1)

                        def turn(s, p, on):
                            if on(3):
                                for c in range(2):
                                    rope(s + 3, 1 - p, c)
                            if on(2) and layer == 1:
                                weigh_heads(s + 2, p)
                            if on(3) and layer == 1:
                                centre(s + 3, 1 - p)

                        run(pool, turn)

                    @block.scalar
                    def _(act):
                        act.wait_ge(set_ok, 7 if layer == 1 else 4)

                        def v_keep(b, p, c):
                            r = R[c]
                            act.wait_ge(v_read, b * 2 + c + 1)
                            wait(act, pv_done, b * 4 - 4)
                            nc.scalar.copy(vaug[p][0:r, c, :, 0:HD], v_row[p][0:r, c, :].rearrange("r (h d) -> r h d", h=H)).then_inc(v_kept, 1)

                        def k_in(b, p, c):
                            r = R[c]
                            act.wait_ge(kT_done, b * 2 + c + 1)
                            nc.scalar.copy(kst[p][:, :, O[c]:O[c] + r], stacked(t16, r=r)).then_inc(k_ready, 1)
                            act.wait_ge(qT_done, b * 2 + c + 1)
                            nc.scalar.copy(qB[p][64:128, :, O[c]:O[c] + r], stacked(v16, 64, 128, r)).then_inc(qb_ready, 1)

                        def exps(b, m):
                            g, c = divmod(m, 2)
                            r, q0 = R[c], first_q(c)
                            act.wait_ge(st_ready, b * 8 + m + 1)
                            wait(act, pv_done, b * 4 + max(g - 1, 0))
                            nc.scalar.activation(prob[g % 2][c][0:r, :, q0:T], st_tile[0:r, :, q0:T], ACT.Exp,
                                                 scale=HD ** -0.5).then_inc(exp_done, 1)

                        def out_in(b, p, g):
                            act.wait_ge(pv_done, b * 4 + g + 1)
                            nc.scalar.copy(oT[p][:, g, :], ps_o[:, 0:T]).then_inc(oT_ready, 1)

                        def squares(b, p, c):
                            r = R[c]
                            act.wait_ge(centred, b * 2 + c + 1)
                            nc.scalar.activation(rw[0:r, c, :, :], ru[p][0:r, c, :, :], ACT.Square).then_inc(squared, 1)

                        def highs(b, p, c):
                            r = R[c]
                            if layer == 1:
                                act.wait_ge(shifted, b * 2 + c + 1)
                            else:
                                act.wait_ge(roped, b * 2 + c + 1)
                            wait(act, qT_done, b * 2)
                            nc.scalar.copy(hl[0:r, c, :, 0, :], ru[p][0:r, c, :, :]).then_inc(hi_ready, 1)

                        def turn_in(done, b, dst, ready):
                            act.wait_ge(done, b * 1 + 1)
                            nc.scalar.copy(dst[:, :, :], ps_t[:, 0:336].rearrange("p (k t) -> p k t", k=KD)[:, :, 0:T]).then_inc(ready, 1)

                        def turn(s, p, on):
                            if on(1):
                                for c in range(2):
                                    v_keep(s + 1, 1 - p, c)
                                k_in(s + 1, 1 - p, 0)
                            if on(0):
                                exps(s, 0)
                            if on(1):
                                k_in(s + 1, 1 - p, 1)
                            for i in range(8):
                                if on(0):
                                    if i:
                                        exps(s, i)
                                    if i in (3, 5, 7):
                                        out_in(s, p, i // 2 - 1)
                                if on(4) and i == 7:
                                    turn_in(xhatT_done, s + 4, xT[p], xT_ready)
                                if on(-1) and i == 4:
                                    turn_in(yT_done, s - 1, yT, yT_ready)
                                if on(2) and i in ((2, 3) if causal else (6, 7)):
                                    highs(s + 2, p, i - (2 if causal else 6))
                            if on(0):
                                out_in(s, p, NG - 1)
                            if on(3) and layer == 1:
                                for c in range(2):
                                    squares(s + 3, 1 - p, c)

                        run(act, turn)

                    @block.tensor
                    def _(pe):
                        pe.wait_ge(loads["consts"], 16 * 16)
                        pe.wait_ge(loads["attn0"], 48)
                        pe.wait_ge(set_ok, 7 if layer == 1 else 4)
                        pe.wait_ge(ones_ok, 4 if causal else 2)

                        v_taken = per_ready if layer == 1 else v_read

                        def turned(src, done):
                            for c in range(2):
                                r = R[c]
                                for k in range(KD):
                                    mm = nc.tensor.transpose(ps_t[:, 168 * k + O[c]:168 * k + O[c] + r],
                                                             src[0:r, c, 128 * k:128 * k + 128], ident[0:r, 0:r])
                            mm.then_inc(done, 1)

                        def product(o, b, p, c, col, n, done):
                            r = R[c]
                            for k in range(KD):
                                mm = nc.tensor.matmul(o[0:r, 0:n], xT[p][:, k, O[c]:O[c] + r], w_qkv[layer][:, k, col:col + n],
                                                      start=(k == 0), stop=(k == KD - 1))
                            mm.then_inc(done, 1)

                        def q_and_k(b, p, c):
                            pe.wait_ge(xT_ready, b * 1 + 1)
                            wait(pe, qk_read, b * 2 + c)
                            if c == 0:
                                wait(pe, resid_done, b * 2 - 8)
                            product(ps_qk, b, p, c, 0, 512, qk_done)

                        def v(b, p, c):
                            wait(pe, qa_ready, b * 2 - 2)
                            wait(pe, qb_ready, b * 2 - 2)
                            wait(pe, v_taken, b * 2 + c)
                            product(ps_v, b, p, c, 2 * D, D + layer, v_done)

                        def stacks(b, c):
                            r = R[c]
                            if c == 0:
                                wait(pe, xT_ready, min(b + 3, B) if isinstance(b, int) else b + 3)
                                wait(pe, resid_done, b * 2 - 4)
                                wait(pe, v_taken, min(b * 2 + 4, 2 * B) if isinstance(b, int) else b * 2 + 4)
                            wait(pe, k_ready, b * 2 + c)
                            pe.wait_ge(twice_ready, b * 4 + 2 * c + 2)
                            for i in range(H // 2):
                                mm = nc.tensor.transpose(t16[:, 84 * i:84 * i + r], hl[0:r, c, H + 2 * i:H + 2 * i + 2, :, :].rearrange("r h s d -> r (h s d)"),
                                                         ident16[0:r, 0:r])
                            mm.then_inc(kT_done, 1)
                            wait(pe, qa_ready, b * 2 + c)
                            wait(pe, qb_ready, b * 2 + c)
                            for i in range(H // 2):
                                mm = nc.tensor.transpose(v16[:, 84 * i:84 * i + r], hl[0:r, c, 2 * i:2 * i + 2, :, :].rearrange("r h s d -> r (h s d)"),
                                                         ident16[0:r, 0:r])
                            mm.then_inc(qT_done, 1)

                        def scores(b, p, n):
                            c, g = divmod(n, NG)
                            r, nk = R[c], key_cols(c)
                            if n == 0:
                                pe.wait_ge(k_ready, b * 2 + 2)
                                pe.wait_ge(qa_ready, b * 2 + 2)
                                pe.wait_ge(qb_ready, b * 2 + 2)
                            wait(pe, max_done, b * 8 + n)
                            for j in range(G):
                                hd = G * g + j
                                mm = nc.tensor.matmul(s_tile[0:r, j, 0:nk], q_of(hd, p)[:, hd // 2, O[c]:O[c] + r],
                                                      kst[p][:, hd // 2, 0:nk], start=True, stop=not causal)
                                if causal:
                                    mm = nc.tensor.matmul(s_tile[0:r, j, O[c]:nk], identb[0:R[0], 0:r],
                                                          mask_s[0:R[0], c, O[c]:nk], start=False, stop=True)
                            mm.then_inc(s_ready, 1)

                        def maxima_T(b):
                            pe.wait_ge(nm_ready, b * 2 + 2)
                            wait(pe, oT_ready, b * 4)
                            for c in range(2):
                                mm = nc.tensor.transpose(ob16[0:H, O[c]:O[c] + R[c]], nm[0:R[c], c, :], identb[0:R[c], 0:R[c]])
                            mm.then_inc(nmT_done, 1)

                        def scores_T(b, p, m):
                            g, c = divmod(m, 2)
                            r, q0 = R[c], first_q(c)
                            if m == 0:
                                pe.wait_ge(nmT_ready, b * (2 if causal else 1) + (2 if causal else 1))
                            wait(pe, exp_done, b * 8 + m)
                            for j in range(G):
                                hd = G * g + j
                                nc.tensor.matmul(st_tile[0:r, j, q0:T], kst[p][:, hd // 2, O[c]:O[c] + r], q_of(hd, p)[:, hd // 2, q0:T],
                                                 start=True, stop=False)
                                mm = nc.tensor.matmul(st_tile[0:r, j, q0:T], selh[:, hd, 0:r], nmT[c if causal else 0][:, q0:T], start=False, stop=True)
                            mm.then_inc(st_ready, 1)

                        def values(b, p, g):
                            pe.wait_ge(exp_done, b * 8 + 2 * g + 2)
                            if g == 0:
                                pe.wait_ge(v_kept, b * 2 + 2)
                            wait(pe, oT_ready, b * 4 + g)
                            for c in range(2):
                                r, q0 = R[c], first_q(c)
                                for j in range(G):
                                    mm = nc.tensor.matmul(ps_o[32 * j:32 * j + 32, q0:T], vaug[p][0:r, c, G * g + j, :],
                                                          prob[g % 2][c][0:r, j, q0:T], start=(c == 0), stop=(c == 1))
                            mm.then_inc(pv_done, 1)

                        def outs_turned(b, p, c):
                            r = R[c]
                            pe.wait_ge(oT_ready, b * 4 + 4)
                            wait(pe, resid_done, b * 2)
                            for g in range(NG):
                                mm = nc.tensor.transpose(two[c][0:r, 128 * g:128 * g + 128], oT[p][:, g, O[c]:O[c] + r], ident[:, :])
                            mm.then_inc(o_done, 1)

                        def project(b, c):
                            r = R[c]
                            pe.wait_ge(yT_ready, b * 1 + 1)
                            for k in range(KD):
                                nc.tensor.matmul(two[c][0:r, 0:D], yT[:, k, O[c]:O[c] + r], w_out[layer][:, k, :],
                                                 start=(k == 0), stop=False)
                            nc.tensor.matmul(two[c][0:r, 0:D], ones_b[:, 0:r], b_out[layer][:, :], start=False, stop=True).then_inc(proj_done, 1)

                        def turn(s, p, on):
                            if on(3):
                                q_and_k(s + 3, 1 - p, 0)
                            if on(0):
                                maxima_T(s)
                            if on(1):
                                stacks(s + 1, 0)
                            if on(0):
                                scores_T(s, p, 0)
                            if on(1):
                                stacks(s + 1, 1)
                            if on(3):
                                q_and_k(s + 3, 1 - p, 1)
                            for i in range(8):
                                if on(0) and i:
                                    scores_T(s, p, i)
                                if on(1):
                                    scores(s + 1, 1 - p, i)
                                if on(3) and i in (0, 1):
                                    v(s + 3, 1 - p, i)
                                if on(4) and i == 7:
                                    pe.wait_ge(xhat_ready, (s + 4) * 2 + 2)
                                    if on(-1):
                                        pe.wait_ge(yT_ready, s * 1)
                                    elif on(1):
                                        pe.wait_ge(k_ready, s * 2 + 4)
                                    turned(xhat, xhatT_done)
                                if on(0) and i in (2, 4, 6):
                                    values(s, p, i // 2 - 1)
                                if on(0) and i == 7:
                                    values(s, p, 3)
                                if on(-1) and i in (1, 2):
                                    if i == 1 and on(3):
                                        pe.wait_ge(qk_read, s * 2 + 8)
                                    if i == 2 and on(3):
                                        pe.wait_ge(v_taken, s * 2 + 8)
                                    if i == 2 and on(1):
                                        pe.wait_ge(qa_ready, s * 2 + 4)
                                        pe.wait_ge(qb_ready, s * 2 + 4)
                                    outs_turned(s - 1, 1 - p, i - 1)
                                if on(-1) and i == 4:
                                    pe.wait_ge(y_ready, s * 2)
                                    if on(1):
                                        pe.wait_ge(k_ready, s * 2 + 4)
                                    turned(y_rows, yT_done)
                                if on(-1) and i in (5, 6):
                                    for c in (i - 5,) if causal else (0, 1) if i == 5 else ():
                                        project(s - 1, c)
                        y_rows = y[:, :, :, :].rearrange("r c h d -> r c (h d)")
                        run(pe, turn)

        def feed_forward():
            with ExitStack() as e:
                xhat = sb("xhat_f", [R[0], 2, D], to=e)
                xT = sb("xT_f", [128, KD, T], to=e)
                pT = sb("pT_f", [RANK + 1, T], to=e)
                hT = [sb(f"hT_f{i}", [128, 4, T], to=e) for i in range(2)]
                qT = sb("qT_f", [RANK + 1, T], to=e)
                start_l, set_ok = sem("start_l_f", e), sem("set_ok_f", e)
                xhat_ready, xhatT_done, xT_ready = sem("xhat_ready_f", e), sem("xhatT_done_f", e), sem("xT_ready_f", e)
                p_done, p_ready, h_done, gelu_done = sem("p_done", e), sem("p_ready", e), sem("h_done", e), sem("gelu_done", e)
                q_done, q_ready, f_done, resid_done = sem("q_done", e), sem("q_ready_f", e), sem("f_done", e), sem("resid_done_f", e)

                def run(eng, turn):
                    for t in range(-3, 2):
                        turn(t, lambda k, t=t: 0 <= t + k < B)
                    with eng.Fori(2, B - 3) as t:
                        turn(t, lambda k: True)
                    for t in range(B - 3, B + 1):
                        turn(t, lambda k, t=t: 0 <= t + k < B)

                with nc.Block() as block:

                    @block.vector
                    def _(dve):
                        nc.vector.memset(pT[RANK:RANK + 1, :], 1.0).then_inc(set_ok, 1)
                        nc.vector.memset(qT[RANK:RANK + 1, :], 1.0).then_inc(set_ok, 1)
                        row_norms(dve, Chain(dve, start_l))

                        def turn(s, on):
                            if on(-1):
                                for c in range(2):
                                    r, t = R[c], (s - 1) * 2 + c
                                    dve.wait_ge(f_done, s * 2)
                                    nc.vector.tensor_tensor(h[0:r, bass.ds(t, 1), :].squeeze(1), h[0:r, bass.ds(t, 1), :].squeeze(1),
                                                            ps_v[0:r, D * c:D * c + D], ALU.add).then_inc(resid_done, 1)
                            if on(1):
                                wait(dve, h_done, s * 2 + 2)
                                dve.wait_ge(p_done, s + 2)
                                nc.vector.tensor_copy(pT[0:RANK, :], ps_qk[0:RANK, 0:T]).then_inc(p_ready, 1)
                            if on(2):
                                wait(dve, p_done, s + 2)
                                dve.wait_ge(xhatT_done, s + 3)
                                nc.vector.tensor_copy(xT[:, :, :], ps_t[:, 0:336].rearrange("p (k t) -> p k t", k=KD)[:, :, 0:T]).then_inc(xT_ready, 1)
                            if on(3):
                                wait(dve, xhatT_done, s + 3)
                                for c in range(2):
                                    normed(s + 3, c, xhat, xhat_ready)
                            if on(-1):
                                row_stats(dve, s - 1, resid_done)
                            if on(0):
                                wait(dve, f_done, s * 2)
                                dve.wait_ge(q_done, s + 1)
                                nc.vector.tensor_copy(qT[0:RANK, :], ps_o[0:RANK, 0:T]).then_inc(q_ready, 1)

                        run(dve, turn)

                    @block.scalar
                    def _(act):
                        def turn(s, on):
                            if on(0):
                                for i in range(2):
                                    wait(act, q_done, s * 1)
                                    act.wait_ge(h_done, s * 2 + i + 1)
                                    nc.scalar.activation(hT[i][:, :, :], ring[i][:, :, 0:T], ACT.Gelu_apprx_tanh).then_inc(gelu_done, 1)

                        run(act, turn)

                    @block.tensor
                    def _(pe):
                        pe.wait_ge(loads["ffn0"], 16 * 5)
                        pe.wait_ge(set_ok, 2)

                        def turn(s, on):
                            if on(0):
                                pe.wait_ge(p_ready, s + 1)
                                for i in range(2):
                                    wait(pe, gelu_done, s * 2 + i - 1)
                                    for j in range(4):
                                        n = 4 * i + j
                                        mm = nc.tensor.matmul(ring[i][:, j, 0:T], v1[:, 128 * n:128 * n + 128], pT[:, :], start=True, stop=True)
                                    mm.then_inc(h_done, 1)
                            if on(-1):
                                pe.wait_ge(q_ready, s * 1)
                                wait(pe, resid_done, s * 2 - 2)
                                for c in range(2):
                                    nc.tensor.matmul(ps_v[0:R[c], D * c:D * c + D], qT[:, O[c]:O[c] + R[c]], v2[:, :],
                                                     start=True, stop=True).then_inc(f_done, 1)
                            if on(1):
                                wait(pe, p_ready, s + 1)
                                pe.wait_ge(xT_ready, s + 2)
                                for k in range(KD):
                                    mm = nc.tensor.matmul(ps_qk[0:RANK, 0:T], u1[:, k, :], xT[:, k, :], start=(k == 0), stop=(k == KD - 1))
                                mm.then_inc(p_done, 1)
                            if on(2):
                                wait(pe, xT_ready, s + 2)
                                pe.wait_ge(xhat_ready, s * 2 + 6)
                                for c in range(2):
                                    for k in range(KD):
                                        mm = nc.tensor.transpose(ps_t[:, 168 * k + O[c]:168 * k + O[c] + R[c]],
                                                                 xhat[0:R[c], c, 128 * k:128 * k + 128], ident[0:R[c], 0:R[c]])
                                mm.then_inc(xhatT_done, 1)
                            if on(0):
                                wait(pe, q_ready, s * 1)
                                for n in range(FF // 128):
                                    if n % 4 == 0:
                                        pe.wait_ge(gelu_done, s * 2 + n // 4 + 1)
                                    mm = nc.tensor.matmul(ps_o[0:RANK, 0:T], u2[:, n, :], hT[n // 4][:, n % 4, :],
                                                          start=(n == 0), stop=(n == FF // 128 - 1))
                                mm.then_inc(q_done, 1)

                        run(pe, turn)

        def route(lane_row, lane_add, lane_weight, block_expert, w1, w2):
            with ExitStack() as e:
                xr = sb("xhat_r", [128, NT, D], to=e)
                xT = [sb(f"xT_r{p}", [128, KD, 128], to=e) for p in range(2)]
                lg = sb("lg", [128, NT, NE], to=e)
                val = sb("val", [128, NT, NE], to=e)
                hot = [sb(f"hot{i}", [128, NT, NE], to=e) for i in range(2)]
                taken = sb("taken", [128, NT + 1, NE], BF16, to=e)
                best = [sb(f"best{i}", [128, NT], to=e) for i in range(2)]
                idx = sb("idx", [128, NT], to=e)
                ex = sb("ex", [128, NT], to=e)
                n_i = sb("n_i", [128, NE], I32, to=e)
                blocks = sb("blocks", [128, NE], to=e)
                first_block = sb("first_block", [128, NE + 1], to=e)
                before = sb("before", [1, NBK, NE], to=e)
                expert_f = sb("expert_f", [1, NBK], to=e)
                weight = [sb(f"weight{i}", [128, NT], to=e) for i in range(2)]
                slot_i = sb("slot_i", [128, NT], I32, to=e)
                part_i = sb("part_i", [128, NT], I32, to=e)
                in_block = sb("in_block", [128, NT, NBK], to=e)
                place = h[:, :, :].rearrange("p t d -> p (t d)")
                in_lane = [place[:, NT * BK * i:NT * BK * (i + 1)].rearrange("p (t l) -> p t l", l=BK) for i in range(2)]
                marks = [place[:, 2 * NT * BK:2 * NT * (BK + NBK)].rearrange("p (t w j) -> p t w j", w=2, j=NBK),
                         sb("marks", [128, NT, 2, NBK], to=e)]
                empty = sb("empty", [128, NBK], to=e)
                chain_s = sem("chain_r", e)
                xhat_ready, xhatT_done, xT_ready = sem("xhat_ready_r", e), sem("xhatT_done_r", e), sem("xT_ready_r", e)
                lg_done, diff_done, exp_done = sem("lg_done", e), sem("diff_done", e), sem("exp_done_r", e)
                taken_set, taken_ready, ranks_done = sem("taken_set", e), sem("taken_ready", e), sem("ranks_done", e)
                marks_ready, lanes_done, rows_written = sem("marks_ready", e), sem("lanes_done", e), sem("rows_written", e)
                lanes = ps_v[:, 0:2 * NBK].rearrange("p (w j) -> p w j", w=2)
                turned = (ps_t, ps_v)
                ranks = ps_qk[:, 0:(NT + 1) * NE].rearrange("p (t x) -> p t x", x=NE)
                with nc.Block() as block:

                    @block.sync
                    def _(sp):
                        for x in range(NE):
                            sp.dma_start(w1[:, x, :, :], a["w1"][:, x, :, :]).then_inc(loads["moe"], 16)
                            sp.dma_start(w2[:, x, :, :], a["w2"][:, x, :, :]).then_inc(loads["moe"], 16)
                        sp.wait_ge(xhat_ready, NT)
                        full = NTOK // 128
                        sp.dma_start(x_rows[0:128 * full, :].rearrange("(t p) d -> p t d", p=128), xr[:, 0:full, :]).then_inc(rows_written, 16)
                        sp.dma_start(x_rows[128 * full:NTOK, :], xr[0:NTOK - 128 * full, full, :]).then_inc(rows_written, 16)
                        sp.wait_ge(rows_written, 32)

                    @block.vector
                    def _(dve):
                        link = Chain(dve, chain_s)
                        nc.vector.memset(taken[:, NT, :], 0.0).then_inc(taken_set, 1)
                        for g, (t0, t1) in enumerate(HALVES):
                            if g:
                                tile_norms(dve, link, g)
                            for t in range(t0, t1):
                                nc.vector.tensor_scalar(xr[:, t, :], hm[:, t, :], mean[:, t:t + 1], rs[:, t:t + 1],
                                                        ALU.subtract, ALU.mult).then_inc(xhat_ready, 1)
                        dve.wait_ge(lg_done, NT)
                        link(nc.vector.tensor_copy(lg[:, :, :], ps_o[:, 0:NT * NE].rearrange("p (t x) -> p t x", x=NE)))
                        full = [128, NT, NE]

                        def over(x):
                            return x[:, :].unsqueeze(2).to_broadcast(full)

                        io = iota[:, :].unsqueeze(1).to_broadcast(full)
                        for i in range(2):
                            link(nc.vector.tensor_reduce(best[i][:, :], lg[:, :, :], AX.X, ALU.max))
                            link(nc.vector.tensor_tensor(val[:, :, :], lg[:, :, :], over(best[i]), ALU.is_lt))
                            link(nc.vector.scalar_tensor_tensor(out=val[:, :, :], in0=val[:, :, :], scalar=float(NE), in1=io, op0=ALU.mult, op1=ALU.add))
                            link(nc.vector.tensor_reduce(idx[:, :], val[:, :, :], AX.X, ALU.min))
                            link(nc.vector.tensor_tensor(hot[i][:, :, :], io, over(idx), ALU.is_equal))
                            if i == 0:
                                link(nc.vector.scalar_tensor_tensor(out=lg[:, :, :], in0=hot[0][:, :, :], scalar=-3e38, in1=lg[:, :, :],
                                                                    op0=ALU.mult, op1=ALU.add))
                        nc.vector.tensor_tensor(ex[:, :], best[1][:, :], best[0][:, :], ALU.subtract).then_inc(diff_done, 1)
                        link(nc.vector.tensor_tensor(val[:, :, :], hot[0][:, :, :], hot[1][:, :, :], ALU.add))
                        dve.wait_ge(taken_set, 1)
                        nc.vector.tensor_tensor(taken[:, 0:NT, :], val[:, :, :], over(valid), ALU.mult).then_inc(taken_ready, 1)
                        dve.wait_ge(exp_done, 1)
                        link(nc.vector.tensor_scalar(weight[0][:, :], ex[:, :], 1.0, None, ALU.add))
                        link(nc.vector.reciprocal(weight[0][:, :], weight[0][:, :]))
                        link(nc.vector.tensor_tensor(weight[1][:, :], ex[:, :], weight[0][:, :], ALU.mult))
                        dve.wait_ge(ranks_done, 1)
                        link(nc.vector.tensor_scalar(n_i[:, :], ranks[:, NT, :], float(BK - 1), None, ALU.add))
                        link(nc.vector.tensor_scalar(n_i[:, :], n_i[:, :], BK.bit_length() - 1, None, ALU.logical_shift_right))
                        link(nc.vector.tensor_copy(blocks[:, :], n_i[:, :]))
                        link(nc.vector.memset(first_block[:, 0:1], 0.0))
                        for x in range(NE):
                            link(nc.vector.tensor_tensor(first_block[:, x + 1:x + 2], first_block[:, x:x + 1], blocks[:, x:x + 1], ALU.add))
                        link(nc.vector.scalar_tensor_tensor(out=val[:, :, :], in0=first_block[:, 0:NE].unsqueeze(1).to_broadcast(full), scalar=float(BK),
                                                            in1=ranks[:, 0:NT, :], op0=ALU.mult, op1=ALU.add))
                        marked = [128, NT, NBK]

                        def on_blocks(x):
                            return x[:, :].unsqueeze(2).to_broadcast(marked)

                        for i in range(2):
                            link(nc.vector.tensor_tensor(hot[i][:, :, :], hot[i][:, :, :], val[:, :, :], ALU.mult))
                            link(nc.vector.tensor_reduce(idx[:, :], hot[i][:, :, :], AX.X, ALU.add))
                            link(nc.vector.tensor_copy(slot_i[:, :], idx[:, :]))
                            link(nc.vector.tensor_scalar(part_i[:, :], slot_i[:, :], BK.bit_length() - 1, None, ALU.logical_shift_right))
                            link(nc.vector.tensor_copy(idx[:, :], part_i[:, :]))
                            link(nc.vector.tensor_tensor(in_block[:, :, :], on_blocks(idx), block_no[:, :].unsqueeze(1).to_broadcast(marked), ALU.is_equal))
                            nc.vector.tensor_tensor(marks[i][:, :, 0, :], in_block[:, :, :], on_blocks(token_1), ALU.mult)
                            nc.vector.tensor_tensor(marks[i][:, :, 1, :], in_block[:, :, :], on_blocks(weight[i]), ALU.mult)
                            link(nc.vector.tensor_scalar(part_i[:, :], slot_i[:, :], BK - 1, None, ALU.bitwise_and))
                            link(nc.vector.tensor_copy(idx[:, :], part_i[:, :]))
                            nc.vector.tensor_tensor(in_lane[i][:, :, :], idx[:, :].unsqueeze(2).to_broadcast([128, NT, BK]),
                                                    lane_no[:, :].unsqueeze(1).to_broadcast([128, NT, BK]), ALU.is_equal).then_inc(marks_ready, 1)
                        link(nc.vector.tensor_tensor(before[:, :, :], first_block[0:1, 1:NE + 1].unsqueeze(1).to_broadcast([1, NBK, NE]),
                                                     block_no[0:1, :].unsqueeze(2).to_broadcast([1, NBK, NE]), ALU.is_le))
                        link(nc.vector.tensor_reduce(expert_f[:, :], before[:, :, :], AX.X, ALU.add))
                        link(nc.vector.tensor_scalar(expert_f[:, :], expert_f[:, :], float(NE - 1), None, ALU.min))
                        link(nc.vector.tensor_copy(block_expert[:, :], expert_f[:, :]))
                        dve.wait_ge(lanes_done, 1)
                        link(nc.vector.tensor_scalar(empty[:, :], lanes[:, 0, :], 0.0, None, ALU.is_equal))
                        link(nc.vector.scalar_tensor_tensor(out=empty[:, :], in0=empty[:, :], scalar=spare_1[:, 0:1], in1=lanes[:, 0, :],
                                                            op0=ALU.mult, op1=ALU.add))
                        link(nc.vector.tensor_scalar(lane_add[:, :], empty[:, :], -1.0, None, ALU.add))
                        link(nc.vector.tensor_scalar(lane_row[:, :], lanes[:, 0, :], 1.0, -1.0, ALU.max, ALU.add))
                        nc.vector.tensor_copy(lane_weight[:, :], lanes[:, 1, :])

                    @block.scalar
                    def _(act):
                        def turn(t, p):
                            wait(act, lg_done, t - 1)
                            act.wait_ge(xhatT_done, t + 1)
                            nc.scalar.copy(xT[p][:, :, :], turned[p][:, 0:KD * 128].rearrange("p (k t) -> p k t", k=KD)).then_inc(xT_ready, 1)

                        for t in range(3):
                            turn(t, t % 2)
                        with act.Fori(0, (NT - 3) // 2) as i:
                            turn(i * 2 + 3, 1)
                            turn(i * 2 + 4, 0)
                        act.wait_ge(diff_done, 1)
                        nc.scalar.activation(ex[:, :], ex[:, :], ACT.Exp).then_inc(exp_done, 1)

                    @block.tensor
                    def _(pe):
                        def transposes(t, p):
                            pe.wait_ge(xhat_ready, t + 1)
                            wait(pe, xT_ready, t - 1)
                            for k in range(KD):
                                mm = nc.tensor.transpose(turned[p][:, 128 * k:128 * k + 128],
                                                         xr[:, t, 128 * k:128 * k + 128], ident[:, :])
                            mm.then_inc(xhatT_done, 1)

                        def logits(t, p):
                            pe.wait_ge(xT_ready, t + 1)
                            for k in range(KD):
                                mm = nc.tensor.matmul(ps_o[:, NE * t:NE * t + NE], xT[p][:, k, :], gate[:, k, :],
                                                      start=(k == 0), stop=(k == KD - 1))
                            mm.then_inc(lg_done, 1)

                        transposes(0, 0)
                        for t in range(1, NT):
                            transposes(t, t % 2)
                            logits(t - 1, (t - 1) % 2)
                        logits(NT - 1, 0)
                        pe.wait_ge(taken_ready, 1)
                        nc.tensor.matmul(ranks[:, :, :], tri[:, :], taken[:, :, :], start=True, stop=False)
                        for t in range(NT):
                            mm = nc.tensor.matmul(ranks[:, t + 1:NT + 1, :], ones_b[:, :], taken[:, t, :].unsqueeze(1).to_broadcast([128, NT - t, NE]),
                                                  start=False, stop=(t == NT - 1))
                        mm.then_inc(ranks_done, 1)
                        for i in range(2):
                            pe.wait_ge(marks_ready, i + 1)
                            for t in range(NT):
                                r = rows_of(t)
                                mm = nc.tensor.matmul(lanes[:, :, :], in_lane[i][0:r, t, :], marks[i][0:r, t, :, :],
                                                      start=(i == 0 and t == 0), stop=(i == 1 and t == NT - 1))
                        mm.then_inc(lanes_done, 1)

        def experts(lane_row, lane_add, lane_weight, block_expert, w1, w2):
            with ExitStack() as e:
                def pair(name, shape):
                    return [sb(f"{name}{p}", shape, to=e) for p in range(2)]

                x_in, xT = pair("x_in", [128, D]), pair("xT_m", [128, KD, 128])
                hs, hT = pair("hs", [128, EF]), pair("hT_m", [128, EF // 128, 128])
                y_out = pair("y_out", [128, D])
                x_loaded, y_added, out_sent = [sem(f"x_loaded{p}", e) for p in range(2)], sem("y_added", e), sem("out_sent", e)
                xT_done, xT_ready, h_done, silu_done = sem("xT_done_m", e), sem("xT_ready_m", e), sem("h_done_m", e), sem("silu_done", e)
                hT_done, hT_ready, y_done, y_ready = sem("hT_done_m", e), sem("hT_ready_m", e), sem("y_done", e), sem("y_ready_m", e)
                y_bank = (ps_o[:, 0:D], st_tile[:, 0, :])
                hT_bank = ring[0][:, 0:2, :].rearrange("p a c -> p (a c)")

                def run(eng, turn, lead):
                    for t in range(-lead, 3):
                        turn(t, t % 2, lambda k, t=t: (t + k) // 2, lambda k, t=t: 0 <= t + k < NBK)
                    n = (NBK - 6) // 2
                    with eng.Fori(0, n) as i:
                        turn(i * 2 + 3, 1, lambda k: i + (k + 3) // 2, lambda k: True)
                        turn(i * 2 + 4, 0, lambda k: i + (k + 4) // 2, lambda k: True)
                    for t in range(2 * n + 3, NBK + 1):
                        turn(t, t % 2, lambda k, t=t: (t + k) // 2, lambda k, t=t: 0 <= t + k < NBK)

                with nc.Block() as block:

                    @block.sync
                    def _(sp):
                        sp.wait_ge(y_added, 16 * NBK)
                        sp.dma_start(out.rearrange("b t d -> (b t) d"), h_rows[0:NTOK, :]).then_inc(out_sent, 16)
                        sp.wait_ge(out_sent, 16)

                    @block.gpsimd
                    def _(pool):
                        pool.wait_ge(spare_cleared, 16)
                        for t in range(-3, NBK + 1):
                            if 0 <= t + 3 < NBK:
                                wait(pool, xT_done, t + 2)
                                pool.indirect_dma_start(x_in[(t + 3) % 2][:, :], None, x_rows,
                                                        bass.IndirectOffsetOnAxis(ap=lane_row[:, t + 3:t + 4], axis=0)).then_inc(x_loaded[(t + 3) % 2], 16)
                            if t - 1 >= 0:
                                pool.wait_ge(y_ready, t)
                                wait(pool, y_added, 16 * (t - 1))
                                pool.indirect_dma_start(h_rows, bass.IndirectOffsetOnAxis(ap=lane_add[:, t - 1:t], axis=0), y_out[(t - 1) % 2][:, :], None,
                                                        compute_op=ALU.add).then_inc(y_added, 16)

                    @block.tensor
                    def _(pe):
                        pe.wait_ge(loads["moe"], 16 * 2 * NE)

                        def turn(t, p, half, on):
                            if on(1):
                                e1 = pe.value_load(block_expert[0:1, bass.ds(t + 1, 1)], min_val=0, max_val=NE - 1)
                            if on(0):
                                e2 = pe.value_load(block_expert[0:1, bass.ds(t, 1)], min_val=0, max_val=NE - 1)
                                pe.wait_ge(silu_done, t + 1)
                                wait(pe, hT_ready, t * 1)
                                for m in range(EF // 128):
                                    mm = nc.tensor.transpose(hT_bank[:, 128 * m:128 * m + 128], hs[p][:, 128 * m:128 * m + 128], ident[:, :])
                                mm.then_inc(hT_done, 1)
                            if on(2):
                                pe.wait_ge(x_loaded[p], half(2) * 16 + 16)
                                wait(pe, xT_ready, t + 2)
                                for k in range(KD):
                                    mm = nc.tensor.transpose(ps_t[:, 128 * k:128 * k + 128], x_in[p][:, 128 * k:128 * k + 128], ident[:, :])
                                mm.then_inc(xT_done, 1)
                            if on(1):
                                pe.wait_ge(xT_ready, t + 2)
                                wait(pe, silu_done, t * 1)
                                for k in range(KD):
                                    mm = nc.tensor.matmul(two[1 - p][:, :], xT[1 - p][:, k, :], w1[:, bass.ds(e1, 1), k, :].squeeze(1),
                                                          start=(k == 0), stop=(k == KD - 1))
                                mm.then_inc(h_done, 1)
                            if on(0):
                                pe.wait_ge(hT_ready, t + 1)
                                wait(pe, y_ready, t - 1)
                                for m in range(EF // 128):
                                    mm = nc.tensor.matmul(y_bank[p], hT[p][:, m, :], w2[:, bass.ds(e2, 1), m, :].squeeze(1),
                                                          start=(m == 0), stop=(m == EF // 128 - 1))
                                mm.then_inc(y_done, 1)

                        run(pe, turn, 2)

                    @block.scalar
                    def _(act):
                        def turn(t, p, half, on):
                            if on(2):
                                act.wait_ge(xT_done, t + 3)
                                wait(act, h_done, t + 1)
                                nc.scalar.copy(xT[p][:, :, :], ps_t[:, 0:KD * 128].rearrange("p (k t) -> p k t", k=KD)).then_inc(xT_ready, 1)
                            if on(1):
                                act.wait_ge(h_done, t + 2)
                                wait(act, hT_done, t * 1)
                                nc.scalar.activation(hs[1 - p][:, :], two[1 - p][:, :], ACT.Silu).then_inc(silu_done, 1)

                        run(act, turn, 2)

                    @block.vector
                    def _(dve):
                        def turn(t, p, half, on):
                            if on(0):
                                dve.wait_ge(hT_done, t + 1)
                                wait(dve, y_done, t - 1)
                                nc.vector.tensor_copy(hT[p][:, :, :], hT_bank.rearrange("p (m t) -> p m t", t=128)).then_inc(hT_ready, 1)
                                dve.wait_ge(y_done, t + 1)
                                wait(dve, y_added, t * 16 - 16)
                                nc.vector.tensor_scalar(y_out[p][:, :], y_bank[p], lane_weight[:, bass.ds(t, 1)], None, ALU.mult).then_inc(y_ready, 1)

                        run(dve, turn, 0)

        attention(0)
        feed_forward()
        hm = sb("hm", [128, NT, D])
        hm_set, tile_stats = sem("hm_set"), sem("tile_stats")
        attention(1)
        with ExitStack() as e:
            lane_row = sb("lane_row", [128, NBK], I32, to=e)
            lane_add = sb("lane_add", [128, NBK], I32, to=e)
            lane_weight = sb("lane_weight", [128, NBK], to=e)
            block_expert = sb("block_expert", [1, NBK], I32, to=e)
            w1 = sb("w1", [128, NE, KD, EF], to=e)
            w2 = sb("w2", [128, NE, EF // 128, D], to=e)
            route(lane_row, lane_add, lane_weight, block_expert, w1, w2)
            experts(lane_row, lane_add, lane_weight, block_expert, w1, w2)


def layouts(v):
    import numpy as np

    f = np.float32
    c = np.ascontiguousarray
    x = v["x"].reshape(B, 3, 6, 16, 6, 16).transpose(1, 3, 5, 0, 2, 4).reshape(PK, 128, B * NP)

    def rows(w):
        return c(w.reshape(-1, 128, w.shape[-1]).transpose(1, 0, 2))

    def halves(w):
        return w.reshape(*w.shape[:-1], -1, 8, 2).swapaxes(-1, -2).reshape(w.shape)

    def chunks(t):
        o = np.zeros((R[0], 2, t.shape[1]), t.dtype)
        for k in range(2):
            o[0:R[k], k] = t[O[k]:O[k] + R[k]]
        return o

    q_w, kv_w = v["L1_attn_q_w"], v["L1_attn_kv_w"]
    q_b, kv_b = v["L1_attn_q_b"], v["L1_attn_kv_b"]
    pos = np.arange(T, dtype=f)
    scale0 = (f(2500) ** (f(2.0) * np.arange(8, dtype=f) / f(16))).astype(f)
    ang0 = pos[:, None] / scale0[None, :]
    mel = f(2595.0 * np.log10(1.0 + 4000.0 / 200.0))
    fb = f(200.0) * (np.power(f(10.0), np.linspace(0.0, mel, 8, dtype=f) / f(2595.0)).astype(f) - f(1.0)) / f(1000.0)
    ang1 = pos[:, None] * fb[None, :].astype(f)
    qi, ki = np.arange(T)[:, None], np.arange(T)[None, :]
    mask = np.where(ki <= qi, 0.0, -1e30).astype(f)
    selh = np.zeros((128, H, R[0]), f)
    for k in range(H):
        selh[k, k] = 1.0
        selh[32:32 + R[0], k] = np.eye(R[0])
    mask_t = np.zeros((128, 2, T), f)
    mask_t[32:32 + R[0]] = chunks(c(mask.T))
    s = {
        "patches": c(x.transpose(1, 0, 2)), "w_tok": rows(c(v["L0_tok_W"].T)), "tok_b": v["L0_tok_b"],
        "cls": v["L0_tok_cls_token"].reshape(1, D), "pos": v["L0_tok_pos_embedding"].reshape(NP + 1, D), "txt": v["txt"],
        "w_qkv0": rows(v["L0_attn_W_attn"]), "b_qkv0": v["L0_attn_b_attn"],
        "w_out0": rows(v["L0_attn_W_proj"]), "b_out0": v["L0_attn_b_proj"].reshape(1, D),
        "w_qkv1": rows(np.concatenate([halves(q_w), halves(kv_w[:, 0:D]), kv_w[:, D:], v["L1_attn_rh_w"]], axis=1)),
        "b_qkv1": np.concatenate([halves(q_b), halves(kv_b[0:D]), kv_b[D:]]),
        "w_out1": rows(v["L1_attn_out_w"]), "b_out1": v["L1_attn_out_b"].reshape(1, D),
        "nrm_w": c(np.stack([v["L1_attn_qn_w"], v["L1_attn_kvn_w"]]).reshape(2, KD, 128).transpose(2, 1, 0)),
        "nrm_b": c(np.stack([v["L1_attn_qn_b"], v["L1_attn_kvn_b"]]).reshape(2, KD, 128).transpose(2, 1, 0)),
        "ln_w": halves(v["L1_attn_ln_w"]), "ln_b": halves(v["L1_attn_ln_b"]), "rh_b": v["L1_attn_rh_b"],
        "u1": rows(v["L0_ffn_U1"]), "v1": np.concatenate([v["L0_ffn_V1"], v["L0_ffn_b1"][None]]),
        "u2": rows(v["L0_ffn_U2"]), "v2": np.concatenate([v["L0_ffn_V2"], v["L0_ffn_b2"][None]]),
        "gate": rows(v["L1_ffn_gate_w"]),
        "w1": c(v["L1_ffn_w1"].reshape(NE, KD, 128, EF).transpose(2, 0, 1, 3)),
        "w2": c(v["L1_ffn_w2"].reshape(NE, EF // 128, 128, D).transpose(2, 0, 1, 3)),
        "ident": np.eye(128, dtype=f), "ident16": np.eye(128, dtype=np.float16),
        "selh": selh, "mask_s": chunks(mask), "mask_t": mask_t,
        "iota": np.arange(NE, dtype=f), "block_no": np.arange(NBK, dtype=f), "lane_no": np.arange(BK, dtype=f),
        "token_1": np.arange(1, 128 * NT + 1, dtype=f).reshape(NT, 128).T, "spare_1": NTOK + 1 + np.arange(BK, dtype=f).reshape(BK, 1),
        "tri": np.triu(np.ones((128, 128), f), 1),
        "valid": (np.arange(128)[:, None] + 128 * np.arange(NT)[None, :] < NTOK).astype(f),
    }
    for n, ang in enumerate((ang0, ang1)):
        co, si = np.cos(ang).astype(f), np.sin(ang).astype(f)
        s[f"cos{n}"] = chunks(np.concatenate([co, co], axis=1))
        s[f"sin{n}"] = chunks(np.concatenate([-si, si], axis=1))
    return {k: c(a) for k, a in s.items()}


def kernel(**inputs):
    import numpy as np
    import concourse.bacc as bacc
    from concourse.bass_utils import run_bass_kernel_spmd

    nc = bacc.Bacc("TRN2", target_bir_lowering=False, num_devices=1)
    arrays = {f"in_{k}": a for k, a in layouts({k: np.asarray(a) for k, a in inputs.items()}).items()}
    a = {k[3:]: nc.dram_tensor(k, x.shape, mybir.dt.from_np(x.dtype), kind="ExternalInput").ap() for k, x in arrays.items()}
    out = nc.dram_tensor("out", (B, T, D), F32, kind="ExternalOutput").ap()
    build_program(nc, a, out)
    r = run_bass_kernel_spmd(nc, [arrays], core_ids=[0])
    return r.results[0]["out"]
```
